# Optimizing a Trainium2 kernel written in Bass

```python
import numpy as np
import jax
import jax.numpy as jnp

def _softmax(x, axis=-1):
    return jax.nn.softmax(x, axis=axis)

def _gelu(x):
    return jax.nn.gelu(x, approximate=True)

def _silu(x):
    return jax.nn.silu(x)

def _sigmoid(x):
    return jax.nn.sigmoid(x)

def _layernorm(x, axis=-1, eps=1e-05):
    m = jnp.mean(x, axis=axis, keepdims=True)
    v = jnp.var(x, axis=axis, keepdims=True)
    return (x - m) / jnp.sqrt(v + eps)

def _scatter_add(tgt, idx, src, axis=0):
    return tgt.at[idx].add(src)

def _segment_sum(src, seg, n):
    return jax.ops.segment_sum(src, seg, n)
kernel_name = 'mk_decoder_postln_d1_seqx_r4_a1853c'

def setup_inputs(seed: int=0):
    np.random.seed(seed)
    _w = jnp.asarray

    def _rec_inputs():
        import jax
        import jax.numpy as jnp
        _rk = jax.random.key(seed)
        x = -0.0002928 + 1 * jax.random.normal(jax.random.fold_in(_rk, 1), (8, 256, 256), jnp.float32)
        _lenS = 256 - jax.random.randint(jax.random.fold_in(_rk, 7), (8,), 0, max(1, 256 // 4) + 1, jnp.int32)
        _lenS2 = 256 - jax.random.randint(jax.random.fold_in(_rk, 8), (8,), 0, max(1, 256 // 4) + 1, jnp.int32)
        _ctx_1024P = jax.random.normal(jax.random.fold_in(_rk, 11), (8, 16, 256), jnp.float32)
        _ctx_1024c = jax.random.dirichlet(jax.random.fold_in(_rk, 511), 0.3 * jnp.ones((16,), jnp.float32), (8, 256))
        _ctx_1024t = jnp.einsum('bsk,bkd->bsd', _ctx_1024c, _ctx_1024P)
        _ctx_1024t = _ctx_1024t * jax.lax.rsqrt(jnp.mean(jnp.square(_ctx_1024t)) + 1e-12) * 0.953939
        ctx_1024 = -1.39393e-06 + 0.999914 * (_ctx_1024t + 0.3 * jax.random.normal(jax.random.fold_in(_rk, 611), (8, 256, 256), jnp.float32))
        _validS = jnp.arange(256)[None, :] < _lenS[:, None]
        _validS2 = jnp.arange(256)[None, :] < _lenS2[:, None]
        _causal = jnp.tril(jnp.ones((256, 256), dtype=bool))
        mask_Bx1x1xS2_ik0 = jnp.where(jnp.broadcast_to(_validS2[:, None, None, :], (8, 1, 1, 256)), 0, 1).astype(jnp.int32)
        return (x, ctx_1024, mask_Bx1x1xS2_ik0)
    x, ctx_1024, mask_Bx1x1xS2_ik0 = _rec_inputs()

    def _L0_attn_setup():
        import jax, jax.numpy as jnp
        import numpy as np
        import math
        TALA_CYCLES = [5, 6, 7, 8]
        N_HEADS = 16
        key = jax.random.key(seed)
        k1, k2, k3, k4 = jax.random.split(key, 4)
        B, T, D = (2, 512, 256)
        x = jax.random.normal(k1, (B, T, D), dtype=jnp.float32)
        w_qkv = jax.random.normal(k2, (D, 3 * D), dtype=jnp.float32) * (1.0 / math.sqrt(D))
        w_out = jax.random.normal(k3, (D, D), dtype=jnp.float32) * (1.0 / math.sqrt(D))
        bandha_gate = jax.random.normal(k4, (N_HEADS, max(TALA_CYCLES)), dtype=jnp.float32)
        return {'x': x, 'w_qkv': w_qkv, 'w_out': w_out, 'bandha_gate': bandha_gate}
    _L0_attn_all = _L0_attn_setup()
    _L0_attn_in = {k: v for k, v in _L0_attn_all.items() if k in ('w_qkv', 'w_out', 'bandha_gate')}
    del _L0_attn_all

    def _L0_xattn_setup():
        import jax, jax.numpy as jnp
        import numpy as np
        D_FEAT = 256
        N_HEAD = 16
        D_HEAD = D_FEAT // N_HEAD
        key = jax.random.key(seed)
        ks = jax.random.split(key, 13)
        B, S = (2, 512)
        scale = 1.0 / np.sqrt(D_FEAT)
        inp = {'Q': jax.random.normal(ks[0], (B, S, D_FEAT), jnp.float32), 'K': jax.random.normal(ks[1], (B, S, D_FEAT), jnp.float32), 'V': jax.random.normal(ks[2], (B, S, D_FEAT), jnp.float32), 'mask': jax.random.randint(ks[3], (B, 1, 1, S), 0, 2, jnp.int32), 'Wq': jax.random.normal(ks[4], (D_FEAT, D_FEAT), jnp.float32) * scale, 'bq': jnp.zeros((D_FEAT,), jnp.float32), 'Wk': jax.random.normal(ks[5], (D_FEAT, D_FEAT), jnp.float32) * scale, 'bk': jnp.zeros((D_FEAT,), jnp.float32), 'Wv': jax.random.normal(ks[6], (D_FEAT, D_FEAT), jnp.float32) * scale, 'bv': jnp.zeros((D_FEAT,), jnp.float32), 'Wo': jax.random.normal(ks[7], (D_FEAT, D_FEAT), jnp.float32) * scale, 'bo': jnp.zeros((D_FEAT,), jnp.float32)}
        return inp
    _L0_xattn_all = _L0_xattn_setup()
    _L0_xattn_in = {k: v for k, v in _L0_xattn_all.items() if k in ('Wq', 'bq', 'Wk', 'bk', 'Wv', 'bv', 'Wo', 'bo')}
    del _L0_xattn_all

    def _L0_ffn_setup():
        import jax, jax.numpy as jnp
        import numpy as np
        B, S, H, E, F = (2, 512, 256, 8, 1024)
        key = jax.random.key(seed)
        k1, k2, k3, k4 = jax.random.split(key, 4)
        h = jax.random.normal(k1, (B, S, H), dtype=jnp.float32)
        Wr = jax.random.normal(k2, (H, E), dtype=jnp.float32) / np.sqrt(H)
        W1 = jax.random.normal(k3, (E, H, F), dtype=jnp.float32) / np.sqrt(H)
        W2 = jax.random.normal(k4, (E, F, H), dtype=jnp.float32) / np.sqrt(F)
        return {'h': h, 'Wr': Wr, 'W1': W1, 'W2': W2}
    _L0_ffn_all = _L0_ffn_setup()
    _L0_ffn_in = {k: v for k, v in _L0_ffn_all.items() if k in ('Wr', 'W1', 'W2')}
    del _L0_ffn_all
    return {'x': x, 'ctx_1024': ctx_1024, 'mask_Bx1x1xS2_ik0': mask_Bx1x1xS2_ik0, 'L0_attn_w_qkv': _L0_attn_in['w_qkv'], 'L0_attn_w_out': _L0_attn_in['w_out'], 'L0_attn_bandha_gate': _L0_attn_in['bandha_gate'], 'L0_xattn_Wq': _L0_xattn_in['Wq'], 'L0_xattn_bq': _L0_xattn_in['bq'], 'L0_xattn_Wk': _L0_xattn_in['Wk'], 'L0_xattn_bk': _L0_xattn_in['bk'], 'L0_xattn_Wv': _L0_xattn_in['Wv'], 'L0_xattn_bv': _L0_xattn_in['bv'], 'L0_xattn_Wo': _L0_xattn_in['Wo'], 'L0_xattn_bo': _L0_xattn_in['bo'], 'L0_ffn_Wr': _L0_ffn_in['Wr'], 'L0_ffn_W1': _L0_ffn_in['W1'], 'L0_ffn_W2': _L0_ffn_in['W2']}

def reference(x, ctx_1024, mask_Bx1x1xS2_ik0, L0_attn_w_qkv, L0_attn_w_out, L0_attn_bandha_gate, L0_xattn_Wq, L0_xattn_bq, L0_xattn_Wk, L0_xattn_bk, L0_xattn_Wv, L0_xattn_bv, L0_xattn_Wo, L0_xattn_bo, L0_ffn_Wr, L0_ffn_W1, L0_ffn_W2):
    import jax
    import jax.numpy as jnp

    def _L0_attn_ref(x, w_qkv, w_out, bandha_gate):
        import jax, jax.numpy as jnp
        import numpy as np
        import math
        TALA_CYCLES = [5, 6, 7, 8]
        N_HEADS = 16
        B, T, D = x.shape
        H = N_HEADS
        hd = D // H
        scale = math.sqrt(hd)
        qkv = x @ w_qkv
        q, k, v = jnp.split(qkv, 3, axis=-1)
        to_heads = lambda t: t.reshape(B, T, H, hd).transpose(0, 2, 1, 3)
        q, k, v = (to_heads(q), to_heads(k), to_heads(v))
        cycles = np.array([TALA_CYCLES[i % len(TALA_CYCLES)] for i in range(H)])
        phases = np.arange(T)[None, :] % cycles[:, None]
        gate = jax.nn.sigmoid(jnp.take_along_axis(bandha_gate, jnp.asarray(phases), axis=1))
        q = q * gate[None, :, :, None]
        scores = jnp.einsum('bhqd,bhkd->bhqk', q, k) / scale
        causal = np.tril(np.ones((T, T), dtype=bool))
        scores = jnp.where(jnp.asarray(causal), scores, -jnp.inf)
        attn = jax.nn.softmax(scores, axis=-1)
        out = jnp.einsum('bhqk,bhkd->bhqd', attn, v)
        out = out.transpose(0, 2, 1, 3).reshape(B, T, D)
        return out @ w_out

    def _L0_xattn_ref(Q, K, V, mask, Wq, bq, Wk, bk, Wv, bv, Wo, bo):
        import jax, jax.numpy as jnp
        import numpy as np
        D_FEAT = 256
        N_HEAD = 16
        D_HEAD = D_FEAT // N_HEAD
        B, S, _ = Q.shape
        Qf = jnp.einsum('bsd,ed->bse', Q, Wq) + bq
        Kf = jnp.einsum('bsd,ed->bse', K, Wk) + bk
        Vf = jnp.einsum('bsd,ed->bse', V, Wv) + bv
        Qs = Qf.reshape(B, S, N_HEAD, D_HEAD).transpose(0, 2, 1, 3)
        Ks = Kf.reshape(B, S, N_HEAD, D_HEAD).transpose(0, 2, 1, 3)
        Vs = Vf.reshape(B, S, N_HEAD, D_HEAD).transpose(0, 2, 1, 3)
        scores = jnp.einsum('bhqd,bhkd->bhqk', Qs, Ks) / np.sqrt(D_FEAT).astype(np.float32)
        scores = jnp.where(mask == 0, jnp.float32(-1000000000.0), scores)
        attention = jax.nn.softmax(scores, axis=-1)
        x_raw = jnp.einsum('bhqk,bhkd->bhqd', attention, Vs)
        x_rsh = x_raw.transpose(0, 2, 1, 3).reshape(B, S, D_FEAT)
        x = jnp.einsum('bsd,ed->bse', x_rsh, Wo) + bo
        return x

    def _L0_ffn_ref(h, Wr, W1, W2):
        import jax, jax.numpy as jnp
        import numpy as np
        B, S, H, E, F = (2, 512, 256, 8, 1024)
        g = jax.nn.softmax(h @ Wr, axis=-1)
        top2_w, top2_idx = jax.lax.top_k(g, 2)
        top2_w = top2_w / jnp.sum(top2_w, axis=-1, keepdims=True)
        hid = jax.nn.relu(jnp.einsum('bsh,ehf->bsef', h, W1))
        expert_out = jnp.einsum('bsef,efh->bseh', hid, W2)
        top2_out = jnp.take_along_axis(expert_out, top2_idx[..., None], axis=2)
        return jnp.sum(top2_out * top2_w[..., None], axis=2)
    x = _layernorm(x + _L0_attn_ref(x, L0_attn_w_qkv, L0_attn_w_out, L0_attn_bandha_gate), axis=-1)
    x = _layernorm(x + _L0_xattn_ref(x, ctx_1024, ctx_1024, mask_Bx1x1xS2_ik0, L0_xattn_Wq, L0_xattn_bq, L0_xattn_Wk, L0_xattn_bk, L0_xattn_Wv, L0_xattn_bv, L0_xattn_Wo, L0_xattn_bo), axis=-1)
    x = _layernorm(x + _L0_ffn_ref(x, L0_ffn_Wr, L0_ffn_W1, L0_ffn_W2), axis=-1)
    return x

_drawn_inputs = setup_inputs


def setup_inputs(seed=0):
    import zlib

    import numpy as np

    out = dict(_drawn_inputs(seed))
    spreads = {'L0_xattn_bq': (0.0, 0.1),
     'L0_xattn_bk': (0.0, 0.1),
     'L0_xattn_bv': (0.0, 0.1),
     'L0_xattn_bo': (0.0, 0.1)}
    factors = {}
    for name, (base, spread) in spreads.items():
        noise = np.random.default_rng([zlib.crc32(name.encode()), seed]).standard_normal(out[name].shape)
        drawn = base * np.exp(spread * noise) if base else spread * noise
        out[name] = jnp.asarray(drawn.astype(out[name].dtype))
    for name, factor in factors.items():
        out[name] = (out[name] * factor).astype(out[name].dtype)
    return out
```

```python
from contextlib import ExitStack

import concourse.bass as bass
from concourse import mybir

F32 = mybir.dt.float32
BF16 = mybir.dt.bfloat16
I32 = mybir.dt.int32
ALU = mybir.AluOpType
ACT = mybir.ActivationFunctionType
X = mybir.AxisListType.X

P = 128
B, S, D = 8, 256, 256
H, HD = 16, 16
KT = D // P
TT = S // P
E, F = 8, 1024
FT = F // P
EPS = 1e-5
CAUSAL_FILL = -1e30
MASKED_SCORE = -1e9
CHUNK = 512
NCHUNK = B * S // CHUNK

Q_PARTS = (0, 0, 0, 1, 1, 2)
K_PARTS = (0, 1, 2, 0, 1, 0)
STACK = HD * len(Q_PARTS)
MASK_ROWS = 3
MAX_ROWS = 3


def wait(eng, sem, value):
    if isinstance(value, int) and value <= 0:
        return
    eng.wait_ge(sem, value)


def fence(eng, sem, value, tick):
    wait(eng, sem, value)
    if not isinstance(value, int):
        eng.sem_inc(tick)


class Steps:

    def __init__(self, eng, sem, per_batch, batch):
        self.eng, self.sem, self.count, self.end = eng, sem, batch * per_batch, per_batch
        self.n = 0

    def link(self, instruction, tick=None):
        self.n += 1
        assert self.n <= self.end
        instruction.then_inc(self.sem, 1)
        if tick is None:
            wait(self.eng, self.sem, self.count + self.n)
        else:
            fence(self.eng, self.sem, self.count + self.n, tick)

    def done(self):
        assert self.n == self.end


class Stream:

    def __init__(self, nc, ctx, name, cross):
        def sb(n, shape, dt):
            return ctx.enter_context(nc.sbuf_tensor(f"{name}_{n}", shape, dt))

        self.name, self.cross = name, cross
        def sem(n):
            return ctx.enter_context(nc.semaphore(f"{name}_{n}"))

        self.src_in = sem("src_in")
        self.src_evac = sem("src_evac")
        self.src_full = sem("src_full")
        self.kv_in = sem("kv_in")
        self.kv_full = sem("kv_full")
        self.kv_evac = sem("kv_evac")
        self.q_full = sem("q_full")
        self.q_evac = sem("q_evac")
        self.k_full = sem("k_full")
        self.k_evac = sem("k_evac")
        self.q_split = sem("q_split")
        self.k_split = sem("k_split")
        self.q_written = sem("q_written")
        self.k_written = sem("k_written")
        self.q_stacked = sem("q_stacked")
        self.k_stacked = sem("k_stacked")
        self.v_full = sem("v_full")
        self.v_evac = sem("v_evac")
        self.max_full = sem("max_full")
        self.max_read = sem("max_read")
        self.nm_split = sem("nm_split")
        self.nm_full = sem("nm_full")
        self.nm_evac = sem("nm_evac")
        self.m_written = sem("m_written")
        self.m_stacked = sem("m_stacked")
        self.st_full = sem("st_full")
        self.exp_done = sem("exp_done")
        self.pv_full = sem("pv_full")
        self.norm_done = sem("norm_done")
        self.o_full = sem("o_full")
        self.res_done = sem("res_done")
        self.res_copied = sem("res_copied")
        self.stats_done = sem("stats_done")
        self.rstd_done = sem("rstd_done")
        self.ln_taken = sem("ln_taken")
        self.root_done = sem("root_done")
        self.newton_chain = sem("newton_chain")
        self.ln_done = sem("ln_done")
        self.pool_chain = sem("pool_chain")
        self.ksplit_chain = sem("ksplit_chain")
        self.nm_chain = sem("nm_chain")
        self.norm_chain = sem("norm_chain")
        self.ln_chain = sem("ln_chain")
        self.keep_in = sem("keep_in")
        self.keep_done = sem("keep_done")
        self.wts_in = sem("wts_in")
        self.wq = sb("wq", [P, KT, D], F32)
        self.wk = sb("wk", [P, KT, D], F32)
        self.wv = sb("wv", [P, KT, D], F32)
        self.wo = sb("wo", [P, 4, D], F32)
        self.src = sb("src", [P, TT, D], F32)
        self.xT = sb("xT", [P, KT, S], F32)
        self.cT = sb("cT", [P, KT, S], F32) if cross else self.xT
        self.res = sb("res", [P, TT, D], F32)
        self.qf = sb("qf", [P, KT, S], F32)
        self.kf = sb("kf", [P, KT, S], F32)
        self.kfm = sb("kfm", [P, KT, S], F32) if cross else self.kf
        self.qr = sb("qr", [P, KT, S], F32)
        self.kr = sb("kr", [P, KT, S], F32)
        self.qp = sb("qp", [P, 3, KT, S], BF16)
        self.kp = sb("kp", [P, 3, KT, S], BF16)
        self.qs = sb("qs", [P, H, S], BF16)
        self.ks = sb("ks", [P, H, S], BF16)
        self.v = sb("v", [P, TT, H, 32], F32)
        self.mx = sb("mx", [P, TT, H], F32)
        self.nf = sb("nf", [P, TT, H], F32)
        self.nr = sb("nr", [P, TT, H], F32)
        self.np = sb("np", [P, TT, 3, H], BF16)
        self.npT = sb("npT", [3 * H, S], BF16)
        self.p = sb("p", [P, 2, 2 * S], F32)
        self.sums = sb("sums", [P, 512], F32)
        self.rec = sb("rec", [P, 512], F32)
        self.aT = sb("aT", [P, 4, S], F32)
        self.r = sb("r", [P, TT, D], F32)
        self.st = sb("st", [P, TT, 6], F32)
        self.mv = sb("mv", [P, TT, 2], F32)
        self.ve = sb("ve", [P, TT], F32)
        self.lnv = sb("lnv", [P, TT], F32)
        self.y0 = sb("y0", [P, TT], F32)
        self.yy = sb("yy", [P, TT], F32)
        self.rstd = sb("rstd", [P, TT], F32)
        self.out = sb("out", [P, TT, D], F32)
        if cross:
            self.bq = sb("bq", [P, KT], F32)
            self.bk = sb("bk", [P, KT], F32)
            self.bv = sb("bv", [1, D], F32)
            self.bo = sb("bo", [1, D], F32)
            self.keep_i = sb("keep_i", [P, S], I32)
            self.keep = sb("keep", [P, S], F32)
        self.mask_rows = MASK_ROWS if cross else 0
        self.max_k = STACK + self.mask_rows
        self.st_k = self.max_k + MAX_ROWS
        self.parts_d = nc.dram_tensor(f"{name}_parts", (2, 3, KT, P, S), BF16, kind="Internal").ap()
        self.m_d = nc.dram_tensor(f"{name}_m", (3, H, S), BF16, kind="Internal").ap()
        self.pp = ctx.enter_context(nc.psum_tensor(f"{name}_pp", [P, 512], F32))
        self.pm = ctx.enter_context(nc.psum_tensor(f"{name}_pm", [P, 512], F32))
        self.ps = ctx.enter_context(nc.psum_tensor(f"{name}_ps", [P, 512], F32))
        self.pv = ctx.enter_context(nc.psum_tensor(f"{name}_pv", [P, 512], F32))


def decoder_layer(nc, x, ctx_in, mask, w_qkv, w_o1, gate_raw, wqT, bq, wkT, bk, wvT, bv, woT, bo,
                  w_r, w_1, w_2, out):
    with ExitStack() as outer:
        xT2 = outer.enter_context(nc.sbuf_tensor("xT2", [P, KT, B * S], F32))
        x2_d = nc.dram_tensor("x2", (B, S, D), F32, kind="Internal").ap()
        with ExitStack() as ctx:
            attention(nc, ctx, xT2, x2_d, x, ctx_in, mask, w_qkv, w_o1, gate_raw, wqT, bq, wkT, bk, wvT, bv, woT, bo)
        with ExitStack() as ctx:
            experts(nc, ctx, xT2, x2_d, w_r, w_1, w_2, out)


def attention(nc, ctx, xT2, x2_d, x, ctx_in, mask, w_qkv, w_o1, gate_raw, wqT, bq, wkT, bk, wvT, bv, woT, bo):
    def sb(n, shape, dt):
        return ctx.enter_context(nc.sbuf_tensor(n, shape, dt))

    def sem(n):
        return ctx.enter_context(nc.semaphore(n))

    A = Stream(nc, ctx, "self", False)
    C = Stream(nc, ctx, "cross", True)
    identf = sb("identf", [P, P], F32)
    identb = sb("identb", [P, P], BF16)
    tri_qk = sb("tri_qk", [P, P], BF16)
    tri_kq = sb("tri_kq", [P, P], BF16)
    ones = sb("ones", [1, P], F32)
    gate = sb("gate", [P, KT, S], F32)
    mrow_i = sb("mrow_i", [B, S], I32)
    mrow = sb("mrow", [B, S], F32)
    mres = sb("mres", [B, S], F32)
    mparts = sb("mparts", [B, 3, S], BF16)
    mparts_d = nc.dram_tensor("mask_parts", (3, B, S), BF16, kind="Internal").ap()

    const_ready = sem("const_ready")
    pool_setup = sem("pool_setup")
    gate_in = sem("gate_in")
    gate_exp = sem("gate_exp")
    gate_chain = sem("gate_chain")
    gate_ready = sem("gate_ready")
    mrow_in = sem("mrow_in")
    mask_chain = sem("mask_chain")
    mask_written = sem("mask_written")
    mask_stacked = sem("mask_stacked")
    x2_written = sem("x2_written")
    x2T_full = sem("x2T_full")
    x2T_evac = sem("x2T_evac")
    dve_setup = sem("dve_setup")
    pool_tick, pe_tick, dve_tick, sp_tick = (sem(n) for n in ("pool_tick", "pe_tick", "dve_tick", "sp_tick"))

    block = ctx.enter_context(nc.Block())

    def schedule(eng, iteration):
        iteration(0)
        iteration(1)
        iteration(2)
        with eng.Fori(3, B - 1) as i:
            iteration(i)
        for i in range(B - 1, B + 2):
            iteration(i)

    def has(i, shift):
        return not isinstance(i, int) or 0 <= i + shift < B

    @block.sync
    def _(sp):
        def load_weights(T, wq, wk, wv, wo):
            for dst, src in ((T.wq, wq), (T.wk, wk), (T.wv, wv)):
                sp.dma_start(dst[:], src.rearrange("(k p) n -> p k n", p=P)).then_inc(T.wts_in, 16)
            sp.wait_ge(const_ready, 1)
            for g in range(4):
                src = wo.rearrange("(r g d) n -> g d r n", g=4, d=HD)
                sp.dma_start(T.wo[32 * g:32 * g + HD], src[g]).then_inc(T.wts_in, 16)

        def load_src(T, src, b, full):
            fence(sp, full, b, sp_tick)
            sp.dma_start(T.src[:], src[b].rearrange("(t p) d -> p t d", p=P)).then_inc(T.src_in, 16)

        def bounce(T, b, which, split, parts, written):
            fence(sp, split, b + 1, sp_tick)
            fence(sp, T.q_stacked if which == 0 else T.k_stacked, 96 * b, sp_tick)
            sp.dma_start(T.parts_d[which].rearrange("s k p t -> p s k t"), parts[:]).then_inc(written, 16)

        def stack(T, b, which, written, order, dst, stacked):
            fence(sp, written, 16 * (b + 1), sp_tick)
            fence(sp, T.st_full, H * b, sp_tick)
            for s, part in enumerate(order):
                src = T.parts_d[which, part].rearrange("k (h d) t -> d (k h) t", d=HD)
                sp.dma_start(dst[HD * s:HD * s + HD], src).then_inc(stacked, 16)

        def stack_max(T, b):
            fence(sp, T.nm_evac, b + 1, sp_tick)
            fence(sp, T.m_stacked, 16 * b, sp_tick)
            sp.dma_start(T.m_d.rearrange("s h t -> (s h) t"), T.npT[:]).then_inc(T.m_written, 16)
            fence(sp, T.m_written, 16 * (b + 1), sp_tick)
            sp.dma_start(T.qs[T.max_k:T.max_k + MAX_ROWS], T.m_d).then_inc(T.m_stacked, 16)

        def project(T, b):
            bounce(T, b, 0, T.q_split, T.qp, T.q_written)
            bounce(T, b, 1, T.k_split, T.kp, T.k_written)
            stack(T, b, 0, T.q_written, Q_PARTS, T.qs, T.q_stacked)
            stack(T, b, 1, T.k_written, K_PARTS, T.ks, T.k_stacked)

        sp.dma_start(gate[:], gate_raw.rearrange("(k p) t -> p k t", p=P)).then_inc(gate_in, 16)
        sp.dma_start(A.src[:], x[0].rearrange("(t p) d -> p t d", p=P)).then_inc(A.src_in, 16)
        load_weights(A, w_qkv[:, 0:D], w_qkv[:, D:2 * D], w_qkv[:, 2 * D:3 * D], w_o1)
        sp.dma_start(mrow_i[:], mask).then_inc(mrow_in, 16)
        load_weights(C, wqT, wkT, wvT, woT)
        sp.dma_start(C.bq[:], bq).then_inc(C.wts_in, 16)
        sp.dma_start(C.bk[:], bk).then_inc(C.wts_in, 16)
        sp.dma_start(C.bv[:], bv.rearrange("(o n) -> o n", o=1)).then_inc(C.wts_in, 16)
        sp.dma_start(C.bo[:], bo.rearrange("(o n) -> o n", o=1)).then_inc(C.wts_in, 16)
        sp.wait_ge(dve_setup, 1)
        sp.dma_start(mparts_d.rearrange("s b t -> b s t"), mparts[:]).then_inc(mask_written, 16)
        sp.wait_ge(mask_written, 16)
        project(A, 0)

        def iteration(i):
            if has(i, 1):
                fence(sp, A.res_copied, i + 1, sp_tick)
                load_src(A, x, i + 1, A.src_full)
            if has(i, -1):
                b = i - 1
                load_src(C, ctx_in, b, C.kv_full)
                fence(sp, C.keep_done, b, sp_tick)
                sp.dma_start(C.keep_i[:], mask[b].partition_broadcast(P)).then_inc(C.keep_in, 16)
            if has(i, 0):
                stack_max(A, i)
            if has(i, -1):
                b = i - 1
                project(C, b)
                fence(sp, C.st_full, H * b, sp_tick)
                rows = mparts_d[:, b, :].unsqueeze(1).to_broadcast((3, H, S))
                sp.dma_start(C.ks[STACK:STACK + MASK_ROWS], rows).then_inc(mask_stacked, 16)
            if has(i, -2):
                b = i - 2
                fence(sp, C.ln_done, b + 1, sp_tick)
                sp.dma_start(x2_d[b].rearrange("(t p) d -> p t d", p=P), C.out[:]).then_inc(x2_written, 16)
            if has(i, 1):
                project(A, i + 1)
            if has(i, -1):
                stack_max(C, i - 1)

        schedule(sp, iteration)
        sp.wait_ge(x2_written, 16 * B)

    @block.gpsimd
    def _(pool):
        setup = Steps(pool, pool_setup, 100, 0)
        for m in (identf, identb, tri_qk, tri_kq):
            setup.link(pool.memset(m[:], 0.0))
        for m in (identf, identb):
            setup.link(pool.affine_select(out=m[:], in_=m[:], compare_op=ALU.not_equal, fill=1.0, base=0,
                                          pattern=[[-1, P]], channel_multiplier=1))
        setup.link(pool.affine_select(out=tri_qk[:], in_=tri_qk[:], compare_op=ALU.is_ge, fill=CAUSAL_FILL,
                                      base=0, pattern=[[-1, P]], channel_multiplier=1))
        setup.link(pool.affine_select(out=tri_kq[:], in_=tri_kq[:], compare_op=ALU.is_ge, fill=CAUSAL_FILL,
                                      base=0, pattern=[[1, P]], channel_multiplier=-1))
        setup.link(pool.memset(ones[:], 1.0))
        for T in (A, C):
            setup.link(pool.memset(T.wo[:], 0.0))
            setup.link(pool.memset(T.v[:], 1.0))
            setup.link(pool.memset(T.qs[STACK:P], 1.0))
            setup.link(pool.memset(T.ks[STACK:P], 1.0))
        pool.drain().then_inc(const_ready, 1)

        def split_q(T, b):
            wait(pool, T.q_evac, b + 1)
            fence(pool, T.q_written, 16 * b, pool_tick)
            c = Steps(pool, T.pool_chain, 3, b)
            c.link(pool.tensor_copy(T.qp[:, 0], T.qf[:]))
            c.link(pool.tensor_tensor(T.qr[:], T.qf[:], T.qp[:, 0], ALU.subtract), pool_tick)
            c.link(pool.tensor_copy(T.qp[:, 1], T.qr[:]))
            c.done()
            pool.tensor_tensor(T.qp[:, 2], T.qr[:], T.qp[:, 1], ALU.subtract).then_inc(T.q_split, 1)

        split_q(A, 0)

        def iteration(i):
            if has(i, 0):
                wait(pool, A.src_in, 16 * (i + 1))
                fence(pool, A.res_done, i, pool_tick)
                pool.tensor_copy(A.res[:], A.src[:]).then_inc(A.res_copied, 1)
            if has(i, -1):
                split_q(C, i - 1)
            if has(i, -1):
                wait(pool, A.ln_done, i)
                fence(pool, C.res_done, i - 1, pool_tick)
                pool.tensor_copy(C.res[:], A.out[:]).then_inc(C.res_copied, 1)
            if has(i, 1):
                split_q(A, i + 1)

        schedule(pool, iteration)

    @block.tensor
    def _(pe):
        pe.wait_ge(const_ready, 1)

        def transpose(T, src, dst_full):
            for k in range(KT):
                for t in range(TT):
                    o = (k * TT + t) * P
                    last = pe.transpose(T.pp[:, o:o + P], src[:, t, k * P:(k + 1) * P], identf[:])
            last.then_inc(dst_full, 1)

        def features(T, w, rhs, full):
            for m in range(KT):
                for k in range(KT):
                    last = pe.matmul(T.pp[:, m * S:(m + 1) * S], w[:, k, m * P:(m + 1) * P], rhs[:, k, :],
                                     start=(k == 0), stop=(k == KT - 1))
            last.then_inc(full, 1)

        def values(T, b, before, count):
            wait(pe, before, count)
            for t in range(TT):
                o = T.pp[:, t * D:(t + 1) * D]
                for k in range(KT):
                    last = pe.matmul(o, T.cT[:, k, t * P:(t + 1) * P], T.wv[:, k, :],
                                     start=(k == 0), stop=(not T.cross and k == KT - 1))
                if T.cross:
                    last = pe.matmul(o, ones[:], T.bv[:], start=False, stop=True)
            last.then_inc(T.v_full, 1)

        def scores_for_max(T, b, h):
            if h == 0:
                wait(pe, T.q_stacked, 96 * (b + 1))
                wait(pe, T.k_stacked, 96 * (b + 1))
                if T.cross:
                    wait(pe, mask_stacked, 16 * (b + 1))
            wait(pe, T.max_read, H * b + h)
            q, k = T.qs[0:T.max_k, h], T.ks[0:T.max_k, h]
            if T.cross:
                for t in range(TT):
                    last = pe.matmul(T.pm[:, t * S:(t + 1) * S], q[:, t * P:(t + 1) * P], k, start=True, stop=True)
            else:
                for t, o in ((0, 0), (1, P)):
                    n = (t + 1) * P
                    pe.matmul(T.pm[:, o:o + n], q[:, t * P:(t + 1) * P], k[:, 0:n], start=True, stop=False)
                    last = pe.matmul(T.pm[:, o + n - P:o + n], identb[:], tri_qk[:], start=False, stop=True)
            last.then_inc(T.max_full, 1)

        def transpose_max(T, b):
            wait(pe, T.nm_split, b + 1)
            fence(pe, T.v_evac, b + 1, pe_tick)
            pp = T.pp[:].bitcast(BF16)
            for t in range(TT):
                last = pe.transpose(pp[0:3 * H, t * P:(t + 1) * P],
                                    T.np[:, t].rearrange("p s h -> p (s h)"), identb[:])
            last.then_inc(T.nm_full, 1)

        def scores(T, b, h):
            if h == 0:
                wait(pe, T.m_stacked, 16 * (b + 1))
            wait(pe, T.exp_done, H * b + h)
            q, k = T.qs[0:T.st_k, h], T.ks[0:T.st_k, h]
            if T.cross:
                for t in range(TT):
                    last = pe.matmul(T.ps[:, t * S:(t + 1) * S], k[:, t * P:(t + 1) * P], q, start=True, stop=True)
            else:
                for t, o in ((0, 0), (1, S)):
                    n = S - t * P
                    pe.matmul(T.ps[:, o:o + n], k[:, t * P:(t + 1) * P], q[:, t * P:S], start=True, stop=False)
                    last = pe.matmul(T.ps[:, o:o + P], identb[:], tri_kq[:], start=False, stop=True)
            last.then_inc(T.st_full, 1)

        def weigh_values(T, b, h):
            wait(pe, T.exp_done, H * b + h + 1)
            if h == 0:
                wait(pe, T.v_evac, b + 1)
            if h % 8 == 0:
                wait(pe, T.norm_done, 2 * b + h // 8)
            g, o = h % 4, (h // 4 % 2) * S
            for t in range(TT):
                q0 = 0 if T.cross or t == 0 else P
                last = pe.matmul(T.pv[32 * g:32 * g + 32, o + q0:o + S], T.v[:, t, h, :],
                                 T.p[:, h % 2, t * S:(t + 1) * S - q0], start=(t == 0), stop=(t == TT - 1))
            last.then_inc(T.pv_full, 1)

        def project_out(T, b, before, count):
            wait(pe, T.norm_done, 2 * (b + 1))
            wait(pe, before, count)
            for t in range(TT):
                o = T.pp[:, t * D:(t + 1) * D]
                for g in range(4):
                    last = pe.matmul(o, T.aT[:, g, t * P:(t + 1) * P], T.wo[:, g, :],
                                     start=(g == 0), stop=(not T.cross and g == 3))
                if T.cross:
                    last = pe.matmul(o, ones[:], T.bo[:], start=False, stop=True)
            last.then_inc(T.o_full, 1)

        def project_a(b, step):
            if step == 0:
                wait(pe, A.src_in, 16 * (b + 1))
                wait(pe, A.nm_evac, b)
                transpose(A, A.src, A.src_full)
            elif step == 1:
                wait(pe, A.src_evac, b + 1)
                features(A, A.wq, A.xT, A.q_full)
            elif step == 2:
                wait(pe, A.q_evac, b + 1)
                features(A, A.wk, A.xT, A.k_full)

        def project_c(b, step):
            if step == 0:
                wait(pe, A.ln_done, b + 1)
                wait(pe, C.nm_evac, b)
                transpose(C, A.out, C.src_full)
            elif step == 1:
                wait(pe, C.src_in, 16 * (b + 1))
                wait(pe, C.src_evac, b + 1)
                transpose(C, C.src, C.kv_full)
            elif step == 2:
                wait(pe, C.kv_evac, b + 1)
                features(C, C.wq, C.xT, C.q_full)
            elif step == 3:
                wait(pe, C.q_evac, b + 1)
                features(C, C.wk, C.cT, C.k_full)

        pe.wait_ge(A.wts_in, 16 * 7)
        for step in range(3):
            project_a(0, step)
        pe.wait_ge(C.wts_in, 16 * 11)

        def iteration(i):
            if has(i, 0):
                if isinstance(i, int) and i == 0:
                    values(A, i, A.k_evac, 1)
                else:
                    values(A, i, A.res_done, i)
            for h in range(H):
                if has(i, 0):
                    scores_for_max(A, i, h)
                if has(i, -2):
                    scores(C, i - 2, h)
                    if h:
                        weigh_values(C, i - 2, h - 1)
                if has(i, -1) and h % 2 == 1 and h < 8:
                    project_c(i - 1, h // 2)
            if has(i, 0):
                transpose_max(A, i)
            if has(i, -2):
                weigh_values(C, i - 2, H - 1)
                if has(i, -1):
                    project_out(C, i - 2, C.k_evac, i)
                else:
                    project_out(C, i - 2, C.nm_evac, i - 1)
                wait(pe, C.ln_done, i - 1)
                transpose(C, C.out, x2T_full)
            if has(i, -1):
                b = i - 1
                if has(i, -2):
                    values(C, b, x2T_evac, b)
                else:
                    values(C, b, C.k_evac, b + 1)
            for h in range(H):
                if has(i, 0):
                    scores(A, i, h)
                    if h:
                        weigh_values(A, i, h - 1)
                if has(i, -1):
                    scores_for_max(C, i - 1, h)
                if has(i, 1) and h % 2 == 1 and h < 6:
                    project_a(i + 1, h // 2)
            if has(i, 0):
                weigh_values(A, i, H - 1)
                if has(i, 1):
                    project_out(A, i, A.k_evac, i + 2)
                else:
                    project_out(A, i, A.nm_evac, i + 1)
            if has(i, -1):
                transpose_max(C, i - 1)

        schedule(pe, iteration)

    @block.scalar
    def _(act):
        act.wait_ge(gate_in, 16)
        act.activation(gate[:], gate[:], ACT.Exp, scale=-1.0).then_inc(gate_exp, 1)
        act.wait_ge(const_ready, 1)

        def copy(dst, src, full, b, evac):
            wait(act, full, b + 1)
            act.copy(dst, src).then_inc(evac, 1)

        def evac_k(T, b):
            wait(act, T.k_full, b + 1)
            wait(act, T.k_split, b)
            if T.cross:
                for m in range(KT):
                    last = act.activation(T.kf[:, m], T.pp[:, m * S:(m + 1) * S], ACT.Identity,
                                          bias=T.bk[:, m:m + 1])
            else:
                last = act.copy(T.kf[:], T.pp[:].rearrange("p (k t) -> p k t", k=KT))
            last.then_inc(T.k_evac, 1)

        def pp3(T):
            return T.pp[:].rearrange("p (k t) -> p k t", k=KT)

        def evac_v(T, b):
            wait(act, T.v_full, b + 1)
            for t in range(TT):
                last = act.copy(T.v[:, t, :, 0:HD],
                                T.pp[:, t * D:(t + 1) * D].rearrange("p (h d) -> p h d", h=H))
            last.then_inc(T.v_evac, 1)

        def exponentials(T, b, h):
            wait(act, T.st_full, H * b + h + 1)
            wait(act, T.pv_full, H * b + h - 1)
            n = 2 * S if T.cross else 2 * S - P
            act.activation(T.p[:, h % 2, 0:n], T.ps[:, 0:n], ACT.Exp).then_inc(T.exp_done, 1)

        def evac_max(T, b):
            wait(act, T.nm_full, b + 1)
            wait(act, T.m_written, 16 * b)
            act.copy(T.npT[:], T.pp[:].bitcast(BF16)[0:3 * H, 0:S]).then_inc(T.nm_evac, 1)

        def root(T, b):
            wait(act, T.stats_done, b + 1)
            wait(act, T.rstd_done, b)
            act.activation(T.lnv[:], T.ve[:], ACT.Ln).then_inc(T.ln_taken, 1)
            wait(act, T.ln_taken, b + 1)
            act.activation(T.y0[:], T.lnv[:], ACT.Exp, scale=-0.5).then_inc(T.root_done, 1)

        copy(A.xT[:], pp3(A), A.src_full, 0, A.src_evac)
        evac_k(A, 0)
        act.wait_ge(C.wts_in, 16 * 11)

        def iteration(i):
            if has(i, 0):
                evac_v(A, i)
            for h in range(H):
                if has(i, -2):
                    exponentials(C, i - 2, h)
                if has(i, -1) and h == 1:
                    copy(C.xT[:], pp3(C), C.src_full, i - 1, C.src_evac)
                if has(i, -1) and h == 3:
                    copy(C.cT[:], pp3(C), C.kv_full, i - 1, C.kv_evac)
                if has(i, -1) and h == 7:
                    evac_k(C, i - 1)
            if has(i, 0):
                evac_max(A, i)
            if has(i, -2):
                b = i - 2
                root(C, b)
                wait(act, x2T_full, b + 1)
                act.copy(xT2[:, :, bass.ds(b * S, S)], pp3(C)).then_inc(x2T_evac, 1)
            if has(i, -1):
                evac_v(C, i - 1)
            for h in range(H):
                if has(i, 0):
                    exponentials(A, i, h)
                if has(i, 1) and h == 1:
                    copy(A.xT[:], pp3(A), A.src_full, i + 1, A.src_evac)
                if has(i, 1) and h == 5:
                    evac_k(A, i + 1)
            if has(i, 0):
                root(A, i)
            if has(i, -1):
                evac_max(C, i - 1)

        schedule(act, iteration)

    @block.vector
    def _(dve):
        g = Steps(dve, gate_chain, 2, 0)
        dve.wait_ge(gate_exp, 1)
        g.link(dve.tensor_scalar(gate[:], gate[:], 1.0, None, ALU.add))
        g.link(dve.reciprocal(gate[:], gate[:]))
        dve.tensor_scalar(gate[:], gate[:], HD ** -0.5, None, ALU.mult).then_inc(gate_ready, 1)
        dve.wait_ge(gate_ready, 1)
        dve.wait_ge(mrow_in, 16)
        m = Steps(dve, mask_chain, 5, 0)
        m.link(dve.tensor_scalar(mrow[:], mrow_i[:], 0.0, MASKED_SCORE, ALU.is_equal, ALU.mult))
        m.link(dve.tensor_copy(mparts[:, 0], mrow[:]))
        m.link(dve.tensor_tensor(mres[:], mrow[:], mparts[:, 0], ALU.subtract))
        m.link(dve.tensor_copy(mparts[:, 1], mres[:]))
        m.link(dve.tensor_tensor(mparts[:, 2], mres[:], mparts[:, 1], ALU.subtract))
        dve.drain().then_inc(dve_setup, 1)

        def evac_q(T, b):
            wait(dve, T.q_full, b + 1)
            wait(dve, T.q_split, b)
            if T.cross:
                for m in range(KT):
                    last = dve.tensor_scalar(T.qf[:, m], T.pp[:, m * S:(m + 1) * S], T.bq[:, m:m + 1],
                                             D ** -0.5, ALU.add, ALU.mult)
            else:
                last = dve.tensor_tensor(T.qf[:], T.pp[:].rearrange("p (k t) -> p k t", k=KT), gate[:], ALU.mult)
            last.then_inc(T.q_evac, 1)

        def split_k(T, b):
            wait(dve, T.k_evac, b + 1)
            wait(dve, T.k_written, 16 * b)
            c = Steps(dve, T.ksplit_chain, 4 if T.cross else 3, b)
            if T.cross:
                wait(dve, T.keep_done, b + 1)
                c.link(dve.tensor_tensor(T.kfm[:], T.kf[:], T.keep[:].unsqueeze(1).to_broadcast((P, KT, S)),
                                         ALU.mult))
            c.link(dve.tensor_copy(T.kp[:, 0], T.kfm[:]))
            c.link(dve.tensor_tensor(T.kr[:], T.kfm[:], T.kp[:, 0], ALU.subtract))
            c.link(dve.tensor_copy(T.kp[:, 1], T.kr[:]))
            c.done()
            dve.tensor_tensor(T.kp[:, 2], T.kr[:], T.kp[:, 1], ALU.subtract).then_inc(T.k_split, 1)

        def read_max(T, b, h):
            wait(dve, T.max_full, H * b + h + 1)
            if T.cross:
                last = dve.tensor_reduce(T.mx[:, :, h], T.pm[:].rearrange("p (t k) -> p t k", t=TT), X, ALU.max)
            else:
                dve.tensor_reduce(T.mx[:, 0, h:h + 1], T.pm[:, 0:P], X, ALU.max)
                last = dve.tensor_reduce(T.mx[:, 1, h:h + 1], T.pm[:, P:P + S], X, ALU.max)
            last.then_inc(T.max_read, 1)

        def split_max(T, b):
            wait(dve, T.max_read, H * (b + 1))
            wait(dve, T.nm_full, b)
            c = Steps(dve, T.nm_chain, 4, b)
            c.link(dve.tensor_scalar(T.nf[:], T.mx[:], -1.0, None, ALU.mult))
            c.link(dve.tensor_copy(T.np[:, :, 0], T.nf[:]))
            c.link(dve.tensor_tensor(T.nr[:], T.nf[:], T.np[:, :, 0], ALU.subtract))
            c.link(dve.tensor_copy(T.np[:, :, 1], T.nr[:]))
            c.done()
            dve.tensor_tensor(T.np[:, :, 2], T.nr[:], T.np[:, :, 1], ALU.subtract).then_inc(T.nm_split, 1)

        def normalise(T, b, half):
            wait(dve, T.pv_full, H * b + 8 * (half + 1))
            wait(dve, T.o_full, b)
            fence(dve, T.norm_done, 2 * b + half, dve_tick)
            c = Steps(dve, T.norm_chain, 2, 2 * b + half)
            c.link(dve.stream_shuffle(T.sums[:], T.pv[:], [HD + i % HD for i in range(32)]))
            c.link(dve.reciprocal(T.rec[:], T.sums[:]))
            c.done()
            dve.tensor_tensor(T.aT[:, 2 * half:2 * half + 2], T.pv[:].rearrange("p (g t) -> p g t", g=2),
                              T.rec[:].rearrange("p (g t) -> p g t", g=2), ALU.mult).then_inc(T.norm_done, 1)

        def residual(T, b):
            wait(dve, T.o_full, b + 1)
            wait(dve, T.res_copied, b + 1)
            wait(dve, T.ln_done, b)
            dve.tensor_tensor(T.r[:], T.pp[:].rearrange("p (t d) -> p t d", t=TT), T.res[:], ALU.add)\
               .then_inc(T.res_done, 1)
            wait(dve, T.res_done, b + 1)
            c = Steps(dve, T.ln_chain, 4, b)
            for t in range(TT):
                c.link(dve.bn_stats(T.st[:, t], T.r[:, t]), dve_tick)
            for t in range(TT):
                c.link(dve.bn_aggr(T.mv[:, t], T.st[:, t]), dve_tick)
            c.done()
            dve.tensor_scalar(T.ve[:], T.mv[:, :, 1], EPS, None, ALU.add).then_inc(T.stats_done, 1)

        def layernorm(T, b, readers):
            wait(dve, T.stats_done, b + 1)
            wait(dve, T.root_done, b + 1)
            c = Steps(dve, T.newton_chain, 2, b)
            c.link(dve.tensor_tensor(T.yy[:], T.y0[:], T.y0[:], ALU.mult))
            c.link(dve.scalar_tensor_tensor(T.yy[:], T.yy[:], -0.5, T.ve[:], ALU.mult, ALU.mult))
            c.done()
            dve.scalar_tensor_tensor(T.rstd[:], T.yy[:], 1.5, T.y0[:], ALU.add, ALU.mult).then_inc(T.rstd_done, 1)
            wait(dve, T.rstd_done, b + 1)
            for sem_, count in readers:
                wait(dve, sem_, count)
            for t in range(TT):
                last = dve.tensor_scalar(T.out[:, t], T.r[:, t], T.mv[:, t, 0:1], T.rstd[:, t:t + 1],
                                         ALU.subtract, ALU.mult)
            last.then_inc(T.ln_done, 1)

        evac_q(A, 0)
        split_k(A, 0)
        dve.wait_ge(C.wts_in, 16 * 11)

        def iteration(i):
            for h in range(H):
                if has(i, 0):
                    read_max(A, i, h)
                if has(i, -2) and h == 8:
                    normalise(C, i - 2, 0)
                if has(i, -1):
                    if h == 5:
                        b = i - 1
                        evac_q(C, b)
                        wait(dve, C.keep_in, 16 * (b + 1))
                        wait(dve, C.k_split, b)
                        dve.tensor_scalar(C.keep[:], C.keep_i[:], 0.0, None, ALU.not_equal).then_inc(C.keep_done, 1)
                    if h == 9:
                        split_k(C, i - 1)
            if has(i, 0):
                split_max(A, i)
            if has(i, -2):
                b = i - 2
                normalise(C, b, 1)
                residual(C, b)
                layernorm(C, b, ((x2_written, 16 * b), (x2T_full, b)))
            for h in range(H):
                if has(i, -1):
                    read_max(C, i - 1, h)
                if has(i, 0) and h == 8:
                    normalise(A, i, 0)
                if has(i, 1):
                    if h == 3:
                        evac_q(A, i + 1)
                    if h == 7:
                        split_k(A, i + 1)
            if has(i, -1):
                split_max(C, i - 1)
            if has(i, 0):
                normalise(A, i, 1)
                residual(A, i)
                layernorm(A, i, ((C.res_copied, i), (C.src_full, i)))

        schedule(dve, iteration)

def experts(nc, ctx, xT2, x2_d, w_r, w_1, w_2, out):
    def sb(n, shape, dt):
        return ctx.enter_context(nc.sbuf_tensor(n, shape, dt))

    def sem(n):
        return ctx.enter_context(nc.semaphore(n))

    NT = B * TT
    CT = CHUNK // P
    wr = sb("wr", [P, KT, E], F32)
    w1 = sb("w1", [P, 2, KT, F], F32)
    w2 = sb("w2", [P, 2, FT, D], F32)
    x2 = sb("x2s", [P, NT, D], F32)
    hid = sb("hid", [P, 2, FT, CHUNK], F32)
    y = sb("y", [P, NT, D], F32)
    lg = sb("lg", [P, NT, E], F32)
    mx = sb("rmx", [P, NT], F32)
    g = sb("g", [P, NT, E], F32)
    gs = sb("gs", [P, NT], F32)
    below = sb("below", [P, E, E], F32)
    gt = sb("gt", [P, NT, E, E], F32)
    eq = sb("eq", [P, NT, E, E], F32)
    rank = sb("rank", [P, NT, E], F32)
    st = sb("fst", [P, NT, 6], F32)
    mv = sb("fmv", [P, NT, 2], F32)
    ve = sb("fve", [P, NT], F32)
    lnv = sb("flnv", [P, NT], F32)
    y0 = sb("fy0", [P, NT], F32)
    yy = sb("fyy", [P, NT], F32)
    rstd = sb("frstd", [P, NT], F32)
    ph = ctx.enter_context(nc.psum_tensor("ph", [P, 4, CHUNK], F32))
    py = ctx.enter_context(nc.psum_tensor("py", [P, 2, 512], F32))
    pr = ctx.enter_context(nc.psum_tensor("pr", [P, NT * E], F32))

    wr_in = sem("wr_in")
    x2_in = sem("x2_in")
    w_in = [sem("w_in0"), sem("w_in1")]
    below_ready = sem("below_ready")
    logits_full = sem("logits_full")
    router = sem("router")
    shifted = sem("shifted")
    exp_done = sem("gate_exp_done")
    h_full = sem("h_full")
    relu_done = sem("relu_done")
    y_full = sem("y_full")
    y_added = sem("y_added")
    fin = sem("fin")
    stats = sem("fstats")
    lns = sem("flns")
    root = sem("froot")
    outs = sem("outs")
    stored = sem("stored")
    tick = sem("sp_tick2")
    block = ctx.enter_context(nc.Block())

    @block.sync
    def _(sp):
        sp.dma_start(wr[:], w_r.rearrange("(k p) e -> p k e", p=P)).then_inc(wr_in, 16)

        def load(e, u, round_):
            if not isinstance(round_, int) or round_ > 0:
                fence(sp, y_full, NT * (e - 1), tick)
            sp.dma_start(w1[:, u], w_1[e].rearrange("(k p) f -> p k f", p=P)).then_inc(w_in[u], 16)
            sp.dma_start(w2[:, u], w_2[e].rearrange("(k p) n -> p k n", p=P)).then_inc(w_in[u], 16)

        load(0, 0, 0)
        load(1, 1, 0)
        sp.dma_start(x2[:], x2_d.rearrange("b (t p) d -> p (b t) d", p=P)).then_inc(x2_in, 16)
        with sp.Fori(1, E // 2) as i:
            for u in range(2):
                load(2 * i + u, u, i)
        for t in range(NT):
            if t % 4 == 0:
                sp.wait_ge(outs, t + 4)
                sp.dma_start(out.rearrange("b (t p) d -> p (b t) d", p=P)[:, t:t + 4], y[:, t:t + 4]).then_inc(stored, 16)
        sp.wait_ge(stored, 16 * NT // 4)

    @block.gpsimd
    def _(pool):
        pool.memset(below[:], 1.0).then_inc(below_ready, 1)
        pool.wait_ge(below_ready, 1)
        pool.affine_select(out=below[:], in_=below[:], compare_op=ALU.is_gt, fill=0.0, base=0,
                           pattern=[[1, E], [-1, E]], channel_multiplier=0).then_inc(below_ready, 1)

    @block.tensor
    def _(pe):
        pe.wait_ge(wr_in, 16)
        for t in range(NT):
            for k in range(KT):
                last = pe.matmul(pr[:, t * E:(t + 1) * E], xT2[:, k, t * P:(t + 1) * P], wr[:, k], start=(k == 0), stop=(k == KT - 1))
        last.then_inc(logits_full, 1)

        def hidden(e, u, c):
            for f in range(FT):
                n = FT * NCHUNK * e + FT * c + f
                if not (isinstance(e, int) and n < 4):
                    pe.wait_ge(relu_done, n - 3)
                for k in range(KT):
                    last = pe.matmul(ph[:, f % 4], w1[:, u, k, f * P:(f + 1) * P],
                                     xT2[:, k, c * CHUNK:(c + 1) * CHUNK], start=(k == 0), stop=(k == KT - 1))
                last.then_inc(h_full, 1)

        def expert(e, u, i):
            pe.wait_ge(w_in[u], 32 * (i + 1))
            for c in range(NCHUNK):
                hidden(e, u, c)
                for t in range(CT):
                    n = NT * e + CT * c + t
                    if not (isinstance(e, int) and n < 2):
                        pe.wait_ge(y_added, n - 1)
                    for f in range(FT):
                        if t == 0:
                            pe.wait_ge(relu_done, FT * NCHUNK * e + FT * c + f + 1)
                        last = pe.matmul(py[:, t % 2, 0:D], hid[:, c % 2, f, t * P:(t + 1) * P], w2[:, u, f],
                                         start=(f == 0), stop=(f == FT - 1))
                    last.then_inc(y_full, 1)

        for u in range(2):
            expert(u, u, 0)
        with pe.Fori(1, E // 2) as i:
            for u in range(2):
                expert(2 * i + u, u, i)

    @block.scalar
    def _(act):
        act.wait_ge(shifted, 1)
        act.activation(g[:], lg[:], ACT.Exp).then_inc(exp_done, 1)

        def expert(e, u):
            for c in range(NCHUNK):
                for f in range(FT):
                    n = FT * NCHUNK * e + FT * c + f
                    act.wait_ge(h_full, n + 1)
                    if f == 0 and not (isinstance(e, int) and e == 0 and c < 2):
                        act.wait_ge(y_full, NT * e + CT * (c - 1))
                    act.activation(hid[:, c % 2, f], ph[:, f % 4], ACT.Relu).then_inc(relu_done, 1)

        for u in range(2):
            expert(u, u)
        with act.Fori(1, E // 2) as i:
            for u in range(2):
                expert(2 * i + u, u)
        act.wait_ge(stats, 1)
        act.activation(lnv[:], ve[:], ACT.Ln).then_inc(lns, 1)
        act.wait_ge(lns, 1)
        act.activation(y0[:], lnv[:], ACT.Exp, scale=-0.5).then_inc(root, 1)

    @block.vector
    def _(dve):
        c = Steps(dve, router, 100, 0)
        c.link(dve.memset(y[:], 0.0))
        dve.wait_ge(logits_full, 1)
        l3 = pr[:].rearrange("p (t e) -> p t e", e=E)
        c.link(dve.tensor_reduce(mx[:], l3, X, ALU.max))
        dve.tensor_tensor(lg[:], l3, mx[:].unsqueeze(2).to_broadcast((P, NT, E)), ALU.subtract).then_inc(shifted, 1)
        dve.wait_ge(exp_done, 1)
        c.link(dve.tensor_reduce(gs[:], g[:], X, ALU.add))
        c.link(dve.reciprocal(gs[:], gs[:]))
        c.link(dve.tensor_tensor(g[:], g[:], gs[:].unsqueeze(2).to_broadcast((P, NT, E)), ALU.mult))
        own = g[:].unsqueeze(3).to_broadcast((P, NT, E, E))
        other = g[:].unsqueeze(2).to_broadcast((P, NT, E, E))
        c.link(dve.tensor_tensor(gt[:], other, own, ALU.is_gt))
        c.link(dve.tensor_tensor(eq[:], other, own, ALU.is_equal))
        dve.wait_ge(below_ready, 2)
        c.link(dve.tensor_tensor(eq[:], eq[:], below[:].unsqueeze(1).to_broadcast((P, NT, E, E)), ALU.mult))
        c.link(dve.tensor_tensor(gt[:], gt[:], eq[:], ALU.add))
        c.link(dve.tensor_reduce(rank[:], gt[:], X, ALU.add))
        c.link(dve.scalar_tensor_tensor(g[:], rank[:], 2.0, g[:], ALU.is_lt, ALU.mult))
        c.link(dve.tensor_reduce(gs[:], g[:], X, ALU.add))
        c.link(dve.reciprocal(gs[:], gs[:]))
        c.link(dve.tensor_tensor(g[:], g[:], gs[:].unsqueeze(2).to_broadcast((P, NT, E)), ALU.mult))

        def expert(e, u, i):
            for t in range(NT):
                n = NT * e + t
                dve.wait_ge(y_full, n + 1)
                if not (isinstance(e, int) and e == 0):
                    dve.wait_ge(y_added, n - NT + 1)
                weight = g[:, t, u:u + 1] if isinstance(e, int) else g[:, t, bass.ds(2 * i + u, 1)]
                dve.scalar_tensor_tensor(y[:, t], py[:, t % 2, 0:D], weight, y[:, t], ALU.mult, ALU.add)\
                   .then_inc(y_added, 1)

        for u in range(2):
            expert(u, u, 0)
        with dve.Fori(1, E // 2) as i:
            for u in range(2):
                expert(2 * i + u, u, i)
        c = Steps(dve, fin, 100, 0)
        dve.wait_ge(x2_in, 16)
        dve.wait_ge(y_added, NT * E)
        c.link(dve.tensor_tensor(y[:], y[:], x2[:], ALU.add))
        for t in range(NT):
            c.link(dve.bn_stats(st[:, t], y[:, t]))
        for t in range(NT):
            c.link(dve.bn_aggr(mv[:, t], st[:, t]))
        dve.tensor_scalar(ve[:], mv[:, :, 1], EPS, None, ALU.add).then_inc(stats, 1)
        dve.wait_ge(root, 1)
        dve.wait_ge(stats, 1)
        c.link(dve.tensor_tensor(yy[:], y0[:], y0[:], ALU.mult))
        c.link(dve.scalar_tensor_tensor(yy[:], yy[:], -0.5, ve[:], ALU.mult, ALU.mult))
        c.link(dve.scalar_tensor_tensor(rstd[:], yy[:], 1.5, y0[:], ALU.add, ALU.mult))
        for t in range(NT):
            dve.tensor_scalar(y[:, t], y[:, t], mv[:, t, 0:1], rstd[:, t:t + 1], ALU.subtract, ALU.mult).then_inc(outs, 1)


def kernel(**inputs):
    import numpy as np
    import concourse.bacc as bacc
    from concourse.bass_utils import run_bass_kernel_spmd

    cycles = np.array([5 + h % 4 for h in range(H)])
    phases = np.arange(S)[None, :] % cycles[:, None]
    raw = np.asarray(inputs["L0_attn_bandha_gate"])
    gate_rows = np.repeat(np.take_along_axis(raw, phases, axis=1), HD, axis=0)
    arrays = {
        "x": inputs["x"], "ctx_in": inputs["ctx_1024"],
        "mask": np.asarray(inputs["mask_Bx1x1xS2_ik0"]).reshape(B, S),
        "w_qkv": inputs["L0_attn_w_qkv"], "w_o1": inputs["L0_attn_w_out"], "gate_raw": gate_rows,
        "wqT": np.asarray(inputs["L0_xattn_Wq"]).T, "bq": np.asarray(inputs["L0_xattn_bq"]).reshape(KT, P).T,
        "wkT": np.asarray(inputs["L0_xattn_Wk"]).T, "bk": np.asarray(inputs["L0_xattn_bk"]).reshape(KT, P).T,
        "wvT": np.asarray(inputs["L0_xattn_Wv"]).T, "bv": inputs["L0_xattn_bv"],
        "woT": np.asarray(inputs["L0_xattn_Wo"]).T, "bo": inputs["L0_xattn_bo"],
        "w_r": inputs["L0_ffn_Wr"], "w_1": inputs["L0_ffn_W1"], "w_2": inputs["L0_ffn_W2"],
    }
    nc = bacc.Bacc("TRN2", target_bir_lowering=False, num_devices=1)
    arrays = {n: np.ascontiguousarray(a) for n, a in arrays.items()}
    args = [nc.dram_tensor(n, a.shape, mybir.dt.from_np(a.dtype), kind="ExternalInput").ap()
            for n, a in arrays.items()]
    args.append(nc.dram_tensor("out", (B, S, D), F32, kind="ExternalOutput").ap())
    decoder_layer(nc, *args)
    r = run_bass_kernel_spmd(nc, [arrays], core_ids=[0])
    return r.results[0]["out"]
```

```python
from contextlib import ExitStack

import concourse.bass as bass
from concourse import mybir

F32 = mybir.dt.float32
BF16 = mybir.dt.bfloat16
I32 = mybir.dt.int32
ALU = mybir.AluOpType
ACT = mybir.ActivationFunctionType
X = mybir.AxisListType.X

P = 128
B, S, D = 8, 256, 256
H, HD = 16, 16
KT = D // P
TT = S // P
E, F = 8, 1024
FT = F // P
EPS = 1e-5
CAUSAL_FILL = -1e30
MASKED_SCORE = -1e9
TOP = 2
NT = B * TT
TILE = 256
NTILE = (B * S * TOP + E * (TILE - 1)) // TILE
ZERO_ROWS = -(-NTILE * TILE // (B * P)) * P

Q_PARTS = (0, 0, 0, 1, 1, 2)
K_PARTS = (0, 1, 2, 0, 1, 0)
STACK = HD * len(Q_PARTS)
MASK_ROWS = 3
MAX_ROWS = 3
LAG = 3
WLAG = 2


def wait(eng, sem, value):
    if isinstance(value, int) and value <= 0:
        return
    eng.wait_ge(sem, value)


def fence(eng, sem, value, tick):
    wait(eng, sem, value)
    if not isinstance(value, int):
        eng.sem_inc(tick)


class Steps:

    def __init__(self, eng, sem, per_batch, batch):
        self.eng, self.sem, self.count, self.end = eng, sem, batch * per_batch, per_batch
        self.n = 0

    def link(self, instruction, tick=None):
        self.n += 1
        assert self.n <= self.end
        instruction.then_inc(self.sem, 1)
        if tick is None:
            wait(self.eng, self.sem, self.count + self.n)
        else:
            fence(self.eng, self.sem, self.count + self.n, tick)

    def done(self):
        assert self.n == self.end


class Stream:

    def __init__(self, nc, ctx, name, cross):
        def sb(n, shape, dt):
            return ctx.enter_context(nc.sbuf_tensor(f"{name}_{n}", shape, dt))

        self.name, self.cross = name, cross
        def sem(n):
            return ctx.enter_context(nc.semaphore(f"{name}_{n}"))

        self.src_in = sem("src_in")
        self.src_evac = sem("src_evac")
        self.src_full = sem("src_full")
        self.kv_in = sem("kv_in")
        self.kv_full = sem("kv_full")
        self.kv_evac = sem("kv_evac")
        self.q_full = sem("q_full")
        self.q_evac = sem("q_evac")
        self.k_full = sem("k_full")
        self.k_evac = sem("k_evac")
        self.q_split = sem("q_split")
        self.k_split = sem("k_split")
        self.q_written = sem("q_written")
        self.k_written = sem("k_written")
        self.q_stacked = sem("q_stacked")
        self.k_stacked = sem("k_stacked")
        self.v_full = sem("v_full")
        self.v_evac = sem("v_evac")
        self.nm_split = sem("nm_split")
        self.nm_full = sem("nm_full")
        self.nm_evac = sem("nm_evac")
        self.m_written = sem("m_written")
        self.m_stacked = sem("m_stacked")
        self.weights_full = sem("weights_full")
        self.aT_full = sem("aT_full")
        self.aT_evac = sem("aT_evac")
        self.norm_done = sem("norm_done")
        self.o_full = sem("o_full")
        self.res_done = sem("res_done")
        self.res_copied = sem("res_copied")
        self.stats_done = sem("stats_done")
        self.rstd_done = sem("rstd_done")
        self.ln_taken = sem("ln_taken")
        self.root_done = sem("root_done")
        self.newton_chain = sem("newton_chain")
        self.ln_done = sem("ln_done")
        self.qsplit_chain = sem("qsplit_chain")
        self.ksplit_chain = sem("ksplit_chain")
        self.nm_chain = sem("nm_chain")
        self.norm_chain = sem("norm_chain")
        self.ln_chain = sem("ln_chain")
        self.keep_in = sem("keep_in")
        self.keep_done = sem("keep_done")
        self.wts_in = sem("wts_in")
        self.wq = sb("wq", [P, KT, D], F32)
        self.wk = sb("wk", [P, KT, D], F32)
        self.wv = sb("wv", [P, KT, D], F32)
        self.wo = sb("wo", [P, KT, D], F32)
        self.src = sb("src", [P, TT, D], F32)
        self.xT = sb("xT", [P, KT, S], F32)
        self.cT = sb("cT", [P, KT, S], F32) if cross else self.xT
        self.res = sb("res", [P, TT, D], F32)
        self.qf = sb("qf", [P, KT, S], F32)
        self.kf = sb("kf", [P, KT, S], F32)
        self.kfm = sb("kfm", [P, KT, S], F32) if cross else self.kf
        self.qr = sb("qr", [P, KT, S], F32)
        self.kr = sb("kr", [P, KT, S], F32)
        self.qp = sb("qp", [P, 3, KT, S], BF16)
        self.kp = sb("kp", [P, 3, KT, S], BF16)
        self.qs = sb("qs", [P, 2, H, S], BF16)
        self.ks = sb("ks", [P, 2, H, S], BF16)
        self.v = sb("v", [P, TT, H, 32], F32)
        self.mx = sb("mx", [P, TT, H], F32)
        self.nf = sb("nf", [P, TT, H], F32)
        self.nr = sb("nr", [P, TT, H], F32)
        self.np = sb("np", [P, TT, 3, H], BF16)
        self.npT = sb("npT", [3 * H, S], BF16)
        self.pvs = sb("pvs", [P, 4, S], F32)
        self.rec = sb("rec", [P, TT, H // 2], F32)
        self.an = sb("an", [P, TT, D], F32)
        self.aT = sb("aT", [P, KT, S], F32)
        self.r = sb("r", [P, TT, D], F32)
        self.st = sb("st", [P, TT, 6], F32)
        self.mv = sb("mv", [P, TT, 2], F32)
        self.ve = sb("ve", [P, TT], F32)
        self.lnv = sb("lnv", [P, TT], F32)
        self.y0 = sb("y0", [P, TT], F32)
        self.yy = sb("yy", [P, TT], F32)
        self.rstd = sb("rstd", [P, TT], F32)
        self.out = sb("out", [P, TT, D], F32)
        if cross:
            self.bq = sb("bq", [P, KT], F32)
            self.bk = sb("bk", [P, KT], F32)
            self.bv = sb("bv", [P, D], F32)
            self.bo = sb("bo", [P, D], F32)
            self.keep_i = sb("keep_i", [P, S], I32)
            self.keep = sb("keep", [P, S], F32)
        self.mask_rows = MASK_ROWS if cross else 0
        self.max_k = STACK + self.mask_rows
        self.st_k = self.max_k + MAX_ROWS
        self.parts_d = nc.dram_tensor(f"{name}_parts", (2, 3, KT, P, S), BF16, kind="Internal").ap()
        self.m_d = nc.dram_tensor(f"{name}_m", (3, H, S), BF16, kind="Internal").ap()
        self.pp = ctx.enter_context(nc.psum_tensor(f"{name}_pp", [P, 512], F32))

    def order(self, b):
        if isinstance(b, int):
            return max(0, 2 * b - 1) if not self.cross else min(2 * b + 2, B + b)
        return 2 * b + 2 if self.cross else 2 * b - 1

    def head(self, b, h):
        return H * self.order(b) + h

    def through(self, b):
        return 0 if isinstance(b, int) and b < 0 else H * (self.order(b) + 1)


def decoder_layer(nc, x, ctx_in, mask, w_qkv, w_o1, gate_raw, wqT, bq, wkT, bk, wvT, bv, woT, bo,
                  w_r, w_1, w_2, out):
    with ExitStack() as outer:
        x2 = outer.enter_context(nc.sbuf_tensor("x2", [P, NT, D], F32))
        lg = outer.enter_context(nc.sbuf_tensor("lg", [P, NT * E], F32))
        xs_d = nc.dram_tensor("sorted_x", (B * ZERO_ROWS, D), F32, kind="Internal").ap()
        with ExitStack() as ctx:
            attention(nc, ctx, x2, lg, xs_d, x, ctx_in, mask, w_qkv, w_o1, gate_raw, wqT, bq, wkT, bk, wvT, bv,
                      woT, bo, w_r)
        with ExitStack() as ctx:
            experts(nc, ctx, x2, lg, xs_d, w_1, w_2, out)


def attention(nc, ctx, x2, lg, xs_d, x, ctx_in, mask, w_qkv, w_o1, gate_raw, wqT, bq, wkT, bk, wvT, bv,
              woT, bo, w_r):
    def sb(n, shape, dt):
        return ctx.enter_context(nc.sbuf_tensor(n, shape, dt))

    def sem(n):
        return ctx.enter_context(nc.semaphore(n))

    A = Stream(nc, ctx, "self", False)
    C = Stream(nc, ctx, "cross", True)
    identf = sb("identf", [P, P], F32)
    identb = sb("identb", [P, P], BF16)
    tri_qk = sb("tri_qk", [P, P], BF16)
    tri_kq = sb("tri_kq", [P, P], BF16)
    gate = sb("gate", [P, KT, S], F32)
    zeros = sb("zeros", [P, D], F32)
    wr = sb("wr", [P, KT, E], F32)
    x2T = sb("x2T", [P, KT, S], F32)
    p = sb("p", [P, 4, 2 * S], F32)
    pm = ctx.enter_context(nc.psum_tensor("pm", [P, 2, 512], F32))
    ps = ctx.enter_context(nc.psum_tensor("ps", [P, 2, 512], F32))
    pv = ctx.enter_context(nc.psum_tensor("pv", [P, 2, 512], F32))
    mrow_i = sb("mrow_i", [B, S], I32)
    mrow = sb("mrow", [B, S], F32)
    mres = sb("mres", [B, S], F32)
    mparts = sb("mparts", [B, 3, S], BF16)
    mparts_d = nc.dram_tensor("mask_parts", (3, B, S), BF16, kind="Internal").ap()

    const_ready = sem("const_ready")
    pool_setup = sem("pool_setup")
    gate_in = sem("gate_in")
    gate_exp = sem("gate_exp")
    gate_chain = sem("gate_chain")
    gate_ready = sem("gate_ready")
    mrow_in = sem("mrow_in")
    mask_chain = sem("mask_chain")
    mask_written = sem("mask_written")
    mask_stacked = sem("mask_stacked")
    x2_written = sem("x2_written")
    x2T_full = sem("x2T_full")
    x2T_evac = sem("x2T_evac")
    wr_in = sem("wr_in")
    max_full = sem("max_full")
    max_read = sem("max_read")
    st_full = sem("st_full")
    exp_done = sem("exp_done")
    pv_full = sem("pv_full")
    pv_evac = sem("pv_evac")
    cleared = sem("cleared")
    logits_full = sem("logits_full")
    logits_evac = sem("logits_evac")
    dve_setup = sem("dve_setup")
    pool_tick, pe_tick, dve_tick, sp_tick = (sem(n) for n in ("pool_tick", "pe_tick", "dve_tick", "sp_tick"))

    block = ctx.enter_context(nc.Block())

    def schedule(eng, iteration):
        for i in range(3):
            iteration(i, i % 2)
        with eng.Fori(1, (B - 1) // 2) as k:
            for u in range(2):
                iteration(2 * k + 1 + u, 1 - u)
        for i in range((B - 1) // 2 * 2 + 1, B + 2):
            iteration(i, i % 2)

    def has(i, shift):
        return not isinstance(i, int) or 0 <= i + shift < B

    @block.sync
    def _(sp):
        def load_weights(T, wq, wk, wv, wo):
            for dst, src in ((T.wq, wq), (T.wk, wk), (T.wv, wv), (T.wo, wo)):
                sp.dma_start(dst[:], src.rearrange("(k p) n -> p k n", p=P)).then_inc(T.wts_in, 16)

        def load_src(T, src, b, full):
            fence(sp, full, b, sp_tick)
            sp.dma_start(T.src[:], src[b].rearrange("(t p) d -> p t d", p=P)).then_inc(T.src_in, 16)

        def bounce(T, b, which, split, parts, written):
            fence(sp, split, b + 1, sp_tick)
            fence(sp, T.q_stacked if which == 0 else T.k_stacked, 96 * b, sp_tick)
            sp.dma_start(T.parts_d[which].rearrange("s k p t -> p s k t"), parts[:]).then_inc(written, 16)

        def stack(T, b, par, which, written, order, dst, stacked):
            fence(sp, written, 16 * (b + 1), sp_tick)
            fence(sp, st_full, T.through(b - 2), sp_tick)
            for s, part in enumerate(order):
                src = T.parts_d[which, part].rearrange("k (h d) t -> d (k h) t", d=HD)
                sp.dma_start(dst[HD * s:HD * s + HD, par], src).then_inc(stacked, 16)

        def stack_max(T, b, par):
            fence(sp, T.nm_evac, b + 1, sp_tick)
            fence(sp, T.m_stacked, 16 * b, sp_tick)
            sp.dma_start(T.m_d.rearrange("s h t -> (s h) t"), T.npT[:]).then_inc(T.m_written, 16)
            fence(sp, T.m_written, 16 * (b + 1), sp_tick)
            sp.dma_start(T.qs[T.max_k:T.max_k + MAX_ROWS, par], T.m_d).then_inc(T.m_stacked, 16)

        def bring_q(T, b, par):
            bounce(T, b, 0, T.q_split, T.qp, T.q_written)
            stack(T, b, par, 0, T.q_written, Q_PARTS, T.qs, T.q_stacked)

        def bring_k(T, b, par):
            bounce(T, b, 1, T.k_split, T.kp, T.k_written)
            stack(T, b, par, 1, T.k_written, K_PARTS, T.ks, T.k_stacked)

        def load_context(b):
            load_src(C, ctx_in, b, C.kv_full)
            fence(sp, C.keep_done, b, sp_tick)
            sp.dma_start(C.keep_i[:], mask[b].partition_broadcast(P)).then_inc(C.keep_in, 16)

        sp.dma_start(gate[:], gate_raw.rearrange("(k p) t -> p k t", p=P)).then_inc(gate_in, 16)
        sp.dma_start(A.src[:], x[0].rearrange("(t p) d -> p t d", p=P)).then_inc(A.src_in, 16)
        load_weights(A, w_qkv[:, 0:D], w_qkv[:, D:2 * D], w_qkv[:, 2 * D:3 * D], w_o1)
        sp.dma_start(wr[:], w_r.rearrange("(k p) e -> p k e", p=P)).then_inc(wr_in, 16)
        sp.dma_start(mrow_i[:], mask).then_inc(mrow_in, 16)
        load_weights(C, wqT, wkT, wvT, woT)
        sp.dma_start(C.bq[:], bq).then_inc(C.wts_in, 16)
        sp.dma_start(C.bk[:], bk).then_inc(C.wts_in, 16)
        sp.dma_start(C.bv[:], bv.partition_broadcast(P)).then_inc(C.wts_in, 16)
        sp.dma_start(C.bo[:], bo.partition_broadcast(P)).then_inc(C.wts_in, 16)
        sp.wait_ge(dve_setup, 1)
        sp.dma_start(mparts_d.rearrange("s b t -> b s t"), mparts[:]).then_inc(mask_written, 16)
        sp.wait_ge(mask_written, 16)
        bring_q(A, 0, 0)
        bring_k(A, 0, 0)

        def iteration(i, odd):
            if has(i, -1):
                b = i - 1
                bring_k(C, b, 1 - odd)
                fence(sp, st_full, C.through(b - 2), sp_tick)
                rows = mparts_d[:, b, :].unsqueeze(1).to_broadcast((3, H, S))
                sp.dma_start(C.ks[STACK:STACK + MASK_ROWS, 1 - odd], rows).then_inc(mask_stacked, 16)
            if has(i, 1):
                fence(sp, A.res_copied, i + 1, sp_tick)
                load_src(A, x, i + 1, A.src_full)
            if has(i, -1):
                bring_q(C, i - 1, 1 - odd)
            if has(i, 0):
                stack_max(A, i, odd)
                load_context(i)
            if has(i, 1):
                bring_q(A, i + 1, 1 - odd)
                bring_k(A, i + 1, 1 - odd)
            if has(i, -2):
                b = i - 2
                fence(sp, C.ln_done, b + 1, sp_tick)
                sp.dma_start(x2[:, bass.ds(b * TT, TT)], C.out[:]).then_inc(x2_written, 16)
                sp.dma_start(xs_d[bass.ds(b * ZERO_ROWS, ZERO_ROWS)].rearrange("(n p) d -> p n d", p=P),
                             zeros[:].unsqueeze(1).to_broadcast((P, ZERO_ROWS // P, D))).then_inc(cleared, 16)
            if has(i, -1):
                stack_max(C, i - 1, 1 - odd)

        schedule(sp, iteration)
        sp.wait_ge(x2_written, 16 * B)
        sp.wait_ge(cleared, 16 * B)

    @block.gpsimd
    def _(pool):
        setup = Steps(pool, pool_setup, 100, 0)
        for m in (identf, identb, tri_qk, tri_kq):
            setup.link(pool.memset(m[:], 0.0))
        for m in (identf, identb):
            setup.link(pool.affine_select(out=m[:], in_=m[:], compare_op=ALU.not_equal, fill=1.0, base=0,
                                          pattern=[[-1, P]], channel_multiplier=1))
        setup.link(pool.affine_select(out=tri_qk[:], in_=tri_qk[:], compare_op=ALU.is_ge, fill=CAUSAL_FILL,
                                      base=0, pattern=[[-1, P]], channel_multiplier=1))
        setup.link(pool.affine_select(out=tri_kq[:], in_=tri_kq[:], compare_op=ALU.is_ge, fill=CAUSAL_FILL,
                                      base=0, pattern=[[1, P]], channel_multiplier=-1))
        setup.link(pool.memset(zeros[:], 0.0))
        for T in (A, C):
            setup.link(pool.memset(T.v[:], 1.0))
            setup.link(pool.memset(T.qs[STACK:P], 1.0))
            setup.link(pool.memset(T.ks[STACK:P], 1.0))
        pool.drain().then_inc(const_ready, 1)

        def split_q(T, b):
            wait(pool, T.q_evac, b + 1)
            fence(pool, T.q_written, 16 * b, pool_tick)
            c = Steps(pool, T.qsplit_chain, 3, b)
            c.link(pool.tensor_copy(T.qp[:, 0], T.qf[:]))
            c.link(pool.tensor_tensor(T.qr[:], T.qf[:], T.qp[:, 0], ALU.subtract), pool_tick)
            c.link(pool.tensor_copy(T.qp[:, 1], T.qr[:]))
            c.done()
            pool.tensor_tensor(T.qp[:, 2], T.qr[:], T.qp[:, 1], ALU.subtract).then_inc(T.q_split, 1)

        split_q(A, 0)
        pool.wait_ge(C.wts_in, 16 * 8)

        def iteration(i, odd):
            if has(i, 0):
                wait(pool, A.src_in, 16 * (i + 1))
                fence(pool, A.res_done, i, pool_tick)
                pool.tensor_copy(A.res[:], A.src[:]).then_inc(A.res_copied, 1)
            if has(i, 1):
                split_q(A, i + 1)
            if has(i, -1):
                wait(pool, A.ln_done, i)
                fence(pool, C.res_done, i - 1, pool_tick)
                pool.tensor_tensor(C.res[:], A.out[:], C.bo[:].unsqueeze(1).to_broadcast((P, TT, D)), ALU.add)\
                    .then_inc(C.res_copied, 1)

        schedule(pool, iteration)

    @block.tensor
    def _(pe):
        pe.wait_ge(const_ready, 1)

        def transpose(T, src, dst_full):
            for k in range(KT):
                for t in range(TT):
                    o = (k * TT + t) * P
                    last = pe.transpose(T.pp[:, o:o + P], src[:, t, k * P:(k + 1) * P], identf[:])
            last.then_inc(dst_full, 1)

        def features(T, w, rhs, full):
            for m in range(KT):
                for k in range(KT):
                    last = pe.matmul(T.pp[:, m * S:(m + 1) * S], w[:, k, m * P:(m + 1) * P], rhs[:, k, :],
                                     start=(k == 0), stop=(k == KT - 1))
            last.then_inc(full, 1)

        def values(T, b, before, count):
            wait(pe, before, count)
            for t in range(TT):
                o = T.pp[:, t * D:(t + 1) * D]
                for k in range(KT):
                    last = pe.matmul(o, T.cT[:, k, t * P:(t + 1) * P], T.wv[:, k, :],
                                     start=(k == 0), stop=(k == KT - 1))
            last.then_inc(T.v_full, 1)

        def scores_for_max(T, b, par, h):
            if h == 0:
                wait(pe, T.q_stacked, 96 * (b + 1))
                wait(pe, T.k_stacked, 96 * (b + 1))
                if T.cross:
                    wait(pe, mask_stacked, 16 * (b + 1))
            wait(pe, max_read, T.head(b, h) - 1)
            q, k = T.qs[0:T.max_k, par, h], T.ks[0:T.max_k, par, h]
            bank = pm[:, h % 2]
            if T.cross:
                for t in range(TT):
                    last = pe.matmul(bank[:, t * S:(t + 1) * S], q[:, t * P:(t + 1) * P], k, start=True, stop=True)
            else:
                for t, o in ((0, 0), (1, P)):
                    n = (t + 1) * P
                    pe.matmul(bank[:, o:o + n], q[:, t * P:(t + 1) * P], k[:, 0:n], start=True, stop=False)
                    last = pe.matmul(bank[:, o + n - P:o + n], identb[:], tri_qk[:], start=False, stop=True)
            last.then_inc(max_full, 1)

        def transpose_max(T, b):
            wait(pe, T.nm_split, b + 1)
            if T.cross and has(b, -1):
                fence(pe, logits_evac, b, pe_tick)
            else:
                fence(pe, T.v_evac, b + 1, pe_tick)
            pp = T.pp[:].bitcast(BF16)
            for t in range(TT):
                last = pe.transpose(pp[0:3 * H, t * P:(t + 1) * P],
                                    T.np[:, t].rearrange("p s h -> p (s h)"), identb[:])
            last.then_inc(T.nm_full, 1)

        def scores(T, b, par, h):
            if h == 0:
                wait(pe, T.m_stacked, 16 * (b + 1))
            wait(pe, exp_done, T.head(b, h) - 1)
            q, k = T.qs[0:T.st_k, par, h], T.ks[0:T.st_k, par, h]
            bank = ps[:, h % 2]
            if T.cross:
                for t in range(TT):
                    last = pe.matmul(bank[:, t * S:(t + 1) * S], k[:, t * P:(t + 1) * P], q, start=True, stop=True)
            else:
                for t, o in ((0, 0), (1, S)):
                    n = S - t * P
                    pe.matmul(bank[:, o:o + n], k[:, t * P:(t + 1) * P], q[:, t * P:S], start=True, stop=False)
                    last = pe.matmul(bank[:, o:o + P], identb[:], tri_kq[:], start=False, stop=True)
            last.then_inc(st_full, 1)

        def weigh_values(T, b, h):
            wait(pe, exp_done, T.head(b, h) + 1)
            if h == 0:
                wait(pe, T.v_evac, b + 1)
            if h % 8 == 0:
                wait(pe, pv_evac, 2 * T.order(b) + h // 8 - 1)
            g, o = h % 4, (h // 4 % 2) * S
            for t in range(TT):
                q0 = 0 if T.cross or t == 0 else P
                last = pe.matmul(pv[32 * g:32 * g + 32, h // 8, o + q0:o + S], T.v[:, t, h, :],
                                 p[:, h % 4, t * S:(t + 1) * S - q0], start=(t == 0), stop=(t == TT - 1))
            last.then_inc(pv_full, 1)

        def transpose_weighted(T, b, half, before, count):
            wait(pe, pv_evac, 2 * T.order(b) + half + 1)
            wait(pe, before, count)
            for t in range(TT):
                for g in range(2):
                    o = (t * 2 + g) * P
                    last = pe.transpose(T.pp[:, o:o + P], T.pvs[:, 2 * half + g, t * P:(t + 1) * P], identf[:])
            last.then_inc(T.weights_full, 1)

        def transpose_out(T, b):
            wait(pe, T.norm_done, 2 * (b + 1))
            transpose(T, T.an, T.aT_full)

        def project_out(T, b):
            wait(pe, T.aT_evac, b + 1)
            for t in range(TT):
                for k in range(KT):
                    last = pe.matmul(T.pp[:, t * D:(t + 1) * D], T.aT[:, k, t * P:(t + 1) * P], T.wo[:, k, :],
                                     start=(k == 0), stop=(k == KT - 1))
            last.then_inc(T.o_full, 1)

        def logits(b):
            wait(pe, x2T_evac, b + 1)
            if has(b, 1):
                wait(pe, C.v_evac, b + 2)
            for t in range(TT):
                for k in range(KT):
                    last = pe.matmul(C.pp[:, t * E:(t + 1) * E], x2T[:, k, t * P:(t + 1) * P], wr[:, k],
                                     start=(k == 0), stop=(k == KT - 1))
            last.then_inc(logits_full, 1)

        def transpose_x(b):
            wait(pe, A.src_in, 16 * (b + 1))
            wait(pe, A.nm_evac, b)
            transpose(A, A.src, A.src_full)

        def transpose_context(b):
            wait(pe, C.src_in, 16 * (b + 1))
            wait(pe, C.nm_evac, b)
            transpose(C, C.src, C.kv_full)

        def end(T, b, s, before, count):
            if s < WLAG:
                weigh_values(T, b, H - WLAG + s)
            if s == 3:
                transpose_weighted(T, b, 0, before, count)
            if s == 4:
                transpose_weighted(T, b, 1, T.norm_done, 2 * b + 1)
            if s == 6:
                transpose_out(T, b)
            if s == 7:
                project_out(T, b)

        pe.wait_ge(A.wts_in, 16 * 4)
        transpose_x(0)
        pe.wait_ge(A.src_evac, 1)
        features(A, A.wq, A.xT, A.q_full)
        pe.wait_ge(A.q_evac, 1)
        features(A, A.wk, A.xT, A.k_full)
        pe.wait_ge(C.wts_in, 16 * 8)
        pe.wait_ge(wr_in, 16)

        def iteration(i, odd):
            for s in range(H + LAG):
                if has(i, 0) and s < H:
                    scores_for_max(A, i, odd, s)
                if has(i, 0) and s == H:
                    transpose_max(A, i)
                if has(i, -2) and s >= LAG:
                    scores(C, i - 2, odd, s - LAG)
                    if s >= LAG + WLAG:
                        weigh_values(C, i - 2, s - LAG - WLAG)
                if has(i, -1):
                    end(A, i - 1, s, *((A.k_evac, i + 1) if has(i, 0) else (A.nm_evac, i)))
                if has(i, 0) and s == 8:
                    if has(i, -1):
                        values(A, i, A.res_done, i)
                    else:
                        values(A, i, A.k_evac, 1)
                if has(i, -1):
                    b = i - 1
                    if s == 0:
                        transpose_context(b)
                    if s == 2:
                        wait(pe, C.kv_evac, b + 1)
                        features(C, C.wk, C.cT, C.k_full)
                    if s == 10:
                        wait(pe, A.ln_done, b + 1)
                        wait(pe, C.k_evac, b + 1)
                        transpose(C, A.out, C.src_full)
                    if s == 12:
                        wait(pe, C.src_evac, b + 1)
                        features(C, C.wq, C.xT, C.q_full)
            for s in range(H + LAG):
                if has(i, -1) and s < H:
                    scores_for_max(C, i - 1, 1 - odd, s)
                if has(i, -1) and s == H:
                    transpose_max(C, i - 1)
                if has(i, 0) and s >= LAG:
                    scores(A, i, odd, s - LAG)
                    if s >= LAG + WLAG:
                        weigh_values(A, i, s - LAG - WLAG)
                if has(i, -2):
                    end(C, i - 2, s, *((C.q_evac, i) if has(i, -1) else (C.nm_evac, i - 1)))
                if has(i, 1):
                    if s == 0:
                        transpose_x(i + 1)
                    if s == 2:
                        wait(pe, A.src_evac, i + 2)
                        features(A, A.wq, A.xT, A.q_full)
                    if s == 5:
                        wait(pe, A.q_evac, i + 2)
                        features(A, A.wk, A.xT, A.k_full)
                if has(i, -1) and s == 8:
                    if has(i, -2):
                        values(C, i - 1, C.res_done, i - 1)
                    else:
                        values(C, i - 1, C.q_evac, i)
                if has(i, -2) and s == 11:
                    wait(pe, C.ln_done, i - 1)
                    if has(i, -1):
                        wait(pe, C.v_evac, i)
                    transpose(C, C.out, x2T_full)
                if has(i, -2) and s == 13:
                    logits(i - 2)

        schedule(pe, iteration)

    @block.scalar
    def _(act):
        nc.scalar.preload_act_table_set("natural_log_exp_and_others")
        act.wait_ge(gate_in, 16)
        act.activation(gate[:], gate[:], ACT.Exp, scale=-1.0).then_inc(gate_exp, 1)
        act.wait_ge(const_ready, 1)

        def copy(dst, src, full, b, evac):
            wait(act, full, b + 1)
            act.copy(dst, src).then_inc(evac, 1)

        def evac_k(T, b):
            wait(act, T.k_full, b + 1)
            wait(act, T.k_split, b)
            if T.cross:
                for m in range(KT):
                    last = act.activation(T.kf[:, m], T.pp[:, m * S:(m + 1) * S], ACT.Identity,
                                          bias=T.bk[:, m:m + 1])
            else:
                last = act.copy(T.kf[:], T.pp[:].rearrange("p (k t) -> p k t", k=KT))
            last.then_inc(T.k_evac, 1)

        def pp3(T):
            return T.pp[:].rearrange("p (k t) -> p k t", k=KT)

        def evac_v(T, b):
            wait(act, T.v_full, b + 1)
            for t in range(TT):
                last = act.copy(T.v[:, t, :, 0:HD],
                                T.pp[:, t * D:(t + 1) * D].rearrange("p (h d) -> p h d", h=H))
            last.then_inc(T.v_evac, 1)

        def exponentials(T, b, h):
            wait(act, st_full, T.head(b, h) + 1)
            wait(act, pv_full, T.head(b, h) - 3)
            n = 2 * S if T.cross else 2 * S - P
            act.activation(p[:, h % 4, 0:n], ps[:, h % 2, 0:n], ACT.Exp).then_inc(exp_done, 1)

        def evac_weighted(T, b, half):
            wait(act, pv_full, T.head(b, 8 * (half + 1)))
            wait(act, T.weights_full, 2 * b - 1 + half)
            act.copy(T.pvs[:, 2 * half:2 * half + 2], pv[:, half].rearrange("p (g t) -> p g t", g=2))\
               .then_inc(pv_evac, 1)

        def evac_max(T, b):
            wait(act, T.nm_full, b + 1)
            wait(act, T.m_written, 16 * b)
            act.copy(T.npT[:], T.pp[:].bitcast(BF16)[0:3 * H, 0:S]).then_inc(T.nm_evac, 1)

        def root(T, b):
            wait(act, T.stats_done, b + 1)
            wait(act, T.rstd_done, b)
            act.activation(T.lnv[:], T.ve[:], ACT.Ln).then_inc(T.ln_taken, 1)
            wait(act, T.ln_taken, b + 1)
            act.activation(T.y0[:], T.lnv[:], ACT.Exp, scale=-0.5).then_inc(T.root_done, 1)

        copy(A.xT[:], pp3(A), A.src_full, 0, A.src_evac)
        evac_k(A, 0)
        act.wait_ge(C.wts_in, 16 * 8)

        def end(T, b, s):
            if s == 2:
                evac_weighted(T, b, 1)
            if s == 7:
                copy(T.aT[:], pp3(T), T.aT_full, b, T.aT_evac)
            if s == 9:
                root(T, b)

        def iteration(i, odd):
            for s in range(H + LAG):
                if has(i, -1):
                    b = i - 1
                    if s == 0:
                        copy(C.cT[:], pp3(C), C.kv_full, b, C.kv_evac)
                    end(A, b, s)
                    if s == 3:
                        evac_k(C, b)
                    if s == 11:
                        copy(C.xT[:], pp3(C), C.src_full, b, C.src_evac)
                if has(i, 0) and s == 9:
                    evac_v(A, i)
                if has(i, -2) and s == LAG + WLAG + 8:
                    evac_weighted(C, i - 2, 0)
                if has(i, 0) and s == H + 1:
                    evac_max(A, i)
                if has(i, -2) and s >= LAG:
                    exponentials(C, i - 2, s - LAG)
            for s in range(H + LAG):
                if has(i, 1):
                    if s == 1:
                        copy(A.xT[:], pp3(A), A.src_full, i + 1, A.src_evac)
                    if s == 6:
                        evac_k(A, i + 1)
                if has(i, -2):
                    b = i - 2
                    end(C, b, s)
                    if s == 12:
                        wait(act, x2T_full, b + 1)
                        wait(act, logits_full, b)
                        act.copy(x2T[:], pp3(C)).then_inc(x2T_evac, 1)
                    if s == 14:
                        wait(act, logits_full, b + 1)
                        act.copy(lg[:, bass.ds(b * TT * E, TT * E)], C.pp[:, 0:TT * E]).then_inc(logits_evac, 1)
                if has(i, 0) and s == LAG + WLAG + 8:
                    evac_weighted(A, i, 0)
                if has(i, -1) and s == H + 1:
                    evac_max(C, i - 1)
                if has(i, 0) and s >= LAG:
                    exponentials(A, i, s - LAG)

        schedule(act, iteration)

    @block.vector
    def _(dve):
        g = Steps(dve, gate_chain, 2, 0)
        dve.wait_ge(gate_exp, 1)
        g.link(dve.tensor_scalar(gate[:], gate[:], 1.0, None, ALU.add))
        g.link(dve.reciprocal(gate[:], gate[:]))
        dve.tensor_scalar(gate[:], gate[:], HD ** -0.5, None, ALU.mult).then_inc(gate_ready, 1)
        dve.wait_ge(gate_ready, 1)
        dve.wait_ge(mrow_in, 16)
        m = Steps(dve, mask_chain, 5, 0)
        m.link(dve.tensor_scalar(mrow[:], mrow_i[:], 0.0, MASKED_SCORE, ALU.is_equal, ALU.mult))
        m.link(dve.tensor_copy(mparts[:, 0], mrow[:]))
        m.link(dve.tensor_tensor(mres[:], mrow[:], mparts[:, 0], ALU.subtract))
        m.link(dve.tensor_copy(mparts[:, 1], mres[:]))
        m.link(dve.tensor_tensor(mparts[:, 2], mres[:], mparts[:, 1], ALU.subtract))
        dve.drain().then_inc(dve_setup, 1)

        def evac_q(T, b):
            wait(dve, T.q_full, b + 1)
            wait(dve, T.q_split, b)
            if T.cross:
                for m in range(KT):
                    last = dve.tensor_scalar(T.qf[:, m], T.pp[:, m * S:(m + 1) * S], T.bq[:, m:m + 1],
                                             D ** -0.5, ALU.add, ALU.mult)
            else:
                last = dve.tensor_tensor(T.qf[:], T.pp[:].rearrange("p (k t) -> p k t", k=KT), gate[:], ALU.mult)
            last.then_inc(T.q_evac, 1)

        def split_k(T, b):
            wait(dve, T.k_evac, b + 1)
            wait(dve, T.k_written, 16 * b)
            c = Steps(dve, T.ksplit_chain, 4 if T.cross else 3, b)
            if T.cross:
                wait(dve, T.keep_done, b + 1)
                c.link(dve.tensor_tensor(T.kfm[:], T.kf[:], T.keep[:].unsqueeze(1).to_broadcast((P, KT, S)),
                                         ALU.mult))
            c.link(dve.tensor_copy(T.kp[:, 0], T.kfm[:]))
            c.link(dve.tensor_tensor(T.kr[:], T.kfm[:], T.kp[:, 0], ALU.subtract))
            c.link(dve.tensor_copy(T.kp[:, 1], T.kr[:]))
            c.done()
            dve.tensor_tensor(T.kp[:, 2], T.kr[:], T.kp[:, 1], ALU.subtract).then_inc(T.k_split, 1)

        def read_max(T, b, h):
            wait(dve, max_full, T.head(b, h) + 1)
            bank = pm[:, h % 2]
            if T.cross:
                last = dve.tensor_reduce(T.mx[:, :, h], bank.rearrange("p (t k) -> p t k", t=TT), X, ALU.max)
            else:
                dve.tensor_reduce(T.mx[:, 0, h:h + 1], bank[:, 0:P], X, ALU.max)
                last = dve.tensor_reduce(T.mx[:, 1, h:h + 1], bank[:, P:P + S], X, ALU.max)
            last.then_inc(max_read, 1)

        def split_max(T, b):
            wait(dve, max_read, T.through(b))
            wait(dve, T.nm_full, b)
            c = Steps(dve, T.nm_chain, 4, b)
            c.link(dve.tensor_scalar(T.nf[:], T.mx[:], -1.0, None, ALU.mult))
            c.link(dve.tensor_copy(T.np[:, :, 0], T.nf[:]))
            c.link(dve.tensor_tensor(T.nr[:], T.nf[:], T.np[:, :, 0], ALU.subtract))
            c.link(dve.tensor_copy(T.np[:, :, 1], T.nr[:]))
            c.done()
            dve.tensor_tensor(T.np[:, :, 2], T.nr[:], T.np[:, :, 1], ALU.subtract).then_inc(T.nm_split, 1)

        def normalise(T, b, half):
            wait(dve, T.weights_full, 2 * b + half + 1)
            wait(dve, T.aT_full, b)
            heads = T.pp[:].rearrange("p (t h c) -> p t h c", t=TT, h=H // 2)
            c = Steps(dve, T.norm_chain, 1, 2 * b + half)
            c.link(dve.reciprocal(T.rec[:], heads[:, :, :, HD]))
            c.done()
            dve.tensor_tensor(T.an[:, :, half * P:(half + 1) * P].rearrange("p t (h c) -> p t h c", c=HD),
                              heads[:, :, :, 0:HD], T.rec[:].unsqueeze(3).to_broadcast((P, TT, H // 2, HD)),
                              ALU.mult).then_inc(T.norm_done, 1)

        def split_q(b):
            wait(dve, C.q_evac, b + 1)
            wait(dve, C.q_written, 16 * b)
            c = Steps(dve, C.qsplit_chain, 3, b)
            c.link(dve.tensor_copy(C.qp[:, 0], C.qf[:]))
            c.link(dve.tensor_tensor(C.qr[:], C.qf[:], C.qp[:, 0], ALU.subtract))
            c.link(dve.tensor_copy(C.qp[:, 1], C.qr[:]))
            c.done()
            dve.tensor_tensor(C.qp[:, 2], C.qr[:], C.qp[:, 1], ALU.subtract).then_inc(C.q_split, 1)

        def evac_v(b):
            wait(dve, C.v_full, b + 1)
            for t in range(TT):
                last = dve.tensor_tensor(C.v[:, t, :, 0:HD],
                                         C.pp[:, t * D:(t + 1) * D].rearrange("p (h d) -> p h d", h=H),
                                         C.bv[:].rearrange("p (h d) -> p h d", h=H), ALU.add)
            last.then_inc(C.v_evac, 1)

        def residual(T, b):
            wait(dve, T.o_full, b + 1)
            wait(dve, T.res_copied, b + 1)
            wait(dve, T.ln_done, b)
            dve.tensor_tensor(T.r[:], T.pp[:].rearrange("p (t d) -> p t d", t=TT), T.res[:], ALU.add)\
               .then_inc(T.res_done, 1)
            wait(dve, T.res_done, b + 1)
            c = Steps(dve, T.ln_chain, 4, b)
            for t in range(TT):
                c.link(dve.bn_stats(T.st[:, t], T.r[:, t]), dve_tick)
            for t in range(TT):
                c.link(dve.bn_aggr(T.mv[:, t], T.st[:, t]), dve_tick)
            c.done()
            dve.tensor_scalar(T.ve[:], T.mv[:, :, 1], EPS, None, ALU.add).then_inc(T.stats_done, 1)

        def layernorm(T, b, readers):
            wait(dve, T.stats_done, b + 1)
            wait(dve, T.root_done, b + 1)
            c = Steps(dve, T.newton_chain, 2, b)
            c.link(dve.tensor_tensor(T.yy[:], T.y0[:], T.y0[:], ALU.mult))
            c.link(dve.scalar_tensor_tensor(T.yy[:], T.yy[:], -0.5, T.ve[:], ALU.mult, ALU.mult))
            c.done()
            dve.scalar_tensor_tensor(T.rstd[:], T.yy[:], 1.5, T.y0[:], ALU.add, ALU.mult).then_inc(T.rstd_done, 1)
            wait(dve, T.rstd_done, b + 1)
            for sem_, count in readers:
                wait(dve, sem_, count)
            for t in range(TT):
                last = dve.tensor_scalar(T.out[:, t], T.r[:, t], T.mv[:, t, 0:1], T.rstd[:, t:t + 1],
                                         ALU.subtract, ALU.mult)
            last.then_inc(T.ln_done, 1)

        evac_q(A, 0)
        split_k(A, 0)
        dve.wait_ge(C.wts_in, 16 * 8)

        def end(T, b, s, readers):
            if s == 3:
                normalise(T, b, 0)
            if s == 4:
                normalise(T, b, 1)
            if s == 7:
                residual(T, b)
            if s == 9:
                layernorm(T, b, readers)

        def iteration(i, odd):
            for s in range(H + LAG):
                if has(i, 0) and s < H:
                    read_max(A, i, s)
                if has(i, 0) and s == H - 1:
                    split_max(A, i)
                if has(i, -1):
                    b = i - 1
                    end(A, b, s, ((C.res_copied, i - 1), (C.src_full, i - 1)))
                    if s == 2:
                        wait(dve, C.keep_in, 16 * (b + 1))
                        wait(dve, C.k_split, b)
                        dve.tensor_scalar(C.keep[:], C.keep_i[:], 0.0, None, ALU.not_equal).then_inc(C.keep_done, 1)
                    if s == 5:
                        split_k(C, b)
                    if s == 12:
                        evac_q(C, b)
                        split_q(b)
            for s in range(H + LAG):
                if has(i, -1) and s < H:
                    read_max(C, i - 1, s)
                if has(i, -1) and s == H - 1:
                    split_max(C, i - 1)
                if has(i, -2):
                    end(C, i - 2, s, ((x2_written, 16 * (i - 2)), (x2T_full, i - 2)))
                if has(i, -1) and s == 8:
                    evac_v(i - 1)
                if has(i, 1):
                    if s == 2:
                        evac_q(A, i + 1)
                    if s == 6:
                        split_k(A, i + 1)

        schedule(dve, iteration)

def experts(nc, ctx, x2, lg, xs_d, w_1, w_2, out):
    def sb(n, shape, dt):
        return ctx.enter_context(nc.sbuf_tensor(n, shape, dt))

    def sem(n):
        return ctx.enter_context(nc.semaphore(n))

    XT = TILE // P
    GROUP = 4
    identf = sb("ident2", [P, P], F32)
    upper = sb("upper", [P, P], BF16)
    all_ones = sb("all_ones", [P, P], BF16)
    below = sb("below", [P, E, E], F32)
    rows_i = sb("rows_i", [P, B * S // TILE], I32)
    rows = sb("rows", [P, B * S // TILE], F32)
    tile_no_i = sb("tile_no_i", [P, NTILE], I32)
    tile_no = sb("tile_no", [P, NTILE], F32)
    mx = sb("rmx", [P, NT], F32)
    lgs = sb("lgs", [P, NT, E], F32)
    g = sb("g", [P, NT, E], F32)
    gs = sb("gs", [P, NT], F32)
    gt = sb("gt", [P, NT, E, E], F32)
    eq = sb("eq", [P, NT, E, E], F32)
    rank = sb("rank", [P, NT, E], F32)
    chosen = sb("chosen", [P, NT, E], BF16)
    pick = sb("pick", [P, TOP, NT, E], F32)
    pw = sb("pw", [P, TOP, NT, E], F32)
    wk = sb("wk", [P, TOP, NT], F32)
    more = sb("more", [P, E, B * S // TILE], F32)
    tiles = sb("tiles", [P, E], F32)
    before = sb("before", [P, E, E], F32)
    first = sb("first", [P, E], F32)
    behind = sb("behind", [P, E], F32)
    passed = sb("passed", [P, NTILE, E], F32)
    owner_f = sb("owner_f", [P, NTILE], F32)
    owner = sb("owner", [P, NTILE], I32)
    place = sb("place", [P, NT, E], F32)
    slot_f = sb("slot_f", [P, TOP, NT], F32)
    slot = sb("slot", [P, TOP, NT], I32)
    w1 = sb("w1", [P, 2, KT, F], F32)
    w2 = sb("w2", [P, 2, FT, D], F32)
    xin = sb("xin", [P, 2, XT, D], F32)
    xT = sb("xTt", [P, 2, KT, TILE], F32)
    hid = sb("hid", [P, 2, FT, TILE], F32)
    yt = sb("yt", [P, 2, XT, D], F32)
    yg = sb("yg", [P, NT, TOP, D], F32)
    y = sb("y", [P, NT, D], F32)
    st = sb("fst", [P, NT, 6], F32)
    mv = sb("fmv", [P, NT, 2], F32)
    ve = sb("fve", [P, NT], F32)
    lnv = sb("flnv", [P, NT], F32)
    y0 = sb("fy0", [P, NT], F32)
    yy = sb("fyy", [P, NT], F32)
    rstd = sb("frstd", [P, NT], F32)
    ph = ctx.enter_context(nc.psum_tensor("ph", [P, 4, 512], F32))
    py = ctx.enter_context(nc.psum_tensor("py", [P, 2, 512], F32))
    pt = ctx.enter_context(nc.psum_tensor("pt", [P, 512], F32))
    pr = ctx.enter_context(nc.psum_tensor("pr", [P, 512], F32))
    ys_d = nc.dram_tensor("sorted_y", (NTILE * TILE, D), F32, kind="Internal").ap()

    tables = sem("tables")
    tables_ready = sem("tables_ready")
    router = sem("router")
    shifted = sem("shifted")
    exp_done = sem("gate_exp_done")
    chosen_ready = sem("chosen_ready")
    places_full = sem("places_full")
    owner_ready = sem("owner_ready")
    slot_ready = sem("slot_ready")
    scattered = sem("scattered")
    w1_in = [sem("w1_in0"), sem("w1_in1")]
    w2_in = [sem("w2_in0"), sem("w2_in1")]
    x_in = [sem("x_in0"), sem("x_in1")]
    t_done = sem("t_done")
    xT_evac = sem("xT_evac")
    h_full = sem("h_full")
    relu_done = sem("relu_done")
    m2_done = sem("m2_done")
    y_evac = sem("y_evac")
    y_stored = [sem("y_stored0"), sem("y_stored1")]
    gathered = [sem(f"gathered{s}") for s in range(NT // GROUP)]
    fin = sem("fin")
    stats = sem("fstats")
    lns = sem("flns")
    root = sem("froot")
    outs = sem("outs")
    stored = sem("stored")
    sp_tick, act_tick = sem("sp_tick2"), sem("act_tick2")
    block = ctx.enter_context(nc.Block())

    PEEL = 4

    def schedule(eng, step):
        for j in range(PEEL):
            step(j, j % 2, j // 2)
        with eng.Fori(PEEL // 2, NTILE // 2) as i:
            for u in range(2):
                step(2 * i + u, u, i)
        for j in range(NTILE // 2 * 2, NTILE):
            step(j, j % 2, j // 2)

    def tile_rows(dram, j):
        return dram[bass.ds(j * TILE, TILE)].rearrange("(t p) d -> p t d", p=P)

    @block.sync
    def _(sp):
        def load_w1(j, u, expert):
            if not (isinstance(j, int) and j < 2):
                fence(sp, h_full, 4 * (j - 1), sp_tick)
            sp.dma_start(w1[:, u], w_1[bass.ds(expert, 1)].rearrange("o (k p) f -> p (o k) f", p=P))\
              .then_inc(w1_in[u], 16)

        def load_w2(j, u, expert):
            if not (isinstance(j, int) and j < 2):
                fence(sp, m2_done, j - 1, sp_tick)
            sp.dma_start(w2[:, u], w_2[bass.ds(expert, 1)].rearrange("o (k p) n -> p (o k) n", p=P))\
              .then_inc(w2_in[u], 16)

        def load_x(j, u):
            if not (isinstance(j, int) and j < 2):
                fence(sp, t_done, j - 1, sp_tick)
            sp.dma_start(xin[:, u], tile_rows(xs_d, j)).then_inc(x_in[u], 16)

        sp.wait_ge(owner_ready, 1)

        def step(j, u, i):
            expert = sp.value_load(owner[0:1, bass.ds(j, 1)], min_val=0, max_val=E - 1)
            load_w1(j, u, expert)
            if isinstance(j, int) and j < 2:
                load_w2(j, u, expert)
                if j == 1:
                    sp.wait_ge(scattered, 16 * TOP * NT)
                    load_x(0, 0)
                    load_x(1, 1)
                    load_x(2, 0)
            else:
                if not (isinstance(j, int) and j == NTILE - 1):
                    load_x(j + 1, 1 - u)
                load_w2(j, u, expert)

        schedule(sp, step)
        for s in range(NT // GROUP):
            sp.wait_ge(outs, s + 1)
            sp.dma_start(out.rearrange("b (t p) d -> p (b t) d", p=P)[:, s * GROUP:(s + 1) * GROUP],
                         y[:, s * GROUP:(s + 1) * GROUP]).then_inc(stored, 16)
        sp.wait_ge(stored, 16 * NT // GROUP)

    @block.gpsimd
    def _(pool):
        c = Steps(pool, tables, 100, 0)
        c.link(pool.memset(below[:], 1.0))
        c.link(pool.affine_select(out=below[:], in_=below[:], compare_op=ALU.is_gt, fill=0.0, base=0,
                                  pattern=[[1, E], [-1, E]], channel_multiplier=0))
        c.link(pool.memset(all_ones[:], 1.0))
        c.link(pool.affine_select(out=upper[:], in_=all_ones[:], compare_op=ALU.is_gt, fill=0.0, base=0,
                                  pattern=[[1, P]], channel_multiplier=-1))
        c.link(pool.iota(rows_i[:], pattern=[[TILE, B * S // TILE]], base=0, channel_multiplier=0))
        c.link(pool.tensor_copy(rows[:], rows_i[:]))
        c.link(pool.iota(tile_no_i[:], pattern=[[1, NTILE]], base=0, channel_multiplier=0))
        c.link(pool.tensor_copy(tile_no[:], tile_no_i[:]))
        c.link(pool.memset(identf[:], 0.0))
        c.link(pool.affine_select(out=identf[:], in_=identf[:], compare_op=ALU.not_equal, fill=1.0, base=0,
                                  pattern=[[-1, P]], channel_multiplier=1))
        pool.drain().then_inc(tables_ready, 1)
        pool.wait_ge(slot_ready, 1)
        for t in range(NT):
            for k in range(TOP):
                pool.indirect_dma_start(xs_d, bass.IndirectOffsetOnAxis(ap=slot[:, k, t:t + 1], axis=0),
                                        x2[:, t], None).then_inc(scattered, 16)
        for u in range(2):
            pool.wait_ge(y_stored[u], 16 * ((NTILE + 1 - u) // 2))
        for t in range(NT):
            for k in range(TOP):
                pool.indirect_dma_start(yg[:, t, k], None, ys_d,
                                        bass.IndirectOffsetOnAxis(ap=slot[:, k, t:t + 1], axis=0))\
                    .then_inc(gathered[t // GROUP], 16)

    @block.tensor
    def _(pe):
        pe.wait_ge(tables_ready, 1)
        pe.wait_ge(chosen_ready, 1)
        pe.matmul(pr[:, 0:NT * E], upper[:], chosen[:].rearrange("p t e -> p (t e)"), start=True, stop=False)
        for t in range(NT - 1):
            n = NT - 1 - t
            pe.matmul(pr[:, (t + 1) * E:NT * E].rearrange("p (t e) -> p t e", e=E), all_ones[:],
                      chosen[:, t:t + 1, :].to_broadcast((P, n, E)), start=False, stop=(n == 1))
        for t in range(NT):
            last = pe.matmul(pr[:, NT * E:(NT + 1) * E], all_ones[:], chosen[:, t], start=(t == 0), stop=(t == NT - 1))
        last.then_inc(places_full, 1)

        def transpose(j, u, i):
            pe.wait_ge(x_in[u], 16 * (i + 1))
            wait(pe, xT_evac, j)
            for k in range(KT):
                for t in range(XT):
                    o = (k * XT + t) * P
                    last = pe.transpose(pt[:, o:o + P], xin[:, u, t, k * P:(k + 1) * P], identf[:])
            last.then_inc(t_done, 1)

        def hidden(j, u, i):
            wait(pe, xT_evac, j + 1)
            pe.wait_ge(w1_in[u], 16 * (i + 1))
            for f in range(FT):
                if f % 2 == 0:
                    wait(pe, relu_done, 4 * j + f // 2 - 3)
                o = ph[:, f // 2, f % 2 * TILE:(f % 2 + 1) * TILE]
                for k in range(KT):
                    last = pe.matmul(o, w1[:, u, k, f * P:(f + 1) * P], xT[:, u, k], start=(k == 0), stop=(k == KT - 1))
                if f % 2 == 1:
                    last.then_inc(h_full, 1)

        def output(j, u, i):
            pe.wait_ge(w2_in[u], 16 * (i + 1))
            wait(pe, relu_done, 4 * (j + 1))
            wait(pe, y_evac, j - 1)
            for t in range(XT):
                for f in range(FT):
                    last = pe.matmul(py[:, u, t * D:(t + 1) * D], hid[:, u, f, t * P:(t + 1) * P], w2[:, u, f],
                                     start=(f == 0), stop=(f == FT - 1))
            last.then_inc(m2_done, 1)

        transpose(0, 0, 0)

        def step(j, u, i):
            if not (isinstance(j, int) and j == NTILE - 1):
                transpose(j + 1, 1 - u, i + u)
            hidden(j, u, i)
            if not (isinstance(j, int) and j == 0):
                output(j - 1, 1 - u, i - 1 + u)

        schedule(pe, step)
        output(NTILE - 1, (NTILE - 1) % 2, (NTILE - 1) // 2)

    @block.scalar
    def _(act):
        act.wait_ge(shifted, 1)
        act.activation(g[:], lgs[:], ACT.Exp).then_inc(exp_done, 1)

        def store(j, u, i):
            fence(act, y_evac, j + 1, act_tick)
            act.dma_start(tile_rows(ys_d, j), yt[:, u]).then_inc(y_stored[u], 16)

        def step(j, u, i):
            for f in range(FT // 2):
                wait(act, h_full, 4 * j + f + 1)
                if f == 0:
                    wait(act, m2_done, j - 1)
                act.activation(hid[:, u, 2 * f:2 * f + 2], ph[:, f].rearrange("p (f t) -> p f t", f=2), ACT.Relu)\
                   .then_inc(relu_done, 1)
            if not (isinstance(j, int) and j < 2):
                store(j - 2, u, i - 1)

        schedule(act, step)
        for j in range(NTILE - 2, NTILE):
            store(j, j % 2, j // 2)
        for s in range(NT // GROUP):
            sl = slice(s * GROUP, (s + 1) * GROUP)
            act.wait_ge(stats, s + 1)
            act.activation(lnv[:, sl], ve[:, sl], ACT.Ln).then_inc(lns, 1)
            act.wait_ge(lns, s + 1)
            act.activation(y0[:, sl], lnv[:, sl], ACT.Exp, scale=-0.5).then_inc(root, 1)

    @block.vector
    def _(dve):
        c = Steps(dve, router, 100, 0)
        l3 = lg[:].rearrange("p (t e) -> p t e", e=E)
        c.link(dve.tensor_reduce(mx[:], l3, X, ALU.max))
        dve.tensor_tensor(lgs[:], l3, mx[:].unsqueeze(2).to_broadcast((P, NT, E)), ALU.subtract).then_inc(shifted, 1)
        dve.wait_ge(exp_done, 1)
        c.link(dve.tensor_reduce(gs[:], g[:], X, ALU.add))
        c.link(dve.reciprocal(gs[:], gs[:]))
        c.link(dve.tensor_tensor(g[:], g[:], gs[:].unsqueeze(2).to_broadcast((P, NT, E)), ALU.mult))
        own = g[:].unsqueeze(3).to_broadcast((P, NT, E, E))
        other = g[:].unsqueeze(2).to_broadcast((P, NT, E, E))
        dve.wait_ge(tables_ready, 1)
        dve.tensor_tensor(gt[:], other, own, ALU.is_gt)
        c.link(dve.tensor_tensor(eq[:], other, own, ALU.is_equal))
        c.link(dve.tensor_tensor(eq[:], eq[:], below[:].unsqueeze(1).to_broadcast((P, NT, E, E)), ALU.mult))
        c.link(dve.tensor_tensor(gt[:], gt[:], eq[:], ALU.add))
        c.link(dve.tensor_reduce(rank[:], gt[:], X, ALU.add))
        dve.tensor_scalar(chosen[:], rank[:], float(TOP), None, ALU.is_lt).then_inc(chosen_ready, 1)
        for k in range(TOP):
            c.link(dve.tensor_scalar(pick[:, k], rank[:], float(k), None, ALU.is_equal))
        dve.wait_ge(places_full, 1)
        count = pr[:, NT * E:(NT + 1) * E]
        c.link(dve.tensor_tensor(more[:], count.unsqueeze(2).to_broadcast((P, E, B * S // TILE)),
                                 rows[:].unsqueeze(1).to_broadcast((P, E, B * S // TILE)), ALU.is_gt))
        c.link(dve.tensor_reduce(tiles[:], more[:], X, ALU.add))
        c.link(dve.tensor_tensor(before[:], tiles[:].unsqueeze(1).to_broadcast((P, E, E)), below[:], ALU.mult))
        c.link(dve.tensor_reduce(first[:], before[:], X, ALU.add))
        c.link(dve.scalar_tensor_tensor(place[:], first[:].unsqueeze(1).to_broadcast((P, NT, E)), float(TILE),
                                        pr[:, 0:NT * E].rearrange("p (t e) -> p t e", e=E), ALU.mult, ALU.add))
        c.link(dve.tensor_tensor(pw[:], pick[:], place[:].unsqueeze(1).to_broadcast((P, TOP, NT, E)), ALU.mult))
        c.link(dve.tensor_reduce(slot_f[:], pw[:], X, ALU.add))
        dve.tensor_copy(slot[:], slot_f[:]).then_inc(slot_ready, 1)
        c.link(dve.tensor_tensor(behind[:], first[:], tiles[:], ALU.add))
        c.link(dve.tensor_tensor(passed[:], behind[:].unsqueeze(1).to_broadcast((P, NTILE, E)),
                                 tile_no[:].unsqueeze(2).to_broadcast((P, NTILE, E)), ALU.is_le))
        c.link(dve.tensor_reduce(owner_f[:], passed[:], X, ALU.add))
        dve.tensor_scalar(owner[:], owner_f[:], float(E - 1), None, ALU.min).then_inc(owner_ready, 1)
        c.link(dve.tensor_tensor(pw[:], pick[:], g[:].unsqueeze(1).to_broadcast((P, TOP, NT, E)), ALU.mult))
        c.link(dve.tensor_reduce(wk[:], pw[:], X, ALU.add))
        c.link(dve.tensor_tensor(gs[:], wk[:, 0], wk[:, 1], ALU.add))
        c.link(dve.reciprocal(gs[:], gs[:]))
        c.link(dve.tensor_tensor(wk[:], wk[:], gs[:].unsqueeze(1).to_broadcast((P, TOP, NT)), ALU.mult))

        def evac_x(j, u):
            dve.wait_ge(t_done, j + 1)
            wait(dve, h_full, 4 * (j - 1))
            dve.tensor_copy(xT[:, u], pt[:].rearrange("p (k t) -> p k t", k=KT)).then_inc(xT_evac, 1)

        def evac_y(j, u, i):
            dve.wait_ge(m2_done, j + 1)
            wait(dve, y_stored[u], 16 * i)
            dve.tensor_copy(yt[:, u], py[:, u].rearrange("p (t d) -> p t d", t=XT)).then_inc(y_evac, 1)

        evac_x(0, 0)

        def step(j, u, i):
            if not (isinstance(j, int) and j == NTILE - 1):
                evac_x(j + 1, 1 - u)
            if not (isinstance(j, int) and j == 0):
                evac_y(j - 1, 1 - u, i - 1 + u)

        schedule(dve, step)
        evac_y(NTILE - 1, (NTILE - 1) % 2, (NTILE - 1) // 2)

        c = Steps(dve, fin, 200, 0)
        for s in range(NT // GROUP):
            sl = slice(s * GROUP, (s + 1) * GROUP)
            dve.wait_ge(gathered[s], 16 * TOP * GROUP)
            for k in range(TOP):
                for t in range(s * GROUP, (s + 1) * GROUP):
                    c.n += 1
                    dve.scalar_tensor_tensor(y[:, t], yg[:, t, k], wk[:, k, t:t + 1], (x2, y)[k][:, t],
                                             ALU.mult, ALU.add).then_inc(fin, 1)
                dve.wait_ge(fin, c.n)
            for t in range(s * GROUP, (s + 1) * GROUP):
                c.n += 1
                dve.bn_stats(st[:, t], y[:, t]).then_inc(fin, 1)
            dve.wait_ge(fin, c.n)
            for t in range(s * GROUP, (s + 1) * GROUP):
                c.n += 1
                dve.bn_aggr(mv[:, t], st[:, t]).then_inc(fin, 1)
            dve.wait_ge(fin, c.n)
            dve.tensor_scalar(ve[:, sl], mv[:, sl, 1], EPS, None, ALU.add).then_inc(stats, 1)
            dve.wait_ge(root, s + 1)
            dve.wait_ge(stats, s + 1)
            c.link(dve.tensor_tensor(yy[:, sl], y0[:, sl], y0[:, sl], ALU.mult))
            c.link(dve.scalar_tensor_tensor(yy[:, sl], yy[:, sl], -0.5, ve[:, sl], ALU.mult, ALU.mult))
            c.link(dve.scalar_tensor_tensor(rstd[:, sl], yy[:, sl], 1.5, y0[:, sl], ALU.add, ALU.mult))
            for t in range(s * GROUP, (s + 1) * GROUP):
                last = dve.tensor_scalar(y[:, t], y[:, t], mv[:, t, 0:1], rstd[:, t:t + 1], ALU.subtract, ALU.mult)
            last.then_inc(outs, 1)


def kernel(**inputs):
    import numpy as np
    import concourse.bacc as bacc
    from concourse.bass_utils import run_bass_kernel_spmd

    cycles = np.array([5 + h % 4 for h in range(H)])
    phases = np.arange(S)[None, :] % cycles[:, None]
    raw = np.asarray(inputs["L0_attn_bandha_gate"])
    gate_rows = np.repeat(np.take_along_axis(raw, phases, axis=1), HD, axis=0)
    arrays = {
        "x": inputs["x"], "ctx_in": inputs["ctx_1024"],
        "mask": np.asarray(inputs["mask_Bx1x1xS2_ik0"]).reshape(B, S),
        "w_qkv": inputs["L0_attn_w_qkv"], "w_o1": inputs["L0_attn_w_out"], "gate_raw": gate_rows,
        "wqT": np.asarray(inputs["L0_xattn_Wq"]).T, "bq": np.asarray(inputs["L0_xattn_bq"]).reshape(KT, P).T,
        "wkT": np.asarray(inputs["L0_xattn_Wk"]).T, "bk": np.asarray(inputs["L0_xattn_bk"]).reshape(KT, P).T,
        "wvT": np.asarray(inputs["L0_xattn_Wv"]).T, "bv": inputs["L0_xattn_bv"],
        "woT": np.asarray(inputs["L0_xattn_Wo"]).T, "bo": inputs["L0_xattn_bo"],
        "w_r": inputs["L0_ffn_Wr"], "w_1": inputs["L0_ffn_W1"], "w_2": inputs["L0_ffn_W2"],
    }
    nc = bacc.Bacc("TRN2", target_bir_lowering=False, num_devices=1)
    arrays = {n: np.ascontiguousarray(a) for n, a in arrays.items()}
    args = [nc.dram_tensor(n, a.shape, mybir.dt.from_np(a.dtype), kind="ExternalInput").ap()
            for n, a in arrays.items()]
    args.append(nc.dram_tensor("out", (B, S, D), F32, kind="ExternalOutput").ap())
    decoder_layer(nc, *args)
    r = run_bass_kernel_spmd(nc, [arrays], core_ids=[0])
    return r.results[0]["out"]
```

```python
from contextlib import ExitStack

import concourse.bass as bass
from concourse import mybir

F32 = mybir.dt.float32
BF16 = mybir.dt.bfloat16
F16 = mybir.dt.float16
I32 = mybir.dt.int32
ALU = mybir.AluOpType
ACT = mybir.ActivationFunctionType
X = mybir.AxisListType.X
PMAX = bass.bass_isa.ReduceOp.max

P = 128
B, S, D = 8, 256, 256
H, HD = 16, 16
KT = D // P
TT = S // P
E, F = 8, 1024
FT = F // P
EPS = 1e-5
CAUSAL_FILL = -1e30
MASKED_SCORE = -1e9
TOP = 2
NT = B * TT
TILE = 256
NTILE = (B * S * TOP + E * (TILE - 1)) // TILE
ROOM = B * S + TILE

Q_PARTS = (0, 0, 0, 1, 1, 2)
K_PARTS = (0, 1, 2, 0, 1, 0)
assert len(K_PARTS) == len(Q_PARTS)
STACK = HD * len(Q_PARTS)
Q_RUNS = ((0, 0, 1, 3), (3, 1, 1, 2), (5, 2, 1, 1))
K_RUNS = ((0, 0, 3, 1), (3, 0, 2, 1), (5, 0, 1, 1))
PRODUCTS = ((0, 1), (1, 0), (0, 0))
X_SCALE = 8.0
W_SCALE = 8.0
LEAST = 2.0 ** -100
EXPONENT = 0x7F800000
TWO_ONES = 1.0 + 0x3F80 / 2 ** 23
MASK_ROWS = 3
MAX_ROWS = 3
LAG = 5
WLAG = 2
WEIGHTED = (3, 2)
OUT_T = (5, 5)
OUT = (7, 7)
NORM = (9, 10)
VALUES = (9, 9)
C_KEYS = 1
C_KEYS_SPLIT = 5
C_TOKENS_T = 11
C_QUERIES = 12
A_QUERIES = 2
A_KEYS = 4
X2_T = 12
LOGITS = 13
RANKS = 17


def wait(eng, sem, value):
    if isinstance(value, int) and value <= 0:
        return
    eng.wait_ge(sem, value)


def fence(eng, sem, value, tick):
    wait(eng, sem, value)
    if not isinstance(value, int):
        eng.sem_inc(tick)


class Steps:

    def __init__(self, eng, sem, per_batch, batch):
        self.eng, self.sem, self.count, self.end = eng, sem, batch * per_batch, per_batch
        self.n = 0

    def link(self, instruction, tick=None):
        self.n += 1
        assert self.n <= self.end
        instruction.then_inc(self.sem, 1)
        if tick is None:
            wait(self.eng, self.sem, self.count + self.n)
        else:
            fence(self.eng, self.sem, self.count + self.n, tick)

    def done(self):
        assert self.n == self.end


class Router:

    def __init__(self, nc, ctx):
        def sb(n, shape, dt):
            return ctx.enter_context(nc.sbuf_tensor(n, shape, dt))

        self.sp_tick = ctx.enter_context(nc.semaphore("sp_tick"))
        self.pool_tick = ctx.enter_context(nc.semaphore("pool_tick"))
        self.act_tick = ctx.enter_context(nc.semaphore("act_tick"))
        self.x2 = sb("x2", [P, NT, D], F32)
        self.pick = sb("pick", [P, TOP, NT, E], F32)
        self.wk = sb("wk", [P, TOP, NT], F32)
        self.place = sb("place", [P, NT, E], F32)
        self.run = sb("run", [P, E], F32)
        self.zeros = sb("zeros", [P, D], F32)
        self.unscale = sb("unscale", [P, E, 2], F32)
        self.parts_d = nc.dram_tensor("expert_parts", (E, 2, P, 2, KT * F), F16, kind="Internal").ap()
        self.below = sb("below", [P, E, E], F32)
        self.rows = sb("rows", [P, B * S // TILE], F32)
        self.tile_no = sb("tile_no", [P, NTILE], F32)
        self.tiles = sb("tiles", [P, E], F32)
        self.first = sb("first", [P, E], F32)
        self.behind = sb("behind", [P, E], F32)
        self.rest = sb("rest", [P, E], I32)
        self.owner = sb("owner", [P, NTILE], I32)
        self.source = sb("source", [P, NTILE], I32)
        self.room_i = sb("room_i", [P, E], I32)
        self.room = sb("room", [P, E], F32)
        self.ys_d = nc.dram_tensor("sorted_y", (NTILE * TILE, D), F32, kind="Internal").ap()
        self.xs_d = nc.dram_tensor("sorted_x", (E * ROOM + TILE, D), F32, kind="Internal").ap()


class Stream:

    def __init__(self, nc, ctx, name, cross):
        def sb(n, shape, dt):
            return ctx.enter_context(nc.sbuf_tensor(f"{name}_{n}", shape, dt))

        self.name, self.cross = name, cross
        def sem(n):
            return ctx.enter_context(nc.semaphore(f"{name}_{n}"))

        self.src_in = sem("src_in")
        self.src_evac = sem("src_evac")
        self.src_full = sem("src_full")
        self.q_full = sem("q_full")
        self.q_evac = sem("q_evac")
        self.k_full = sem("k_full")
        self.k_evac = sem("k_evac")
        self.q_split = sem("q_split")
        self.k_split = sem("k_split")
        self.q_written = sem("q_written")
        self.k_written = sem("k_written")
        self.q_stacked = sem("q_stacked")
        self.k_stacked = sem("k_stacked")
        self.v_full = sem("v_full")
        self.v_evac = sem("v_evac")
        self.nm_split = sem("nm_split")
        self.nm_full = sem("nm_full")
        self.nm_evac = sem("nm_evac")
        self.m_written = sem("m_written")
        self.m_stacked = sem("m_stacked")
        self.weights_full = sem("weights_full")
        self.aT_full = sem("aT_full")
        self.aT_evac = sem("aT_evac")
        self.norm_done = sem("norm_done")
        self.o_full = sem("o_full")
        self.res_done = sem("res_done")
        self.res_copied = sem("res_copied")
        self.stats_done = sem("stats_done")
        self.rstd_done = sem("rstd_done")
        self.ln_taken = sem("ln_taken")
        self.root_done = sem("root_done")
        self.ln_done = sem("ln_done")
        self.qsplit_chain = sem("qsplit_chain")
        self.ksplit_chain = sem("ksplit_chain")
        self.nm_chain = sem("nm_chain")
        self.norm_chain = sem("norm_chain")
        self.ln_chain = sem("ln_chain")
        self.wts_in = sem("wts_in")
        self.wq_in = self.wts_in if cross else sem("wq_in")
        self.wk_in = self.wts_in if cross else sem("wk_in")
        self.wq = sb("wq", [P, KT, D], F32)
        self.wk = sb("wk", [P, KT, D], F32)
        self.wv = sb("wv", [P, KT, D], F32)
        self.wo = sb("wo", [P, KT, D], F32)
        self.src = sb("src", [P, TT, D], F32)
        self.xT = sb("xT", [P, KT, S], F32)
        self.cT = sb("cT", [P, KT, S], F32) if cross else self.xT
        self.res = sb("res", [P, TT, D], F32)
        self.qf = sb("qf", [P, KT, S], F32)
        self.kf = sb("kf", [P, KT, S], F32)
        self.qp = sb("qp", [P, 3, KT, S], BF16)
        self.kp = sb("kp", [P, 3, KT, S], BF16)
        self.qs = sb("qs", [P, 2, H, S], BF16)
        self.ks = sb("ks", [P, 2, H, S], BF16)
        self.v = sb("v", [P, TT, H, 32], F32)
        self.mx = sb("mx", [P, TT if cross else TT + 1, H], F32)
        self.nf = sb("nf", [P, TT, H], F32)
        self.nr = sb("nr", [P, TT, H], F32)
        self.np = sb("np", [P, TT, 3, H], BF16)
        self.npT = sb("npT", [3 * H, S], BF16)
        self.pvs = sb("pvs", [P, 4, S], F32)
        self.rec = sb("rec", [P, TT, H // 2], F32)
        self.an = sb("an", [P, TT, D], F32)
        self.aT = self.xT if cross else sb("aT", [P, KT, S], F32)
        self.r = self.an
        self.st = sb("st", [P, TT, 6], F32)
        self.mv = sb("mv", [P, TT, 2], F32)
        self.ve = sb("ve", [P, TT], F32)
        self.lnv = sb("lnv", [P, TT], F32)
        self.y0 = sb("y0", [P, TT], F32)
        self.yy = sb("yy", [P, TT], F32)
        self.rstd = sb("rstd", [P, TT], F32)
        self.out = sb("out", [P, TT, D], F32)
        if cross:
            self.kv_full = sem("kv_full")
            self.kv_evac = sem("kv_evac")
            self.keep_in = sem("keep_in")
            self.keep_done = sem("keep_done")
            self.bq = sb("bq", [P, KT], F32)
            self.bk = sb("bk", [P, KT], F32)
            self.bv = sb("bv", [P, D], F32)
            self.bo = sb("bo", [P, D], F32)
            self.keep_i = sb("keep_i", [P, S], I32)
            self.keep = sb("keep", [P, S], F32)
        self.mask_rows = MASK_ROWS if cross else 0
        self.max_k = STACK + self.mask_rows
        self.st_k = self.max_k + MAX_ROWS
        self.parts_d = nc.dram_tensor(f"{name}_parts", (2, 3, HD, H * S), BF16, kind="Internal").ap()
        self.m_d = nc.dram_tensor(f"{name}_m", (3, H, S), BF16, kind="Internal").ap()
        self.pp = ctx.enter_context(nc.psum_tensor(f"{name}_pp", [P, 512], F32))

    def order(self, b):
        if isinstance(b, int):
            return max(0, 2 * b - 1) if not self.cross else min(2 * b + 2, B + b)
        return 2 * b + 2 if self.cross else 2 * b - 1

    def head(self, b, h):
        return H * self.order(b) + h

    def through(self, b):
        return 0 if isinstance(b, int) and b < 0 else H * (self.order(b) + 1)


def decoder_layer(nc, x, ctx_in, mask, w_q1, w_k1, w_v1, w_o1, gate_raw, wqT, bq, wkT, bk, wvT, bv, woT, bo,
                  w_r, w_1, w_2, out):
    with ExitStack() as outer:
        R = Router(nc, outer)
        with ExitStack() as ctx:
            attention(nc, ctx, R, x, ctx_in, mask, w_q1, w_k1, w_v1, w_o1, gate_raw, wqT, bq, wkT, bk, wvT, bv,
                      woT, bo, w_r, w_1, w_2)
        with ExitStack() as ctx:
            experts(nc, ctx, R, out)


def attention(nc, ctx, R, x, ctx_in, mask, w_q1, w_k1, w_v1, w_o1, gate_raw, wqT, bq, wkT, bk, wvT, bv,
              woT, bo, w_r, w_1, w_2):
    def sb(n, shape, dt):
        return ctx.enter_context(nc.sbuf_tensor(n, shape, dt))

    def sem(n):
        return ctx.enter_context(nc.semaphore(n))

    A = Stream(nc, ctx, "self", False)
    C = Stream(nc, ctx, "cross", True)
    identf = sb("identf", [P, P], F32)
    identb = sb("identb", [P, P], BF16)
    tri_qk = sb("tri_qk", [P, P], BF16)
    tri_kq = sb("tri_kq", [P, P], BF16)
    gate = sb("gate", [P, KT, S], F32)
    more = sb("more", [P, E, B * S // TILE], F32)
    before = sb("before", [P, E, E], F32)
    passed = sb("passed", [P, NTILE, E], F32)
    skipped = sb("skipped", [P, NTILE, E], F32)
    owner_f = sb("owner_f", [P, NTILE], F32)
    start = sb("start", [P, NTILE], F32)
    some = sb("some", [P, NTILE], F32)
    source_f = sb("source_f", [P, NTILE], F32)
    rows_i = sb("rows_i", [P, B * S // TILE], I32)
    tile_no_i = sb("tile_no_i", [P, NTILE], I32)
    stage = sb("stage", [P, KT * F], F32)
    parts = sb("parts", [P, 2, KT * F], F16)
    largest = sb("largest", [P, 1], F32)
    largest_all = sb("largest_all", [P, 1], F32)
    power = sb("power", [P, 1], F32)
    scale = sb("scale", [P, 1], F32)
    x2, zeros, below = R.x2, R.zeros, R.below
    upper = sb("upper", [P, P], BF16)
    all_ones = sb("all_ones", [P, P], BF16)
    lgm = sb("lgm", [P, TT], F32)
    lgs = sb("lgs", [P, TT, E], F32)
    g = sb("g", [P, TT, E], F32)
    gs = sb("gs", [P, TT], F32)
    gt = sb("gt", [P, TT, E, E], F32)
    eq = sb("eq", [P, TT, E, E], F32)
    rank = sb("rank", [P, TT, E], F32)
    chosen = sb("chosen", [P, TT, E], BF16)
    at = sb("at", [P, TT, E], F32)
    pw = sb("pw", [P, TOP, TT, E], F32)
    slot_f = sb("slot_f", [P, TOP, TT], F32)
    slot = sb("slot", [P, TOP, TT], I32)
    wr = sb("wr", [P, KT, E], F32)
    x2T = sb("x2T", [P, KT, S], F32)
    p = sb("p", [P, 4, 2 * S], F32)
    pm = ctx.enter_context(nc.psum_tensor("pm", [P, 2, 512], F32))
    ps = ctx.enter_context(nc.psum_tensor("ps", [P, 2, 512], F32))
    pv = ctx.enter_context(nc.psum_tensor("pv", [P, 2, 512], F32))
    mrow_i = stage[0:B, 0:S].bitcast(I32)
    mrow = stage[0:B, S:2 * S]
    mres = stage[0:B, 2 * S:3 * S]
    mparts = stage[0:B, 3 * S:3 * S + 3 * S // 2].bitcast(BF16).rearrange("b (s t) -> b s t", s=3)
    mparts_d = nc.dram_tensor("mask_parts", (3, B, S), BF16, kind="Internal").ap()

    ident_ready = sem("ident_ready")
    const_ready = sem("const_ready")
    rows_ready = sem("rows_ready")
    dve_chain = sem("dve_chain")
    pool_setup = sem("pool_setup")
    gate_in = sem("gate_in")
    gate_exp = sem("gate_exp")
    gate_ready = sem("gate_ready")
    mask_written = sem("mask_written")
    mask_stacked = sem("mask_stacked")
    x2_written = sem("x2_written")
    x2T_full = sem("x2T_full")
    x2T_evac = sem("x2T_evac")
    max_full = sem("max_full")
    max_read = sem("max_read")
    st_full = sem("st_full")
    exp_done = sem("exp_done")
    pv_full = sem("pv_full")
    pv_evac = sem("pv_evac")
    route_chain = sem("route_chain")
    stage_in = sem("stage_in")
    largest_ready = sem("largest_ready")
    largest_all_ready = sem("largest_all_ready")
    scale_chain = sem("scale_chain")
    scale_ready = sem("scale_ready")
    scaled = sem("scaled")
    high_ready = sem("high_ready")
    low_ready = sem("low_ready")
    parts_written = sem("parts_written")
    logits_read = sem("logits_read")
    gate_weights = sem("gate_weights")
    chosen_ready = sem("chosen_ready")
    places_full = sem("places_full")
    places_read = sem("places_read")
    rest_ready = sem("rest_ready")
    slot_ready = sem("slot_ready")
    scattered = sem("scattered")
    logits_full = sem("logits_full")
    dve_setup = sem("dve_setup")
    pe_tick, dve_tick = sem("pe_tick"), sem("dve_tick")
    sp_tick, pool_tick = R.sp_tick, R.pool_tick

    block = ctx.enter_context(nc.Block())

    def schedule(eng, iteration):
        for i in range(3):
            iteration(i, i % 2)
        with eng.Fori(1, (B - 1) // 2) as k:
            for u in range(2):
                iteration(2 * k + 1 + u, 1 - u)
        for i in range((B - 1) // 2 * 2 + 1, B + 2):
            iteration(i, i % 2)

    def has(i, shift):
        return not isinstance(i, int) or 0 <= i + shift < B

    @block.sync
    def _(sp):
        def load_weights(T, wq, wk, wv, wo):
            for dst, src, loaded in ((T.wq, wq, T.wq_in), (T.wk, wk, T.wk_in), (T.wv, wv, T.wts_in),
                                     (T.wo, wo, T.wts_in)):
                sp.dma_start(dst[:], src.rearrange("(k p) n -> p k n", p=P)).then_inc(loaded, 16)

        def load_src(T, src, b, full):
            fence(sp, full, b, sp_tick)
            sp.dma_start(T.src[:], src[b].rearrange("(t p) d -> p t d", p=P)).then_inc(T.src_in, 16)

        def bounce(T, b, which, split, parts, written):
            fence(sp, split, b + 1, sp_tick)
            fence(sp, T.q_stacked if which == 0 else T.k_stacked, 48 * b, sp_tick)
            sp.dma_start(T.parts_d[which].rearrange("s (k f) (h t) -> (f h) s k t", k=KT, t=S), parts[:])\
              .then_inc(written, 16)

        def stack(T, b, par, which, written, runs, dst, stacked):
            fence(sp, written, 16 * (b + 1), sp_tick)
            fence(sp, st_full, T.through(b - 2), sp_tick)
            for place, part, parts, repeats in runs:
                if parts > 1:
                    src = T.parts_d[which, part:part + parts].rearrange("s f (h t) -> (s f) (h t)", t=S)
                else:
                    src = T.parts_d[which, part:part + 1].to_broadcast((repeats, HD, H * S))
                rows = dst[HD * place:HD * (place + parts * repeats), par]
                sp.dma_start(rows.rearrange("p h t -> p (h t)"), src).then_inc(stacked, 16)

        def stack_max(T, b, par):
            fence(sp, T.nm_evac, b + 1, sp_tick)
            fence(sp, T.m_stacked, 16 * b, sp_tick)
            sp.dma_start(T.m_d.rearrange("s h t -> (s h) t"), T.npT[:]).then_inc(T.m_written, 16)
            fence(sp, T.m_written, 16 * (b + 1), sp_tick)
            sp.dma_start(T.qs[T.max_k:T.max_k + MAX_ROWS, par], T.m_d).then_inc(T.m_stacked, 16)

        def bring_q(T, b, par):
            bounce(T, b, 0, T.q_split, T.qp, T.q_written)
            stack(T, b, par, 0, T.q_written, Q_RUNS, T.qs, T.q_stacked)

        def bring_k(T, b, par):
            bounce(T, b, 1, T.k_split, T.kp, T.k_written)
            stack(T, b, par, 1, T.k_written, K_RUNS, T.ks, T.k_stacked)

        def load_context(b):
            load_src(C, ctx_in, b, C.kv_full)
            fence(sp, C.keep_done, b, sp_tick)
            sp.dma_start(C.keep_i[:], mask[b].partition_broadcast(P)).then_inc(C.keep_in, 16)

        sp.dma_start(A.src[:], x[0].rearrange("(t p) d -> p t d", p=P)).then_inc(A.src_in, 16)
        sp.dma_start(gate[:], gate_raw.rearrange("(k p) t -> p k t", p=P)).then_inc(gate_in, 16)
        sp.dma_start(mrow_i[:], mask).then_inc(gate_in, 16)
        load_weights(A, w_q1, w_k1, w_v1, w_o1)
        sp.dma_start(wr[:], w_r.rearrange("(k p) e -> p k e", p=P)).then_inc(C.wts_in, 16)
        load_weights(C, wqT, wkT, wvT, woT)
        sp.dma_start(C.bq[:], bq).then_inc(C.wts_in, 16)
        sp.dma_start(C.bk[:], bk).then_inc(C.wts_in, 16)
        sp.dma_start(C.bv[:], bv.partition_broadcast(P)).then_inc(C.wts_in, 16)
        sp.dma_start(C.bo[:], bo.partition_broadcast(P)).then_inc(C.wts_in, 16)
        sp.wait_ge(dve_setup, 1)
        sp.dma_start(mparts_d.rearrange("s b t -> b s t"), mparts[:]).then_inc(mask_written, 16)
        sp.wait_ge(mask_written, 16)
        bring_q(A, 0, 0)
        bring_k(A, 0, 0)
        def load_matrix(e, m):
            n = 2 * e + m
            fence(sp, low_ready, n, sp_tick)
            src = (w_1, w_2)[m][bass.ds(e, 1)]
            dst = stage[:].rearrange("p (k n) -> p k n", k=(KT, FT)[m])
            sp.dma_start(dst, src.rearrange("o (k p) n -> p (o k) n", p=P)).then_inc(stage_in, 16)

        def store_matrix(e, m):
            fence(sp, low_ready, 2 * e + m + 1, sp_tick)
            sp.dma_start(R.parts_d[bass.ds(e, 1), m].rearrange("o p s n -> p (o s n)"),
                         parts[:].rearrange("p s n -> p (s n)")).then_inc(parts_written, 16)

        sp.wait_ge(const_ready, 1)
        sp.dma_start(R.xs_d[E * ROOM:E * ROOM + TILE].rearrange("(n p) d -> p n d", p=P),
                     zeros[:].unsqueeze(1).to_broadcast((P, TILE // P, D))).then_inc(mask_written, 16)
        sp.dma_start(R.ys_d[B * S * TOP:NTILE * TILE].rearrange("(n p) d -> p n d", p=P),
                     zeros[:].unsqueeze(1).to_broadcast((P, NTILE * TILE // P - B * S * TOP // P, D)))\
          .then_inc(mask_written, 16)

        def iteration(i, odd):
            if has(i, -1):
                b = i - 1
                bring_k(C, b, 1 - odd)
                fence(sp, st_full, C.through(b - 2), sp_tick)
                if isinstance(i, int) and i == 1:
                    sp.wait_ge(const_ready, 2)
                rows = mparts_d[:, b, :].unsqueeze(1).to_broadcast((3, H, S))
                sp.dma_start(C.ks[STACK:STACK + MASK_ROWS, 1 - odd], rows).then_inc(mask_stacked, 16)
                store_matrix(i - 1, 1)
            if has(i, 0):
                load_matrix(i, 0)
            if has(i, 1):
                fence(sp, A.res_copied, i + 1, sp_tick)
                load_src(A, x, i + 1, A.src_full)
            if has(i, -1):
                bring_q(C, i - 1, 1 - odd)
            if has(i, 0):
                stack_max(A, i, odd)
                load_context(i)
                store_matrix(i, 0)
                load_matrix(i, 1)
            if has(i, 1):
                bring_q(A, i + 1, 1 - odd)
                bring_k(A, i + 1, 1 - odd)
            if has(i, -2):
                b = i - 2
                fence(sp, C.ln_done, b + 1, sp_tick)
                sp.dma_start(x2[:, bass.ds(b * TT, TT)], C.out[:]).then_inc(x2_written, 16)
            if has(i, -1):
                stack_max(C, i - 1, 1 - odd)

        schedule(sp, iteration)
        sp.wait_ge(rest_ready, 1)
        for e in range(E):
            row = sp.value_load(R.rest[0:1, e:e + 1], min_val=0, max_val=E * ROOM - TILE)
            sp.dma_start(R.xs_d[bass.ds(row, TILE)].rearrange("(n p) d -> p n d", p=P),
                         R.zeros[:].unsqueeze(1).to_broadcast((P, TILE // P, D))).then_inc(mask_written, 16)
        sp.wait_ge(x2_written, 16 * B)
        sp.wait_ge(mask_written, 16 * (3 + E))
        sp.wait_ge(parts_written, 16 * 2 * E)

    @block.gpsimd
    def _(pool):
        setup = Steps(pool, pool_setup, 100, 0)
        setup.link(pool.memset(identf[:], 0.0))
        setup.link(pool.affine_select(out=identf[:], in_=identf[:], compare_op=ALU.not_equal, fill=1.0, base=0,
                                      pattern=[[-1, P]], channel_multiplier=1))
        pool.drain().then_inc(ident_ready, 1)
        for m in (identb, tri_qk, tri_kq):
            setup.link(pool.memset(m[:], 0.0))
        setup.link(pool.affine_select(out=identb[:], in_=identb[:], compare_op=ALU.not_equal, fill=1.0, base=0,
                                      pattern=[[-1, P]], channel_multiplier=1))
        setup.link(pool.affine_select(out=tri_qk[:], in_=tri_qk[:], compare_op=ALU.is_ge, fill=CAUSAL_FILL,
                                      base=0, pattern=[[-1, P]], channel_multiplier=1))
        setup.link(pool.affine_select(out=tri_kq[:], in_=tri_kq[:], compare_op=ALU.is_ge, fill=CAUSAL_FILL,
                                      base=0, pattern=[[1, P]], channel_multiplier=-1))
        setup.link(pool.memset(zeros[:], 0.0))
        setup.link(pool.memset(R.run[:], 0.0))
        setup.link(pool.memset(below[:], 1.0))
        setup.link(pool.affine_select(out=below[:], in_=below[:], compare_op=ALU.is_gt, fill=0.0, base=0,
                                      pattern=[[1, E], [-1, E]], channel_multiplier=0))
        setup.link(pool.memset(all_ones[:], 1.0))
        setup.link(pool.affine_select(out=upper[:], in_=all_ones[:], compare_op=ALU.is_gt, fill=0.0, base=0,
                                      pattern=[[1, P]], channel_multiplier=-1))
        setup.link(pool.iota(rows_i[:], pattern=[[TILE, B * S // TILE]], base=0, channel_multiplier=0))
        setup.link(pool.tensor_copy(R.rows[:], rows_i[:]))
        setup.link(pool.iota(tile_no_i[:], pattern=[[1, NTILE]], base=0, channel_multiplier=0))
        setup.link(pool.tensor_copy(R.tile_no[:], tile_no_i[:]))
        setup.link(pool.iota(R.room_i[:], pattern=[[ROOM, E]], base=0, channel_multiplier=0))
        setup.link(pool.tensor_copy(R.room[:], R.room_i[:]))
        pool.drain().then_inc(const_ready, 1)
        setup.link(pool.memset(C.v[:], 1.0))
        setup.link(pool.memset(C.qs[STACK:P].bitcast(F32), TWO_ONES))
        setup.link(pool.memset(C.ks[STACK:P].bitcast(F32), TWO_ONES))
        pool.drain().then_inc(const_ready, 1)

        def split_q(T, b):
            wait(pool, T.q_evac, b + 1)
            fence(pool, T.q_written, 16 * b, pool_tick)
            c = Steps(pool, T.qsplit_chain, 3, b)
            c.link(pool.tensor_copy(T.qp[:, 0], T.qf[:]))
            c.link(pool.tensor_tensor(T.qf[:], T.qf[:], T.qp[:, 0], ALU.subtract), pool_tick)
            c.link(pool.tensor_copy(T.qp[:, 1], T.qf[:]))
            c.done()
            pool.tensor_tensor(T.qp[:, 2], T.qf[:], T.qp[:, 1], ALU.subtract).then_inc(T.q_split, 1)

        pool.wait_ge(C.wts_in, 16 * 9)

        def largest_of_all(e, m):
            wait(pool, largest_ready, 2 * e + m + 1)
            fence(pool, scale_chain, 3 * (2 * e + m), pool_tick)
            pool.partition_all_reduce(largest_all[:], largest[:], P, PMAX).then_inc(largest_all_ready, 1)

        def low_part(e, m):
            wait(pool, high_ready, 2 * e + m + 1)
            pool.tensor_tensor(parts[:, 1], stage[:], parts[:, 0], ALU.subtract).then_inc(low_ready, 1)

        def iteration(i, odd):
            if has(i, -1):
                low_part(i - 1, 1)
            if has(i, 0):
                wait(pool, A.src_in, 16 * (i + 1))
                fence(pool, A.res_done, i, pool_tick)
                pool.tensor_copy(A.res[:], A.src[:]).then_inc(A.res_copied, 1)
                largest_of_all(i, 0)
                low_part(i, 0)
            if has(i, 1):
                split_q(A, i + 1)
            if has(i, -1):
                wait(pool, A.ln_done, i)
                fence(pool, C.res_done, i - 1, pool_tick)
                pool.tensor_tensor(C.res[:], A.out[:], C.bo[:].unsqueeze(1).to_broadcast((P, TT, D)), ALU.add)\
                    .then_inc(C.res_copied, 1)
            if has(i, 0):
                largest_of_all(i, 1)
            if has(i, -2):
                fence(pool, slot_ready, i - 1, pool_tick)
                for k in range(TOP):
                    for t in range(TT):
                        pool.indirect_dma_start(R.xs_d, bass.IndirectOffsetOnAxis(ap=slot[:, k, t:t + 1], axis=0),
                                                C.out[:, t], None).then_inc(scattered, 16)

        schedule(pool, iteration)
        pool.wait_ge(scattered, 16 * TOP * TT * B)

    @block.tensor
    def _(pe):
        pe.wait_ge(ident_ready, 1)

        def transpose(T, src, dst_full):
            for k in range(KT):
                for t in range(TT):
                    o = (k * TT + t) * P
                    last = pe.transpose(T.pp[:, o:o + P], src[:, t, k * P:(k + 1) * P], identf[:])
            last.then_inc(dst_full, 1)

        def features(T, w, rhs, full):
            for m in range(KT):
                for k in range(KT):
                    last = pe.matmul(T.pp[:, m * S:(m + 1) * S], w[:, k, m * P:(m + 1) * P], rhs[:, k, :],
                                     start=(k == 0), stop=(k == KT - 1))
            last.then_inc(full, 1)

        def values(T, b, before, count):
            wait(pe, before, count)
            for t in range(TT):
                o = T.pp[:, t * D:(t + 1) * D]
                for k in range(KT):
                    last = pe.matmul(o, T.cT[:, k, t * P:(t + 1) * P], T.wv[:, k, :],
                                     start=(k == 0), stop=(k == KT - 1))
            last.then_inc(T.v_full, 1)

        def scores_for_max(T, b, par, h):
            if h == 0:
                if T.cross and isinstance(b, int) and b == 0:
                    pe.wait_ge(const_ready, 2)
                wait(pe, T.q_stacked, 48 * (b + 1))
                wait(pe, T.k_stacked, 48 * (b + 1))
                if T.cross:
                    wait(pe, mask_stacked, 16 * (b + 1))
            wait(pe, max_read, T.head(b, h) - 1)
            q, k = T.qs[0:T.max_k, par, h], T.ks[0:T.max_k, par, h]
            bank = pm[:, h % 2]
            if T.cross:
                for t in range(TT):
                    last = pe.matmul(bank[:, t * S:(t + 1) * S], q[:, t * P:(t + 1) * P], k, start=True, stop=True)
            else:
                for t, o in ((0, 0), (1, P)):
                    n = (t + 1) * P
                    pe.matmul(bank[:, o:o + n], q[:, t * P:(t + 1) * P], k[:, 0:n], start=True, stop=False)
                    last = pe.matmul(bank[:, o + n - P:o + n], identb[:], tri_qk[:], start=False, stop=True)
            last.then_inc(max_full, 1)

        def transpose_max(T, b):
            wait(pe, T.nm_split, b + 1)
            if T.cross and has(b, -1):
                fence(pe, logits_read, b, pe_tick)
            else:
                fence(pe, T.v_evac, b + 1, pe_tick)
            pp = T.pp[:].bitcast(BF16)
            for t in range(TT):
                last = pe.transpose(pp[0:3 * H, t * P:(t + 1) * P],
                                    T.np[:, t].rearrange("p s h -> p (s h)"), identb[:])
            last.then_inc(T.nm_full, 1)

        def scores(T, b, par, h):
            if h == 0:
                wait(pe, T.m_stacked, 16 * (b + 1))
            wait(pe, exp_done, T.head(b, h) - 1)
            q, k = T.qs[0:T.st_k, par, h], T.ks[0:T.st_k, par, h]
            bank = ps[:, h % 2]
            if T.cross:
                for t in range(TT):
                    last = pe.matmul(bank[:, t * S:(t + 1) * S], k[:, t * P:(t + 1) * P], q, start=True, stop=True)
            else:
                for t, o in ((0, 0), (1, S)):
                    n = S - t * P
                    pe.matmul(bank[:, o:o + n], k[:, t * P:(t + 1) * P], q[:, t * P:S], start=True, stop=False)
                    last = pe.matmul(bank[:, o:o + P], identb[:], tri_kq[:], start=False, stop=True)
            last.then_inc(st_full, 1)

        def weigh_values(T, b, h):
            wait(pe, exp_done, T.head(b, h) + 1)
            if h == 0:
                wait(pe, T.v_evac, b + 1)
            if h % 8 == 0:
                wait(pe, pv_evac, 2 * T.order(b) + h // 8 - 1)
            g, o = h % 4, (h // 4 % 2) * S
            for t in range(TT):
                q0 = 0 if T.cross or t == 0 else P
                last = pe.matmul(pv[32 * g:32 * g + 32, h // 8, o + q0:o + S], T.v[:, t, h, :],
                                 p[:, h % 4, t * S:(t + 1) * S - q0], start=(t == 0), stop=(t == TT - 1))
            last.then_inc(pv_full, 1)

        def transpose_weighted(T, b, half, before, count):
            wait(pe, pv_evac, 2 * T.order(b) + half + 1)
            wait(pe, before, count)
            for t in range(TT):
                for g in range(2):
                    o = (t * 2 + g) * P
                    last = pe.transpose(T.pp[:, o:o + P], T.pvs[:, 2 * half + g, t * P:(t + 1) * P], identf[:])
            last.then_inc(T.weights_full, 1)

        def transpose_out(T, b):
            wait(pe, T.norm_done, 2 * (b + 1))
            transpose(T, T.an, T.aT_full)

        def project_out(T, b):
            wait(pe, T.aT_evac, b + 1)
            for t in range(TT):
                for k in range(KT):
                    last = pe.matmul(T.pp[:, t * D:(t + 1) * D], T.aT[:, k, t * P:(t + 1) * P], T.wo[:, k, :],
                                     start=(k == 0), stop=(k == KT - 1))
            last.then_inc(T.o_full, 1)

        def logits(b):
            wait(pe, x2T_evac, b + 1)
            if has(b, 1):
                wait(pe, C.v_evac, b + 2)
            for t in range(TT):
                for k in range(KT):
                    last = pe.matmul(C.pp[:, t * E:(t + 1) * E], x2T[:, k, t * P:(t + 1) * P], wr[:, k],
                                     start=(k == 0), stop=(k == KT - 1))
            last.then_inc(logits_full, 1)

        def places(b):
            wait(pe, chosen_ready, b + 1)
            if has(b, 1):
                wait(pe, C.nm_evac, b + 2)
            rows = chosen[:].rearrange("p t e -> p (t e)")
            pe.matmul(C.pp[:, 0:TT * E], upper[:], rows, start=True, stop=False)
            pe.matmul(C.pp[:, E:TT * E], all_ones[:], chosen[:, 0], start=False, stop=True)
            for t in range(TT):
                last = pe.matmul(C.pp[:, TT * E:(TT + 1) * E], all_ones[:], chosen[:, t],
                                 start=(t == 0), stop=(t == TT - 1))
            last.then_inc(places_full, 1)

        def transpose_x(b):
            wait(pe, A.src_in, 16 * (b + 1))
            wait(pe, A.nm_evac, b)
            transpose(A, A.src, A.src_full)

        def transpose_context(b):
            wait(pe, C.src_in, 16 * (b + 1))
            wait(pe, C.nm_evac, b)
            if has(b, -2):
                wait(pe, places_read, b - 1)
            transpose(C, C.src, C.kv_full)

        def end(T, b, s, before, count):
            if s < WLAG:
                weigh_values(T, b, H - WLAG + s)
            if s == WEIGHTED[T.cross]:
                transpose_weighted(T, b, 0, before, count)
            if s == WEIGHTED[T.cross] + 1:
                transpose_weighted(T, b, 1, T.norm_done, 2 * b + 1)
            if s == OUT_T[T.cross]:
                transpose_out(T, b)
            if s == OUT[T.cross]:
                project_out(T, b)

        transpose_x(0)
        pe.wait_ge(A.src_evac, 1)
        pe.wait_ge(A.wq_in, 16)
        features(A, A.wq, A.xT, A.q_full)
        pe.wait_ge(A.wk_in, 16)
        pe.wait_ge(A.q_evac, 1)
        features(A, A.wk, A.xT, A.k_full)
        pe.wait_ge(A.wts_in, 16 * 2)
        pe.wait_ge(C.wts_in, 16 * 9)
        pe.wait_ge(rows_ready, 1)
        pe.wait_ge(const_ready, 1)

        def iteration(i, odd):
            for s in range(H + LAG):
                if has(i, 0) and s < H:
                    scores_for_max(A, i, odd, s)
                if has(i, -2) and s >= LAG:
                    scores(C, i - 2, odd, s - LAG)
                    if s >= LAG + WLAG:
                        weigh_values(C, i - 2, s - LAG - WLAG)
                if has(i, 0) and s == H + 1:
                    transpose_max(A, i)
                if has(i, -1):
                    end(A, i - 1, s, *((A.k_evac, i + 1) if has(i, 0) else (A.nm_evac, i)))
                if has(i, 0) and s == VALUES[0]:
                    if has(i, -1):
                        values(A, i, A.res_done, i)
                    else:
                        values(A, i, A.k_evac, 1)
                if has(i, -1):
                    b = i - 1
                    if s == 0:
                        transpose_context(b)
                    if s == C_KEYS:
                        wait(pe, C.kv_evac, b + 1)
                        features(C, C.wk, C.cT, C.k_full)
                    if s == C_TOKENS_T:
                        wait(pe, A.ln_done, b + 1)
                        wait(pe, C.k_evac, b + 1)
                        transpose(C, A.out, C.src_full)
                    if s == C_QUERIES:
                        wait(pe, C.src_evac, b + 1)
                        features(C, C.wq, C.xT, C.q_full)
            for s in range(H + LAG):
                if has(i, -1) and s < H:
                    scores_for_max(C, i - 1, 1 - odd, s)
                if has(i, 0) and s >= LAG:
                    scores(A, i, odd, s - LAG)
                    if s >= LAG + WLAG:
                        weigh_values(A, i, s - LAG - WLAG)
                if has(i, -1) and s == H + 1:
                    transpose_max(C, i - 1)
                if has(i, -2):
                    if s == WEIGHTED[1] and not has(i, -1):
                        wait(pe, places_read, i - 2)
                    end(C, i - 2, s, *((C.q_evac, i) if has(i, -1) else (C.nm_evac, i - 1)))
                if has(i, 1):
                    if s == 0:
                        transpose_x(i + 1)
                    if s == A_QUERIES:
                        wait(pe, A.src_evac, i + 2)
                        features(A, A.wq, A.xT, A.q_full)
                    if s == A_KEYS:
                        wait(pe, A.q_evac, i + 2)
                        features(A, A.wk, A.xT, A.k_full)
                if has(i, -1) and s == VALUES[1]:
                    if has(i, -2):
                        values(C, i - 1, C.res_done, i - 1)
                    else:
                        values(C, i - 1, C.q_evac, i)
                if has(i, -2) and s == X2_T:
                    wait(pe, C.ln_done, i - 1)
                    if has(i, -1):
                        wait(pe, C.v_evac, i)
                    transpose(C, C.out, x2T_full)
                if has(i, -2) and s == LOGITS:
                    logits(i - 2)
                if has(i, -2) and s == H + LAG - 1:
                    places(i - 2)

        schedule(pe, iteration)

    @block.scalar
    def _(act):
        nc.scalar.preload_act_table_set("natural_log_exp_and_others")
        act.wait_ge(gate_in, 32)
        act.activation(gate[:], gate[:], ACT.Exp, scale=-1.0).then_inc(gate_exp, 1)
        act.wait_ge(rows_ready, 1)

        def copy(dst, src, full, b, evac):
            wait(act, full, b + 1)
            act.copy(dst, src).then_inc(evac, 1)

        def evac_k(T, b):
            wait(act, T.k_full, b + 1)
            wait(act, T.k_split, b)
            if T.cross:
                for m in range(KT):
                    last = act.activation(T.kf[:, m], T.pp[:, m * S:(m + 1) * S], ACT.Identity,
                                          bias=T.bk[:, m:m + 1])
            else:
                last = act.copy(T.kf[:], T.pp[:].rearrange("p (k t) -> p k t", k=KT))
            last.then_inc(T.k_evac, 1)

        def pp3(T):
            return T.pp[:].rearrange("p (k t) -> p k t", k=KT)

        def evac_v(T, b):
            wait(act, T.v_full, b + 1)
            for t in range(TT):
                last = act.copy(T.v[:, t, :, 0:HD],
                                T.pp[:, t * D:(t + 1) * D].rearrange("p (h d) -> p h d", h=H))
            last.then_inc(T.v_evac, 1)

        def exponentials(T, b, h):
            wait(act, st_full, T.head(b, h) + 1)
            wait(act, pv_full, T.head(b, h) - 3)
            n = 2 * S if T.cross else 2 * S - P
            act.activation(p[:, h % 4, 0:n], ps[:, h % 2, 0:n], ACT.Exp).then_inc(exp_done, 1)

        def evac_weighted(T, b, half):
            wait(act, pv_full, T.head(b, 8 * (half + 1)))
            wait(act, T.weights_full, 2 * b - 1 + half)
            act.copy(T.pvs[:, 2 * half:2 * half + 2], pv[:, half].rearrange("p (g t) -> p g t", g=2))\
               .then_inc(pv_evac, 1)

        def evac_max(T, b):
            wait(act, T.nm_full, b + 1)
            wait(act, T.m_written, 16 * b)
            act.copy(T.npT[:], T.pp[:].bitcast(BF16)[0:3 * H, 0:S]).then_inc(T.nm_evac, 1)

        def root(T, b):
            wait(act, T.stats_done, b + 1)
            wait(act, T.rstd_done, b)
            act.activation(T.lnv[:], T.ve[:], ACT.Ln).then_inc(T.ln_taken, 1)
            wait(act, T.ln_taken, b + 1)
            act.activation(T.y0[:], T.lnv[:], ACT.Exp, scale=-0.5).then_inc(T.root_done, 1)

        copy(A.xT[:], pp3(A), A.src_full, 0, A.src_evac)
        evac_k(A, 0)
        act.wait_ge(C.wts_in, 16 * 9)
        act.wait_ge(const_ready, 2)

        def end(T, b, s):
            if s == 2:
                evac_weighted(T, b, 1)
            if s == OUT_T[T.cross] + 1:
                copy(T.aT[:], pp3(T), T.aT_full, b, T.aT_evac)
            if s == NORM[T.cross]:
                root(T, b)

        def high_part(e, m, s):
            n = 2 * e + m
            if s == 0:
                wait(act, scale_ready, n + 1)
                act.activation(stage[:], stage[:], ACT.Identity, scale=scale[:, 0:1]).then_inc(scaled, 1)
            if s == 1:
                wait(act, scaled, n + 1)
                wait(act, parts_written, 16 * n)
                act.copy(parts[:, 0], stage[:]).then_inc(high_ready, 1)

        def iteration(i, odd):
            for s in range(H + LAG):
                if has(i, -1):
                    b = i - 1
                    if s == 0:
                        copy(C.cT[:], pp3(C), C.kv_full, b, C.kv_evac)
                    high_part(b, 1, s)
                    end(A, b, s)
                    if s == C_KEYS + 1:
                        evac_k(C, b)
                    if s == C_TOKENS_T + 1:
                        copy(C.xT[:], pp3(C), C.src_full, b, C.src_evac)
                if has(i, 0) and s == VALUES[0] + 1:
                    evac_v(A, i)
                if has(i, -2) and s == LAG + WLAG + 8:
                    evac_weighted(C, i - 2, 0)
                if has(i, 0) and s == H + 1:
                    evac_max(A, i)
                if has(i, -2) and s >= LAG:
                    exponentials(C, i - 2, s - LAG)
            for s in range(H + LAG):
                if has(i, 1):
                    if s == 1:
                        copy(A.xT[:], pp3(A), A.src_full, i + 1, A.src_evac)
                    if s == A_KEYS + 1:
                        evac_k(A, i + 1)
                if has(i, 0):
                    high_part(i, 0, s)
                if has(i, -2):
                    b = i - 2
                    end(C, b, s)
                    if s == X2_T + 1:
                        wait(act, x2T_full, b + 1)
                        wait(act, logits_full, b)
                        act.copy(x2T[:], pp3(C)).then_inc(x2T_evac, 1)
                    if s == LOGITS + 2:
                        wait(act, logits_read, b + 1)
                        act.activation(g[:], lgs[:], ACT.Exp).then_inc(gate_weights, 1)
                if has(i, 0) and s == LAG + WLAG + 8:
                    evac_weighted(A, i, 0)
                if has(i, -1) and s == H + 1:
                    evac_max(C, i - 1)
                if has(i, 0) and s >= LAG:
                    exponentials(A, i, s - LAG)

        schedule(act, iteration)

    @block.vector
    def _(dve):
        setup = Steps(dve, dve_chain, 100, 0)
        setup.link(dve.memset(A.v[:], 1.0))
        setup.link(dve.memset(A.ks[STACK:P].bitcast(F32), TWO_ONES))
        dve.drain().then_inc(rows_ready, 1)
        dve.wait_ge(gate_exp, 1)
        setup.link(dve.tensor_scalar(gate[:], gate[:], 1.0, None, ALU.add))
        setup.link(dve.reciprocal(gate[:], gate[:]))
        dve.tensor_scalar(gate[:], gate[:], HD ** -0.5, None, ALU.mult).then_inc(gate_ready, 1)
        dve.wait_ge(gate_ready, 1)
        dve.wait_ge(gate_in, 32)
        setup.link(dve.tensor_scalar(mrow[:], mrow_i[:], 0.0, MASKED_SCORE, ALU.is_equal, ALU.mult))
        setup.link(dve.tensor_copy(mparts[:, 0], mrow[:]))
        setup.link(dve.tensor_tensor(mres[:], mrow[:], mparts[:, 0], ALU.subtract))
        setup.link(dve.tensor_copy(mparts[:, 1], mres[:]))
        setup.link(dve.tensor_tensor(mparts[:, 2], mres[:], mparts[:, 1], ALU.subtract))
        dve.drain().then_inc(dve_setup, 1)

        def evac_q(T, b):
            wait(dve, T.q_full, b + 1)
            wait(dve, T.q_split, b)
            if T.cross:
                for m in range(KT):
                    last = dve.tensor_scalar(T.qf[:, m], T.pp[:, m * S:(m + 1) * S], T.bq[:, m:m + 1],
                                             D ** -0.5, ALU.add, ALU.mult)
            else:
                last = dve.tensor_tensor(T.qf[:], T.pp[:].rearrange("p (k t) -> p k t", k=KT), gate[:], ALU.mult)
            last.then_inc(T.q_evac, 1)

        def split_k(T, b):
            wait(dve, T.k_evac, b + 1)
            wait(dve, T.k_written, 16 * b)
            c = Steps(dve, T.ksplit_chain, 4 if T.cross else 3, b)
            if T.cross:
                wait(dve, T.keep_done, b + 1)
                c.link(dve.tensor_tensor(T.kf[:], T.kf[:], T.keep[:].unsqueeze(1).to_broadcast((P, KT, S)),
                                         ALU.mult))
            c.link(dve.tensor_copy(T.kp[:, 0], T.kf[:]))
            c.link(dve.tensor_tensor(T.kf[:], T.kf[:], T.kp[:, 0], ALU.subtract))
            c.link(dve.tensor_copy(T.kp[:, 1], T.kf[:]))
            c.done()
            dve.tensor_tensor(T.kp[:, 2], T.kf[:], T.kp[:, 1], ALU.subtract).then_inc(T.k_split, 1)

        def read_max(T, b, h):
            wait(dve, max_full, T.head(b, h) + 1)
            bank = pm[:, h % 2]
            if T.cross:
                last = dve.tensor_reduce(T.mx[:, :, h], bank.rearrange("p (t k) -> p t k", t=TT), X, ALU.max)
            else:
                last = dve.tensor_reduce(T.mx[:, :, h], bank[:, 0:3 * P].rearrange("p (t k) -> p t k", t=3), X, ALU.max)
            last.then_inc(max_read, 1)

        def split_max(T, b):
            wait(dve, max_read, T.through(b))
            wait(dve, T.nm_full, b)
            c = Steps(dve, T.nm_chain, 4 if T.cross else 5, b)
            if not T.cross:
                c.link(dve.tensor_tensor(T.mx[:, 1], T.mx[:, 1], T.mx[:, 2], ALU.max))
            c.link(dve.tensor_scalar(T.nf[:], T.mx[:, 0:TT], -1.0, None, ALU.mult))
            c.link(dve.tensor_copy(T.np[:, :, 0], T.nf[:]))
            c.link(dve.tensor_tensor(T.nr[:], T.nf[:], T.np[:, :, 0], ALU.subtract))
            c.link(dve.tensor_copy(T.np[:, :, 1], T.nr[:]))
            c.done()
            dve.tensor_tensor(T.np[:, :, 2], T.nr[:], T.np[:, :, 1], ALU.subtract).then_inc(T.nm_split, 1)

        def normalise(T, b, half):
            wait(dve, T.weights_full, 2 * b + half + 1)
            wait(dve, T.aT_full, b)
            heads = T.pp[:].rearrange("p (t h c) -> p t h c", t=TT, h=H // 2)
            c = Steps(dve, T.norm_chain, 1, 2 * b + half)
            c.link(dve.reciprocal(T.rec[:], heads[:, :, :, HD]))
            c.done()
            dve.tensor_tensor(T.an[:, :, half * P:(half + 1) * P].rearrange("p t (h c) -> p t h c", c=HD),
                              heads[:, :, :, 0:HD], T.rec[:].unsqueeze(3).to_broadcast((P, TT, H // 2, HD)),
                              ALU.mult).then_inc(T.norm_done, 1)

        def split_q(T, b, step):
            def link(instruction, n):
                instruction.then_inc(T.qsplit_chain, 1)
                wait(dve, T.qsplit_chain, 3 * b + n)

            if step == 0:
                wait(dve, T.q_evac, b + 1)
                wait(dve, T.q_written, 16 * b)
                link(dve.tensor_copy(T.qp[:, 0], T.qf[:]), 1)
            if step == 1:
                link(dve.tensor_tensor(T.qf[:], T.qf[:], T.qp[:, 0], ALU.subtract), 2)
                link(dve.tensor_copy(T.qp[:, 1], T.qf[:]), 3)
            if step == 2:
                dve.tensor_tensor(T.qp[:, 2], T.qf[:], T.qp[:, 1], ALU.subtract).then_inc(T.q_split, 1)

        def evac_v(b):
            wait(dve, C.v_full, b + 1)
            for t in range(TT):
                last = dve.tensor_tensor(C.v[:, t, :, 0:HD],
                                         C.pp[:, t * D:(t + 1) * D].rearrange("p (h d) -> p h d", h=H),
                                         C.bv[:].rearrange("p (h d) -> p h d", h=H), ALU.add)
            last.then_inc(C.v_evac, 1)

        def residual(T, b):
            wait(dve, T.o_full, b + 1)
            wait(dve, T.res_copied, b + 1)
            wait(dve, T.ln_done, b)
            dve.tensor_tensor(T.r[:], T.pp[:].rearrange("p (t d) -> p t d", t=TT), T.res[:], ALU.add)\
               .then_inc(T.res_done, 1)
            wait(dve, T.res_done, b + 1)
            c = Steps(dve, T.ln_chain, 6, b)
            for t in range(TT):
                c.link(dve.bn_stats(T.st[:, t], T.r[:, t]), dve_tick)
            for t in range(TT):
                c.link(dve.bn_aggr(T.mv[:, t], T.st[:, t]), dve_tick)
            dve.tensor_scalar(T.ve[:], T.mv[:, :, 1], EPS, None, ALU.add).then_inc(T.stats_done, 1)

        def layernorm(T, b, readers):
            wait(dve, T.stats_done, b + 1)
            wait(dve, T.root_done, b + 1)
            c = Steps(dve, T.ln_chain, 6, b)
            c.n = 4
            c.link(dve.tensor_tensor(T.yy[:], T.y0[:], T.y0[:], ALU.mult))
            c.link(dve.scalar_tensor_tensor(T.yy[:], T.yy[:], -0.5, T.ve[:], ALU.mult, ALU.mult))
            c.done()
            dve.scalar_tensor_tensor(T.rstd[:], T.yy[:], 1.5, T.y0[:], ALU.add, ALU.mult).then_inc(T.rstd_done, 1)
            wait(dve, T.rstd_done, b + 1)
            for sem_, count in readers:
                wait(dve, sem_, count)
            for t in range(TT):
                last = dve.tensor_scalar(T.out[:, t], T.r[:, t], T.mv[:, t, 0:1], T.rstd[:, t:t + 1],
                                         ALU.subtract, ALU.mult)
            last.then_inc(T.ln_done, 1)

        evac_q(A, 0)
        for step in range(3):
            split_q(A, 0, step)
        split_k(A, 0)
        dve.wait_ge(C.wts_in, 16 * 9)
        dve.wait_ge(const_ready, 1)

        def route(b, step):
            first = {0: 0, 1: 1, 2: 6, 3: 9, 4: 11}[step]
            c = Steps(dve, route_chain, 15, b)
            c.n = first
            if step == 0:
                wait(dve, logits_full, b + 1)
                l3 = C.pp[:, 0:TT * E].rearrange("p (t e) -> p t e", e=E)
                c.link(dve.tensor_reduce(lgm[:], l3, X, ALU.max))
                dve.tensor_tensor(lgs[:], l3, lgm[:].unsqueeze(2).to_broadcast((P, TT, E)), ALU.subtract)\
                   .then_inc(logits_read, 1)
            if step == 1:
                wait(dve, gate_weights, b + 1)
                c.link(dve.tensor_reduce(gs[:], g[:], X, ALU.add))
                c.link(dve.reciprocal(gs[:], gs[:]))
                c.link(dve.tensor_tensor(g[:], g[:], gs[:].unsqueeze(2).to_broadcast((P, TT, E)), ALU.mult))
                own = g[:].unsqueeze(3).to_broadcast((P, TT, E, E))
                other = g[:].unsqueeze(2).to_broadcast((P, TT, E, E))
                dve.tensor_tensor(gt[:], other, own, ALU.is_gt)
                c.link(dve.tensor_tensor(eq[:], other, own, ALU.is_equal))
                c.link(dve.tensor_tensor(eq[:], eq[:], below[:].unsqueeze(1).to_broadcast((P, TT, E, E)), ALU.mult))
            if step == 2:
                c.link(dve.tensor_tensor(gt[:], gt[:], eq[:], ALU.add))
                c.link(dve.tensor_reduce(rank[:], gt[:], X, ALU.add))
                wait(dve, places_full, b)
                dve.tensor_scalar(chosen[:], rank[:], float(TOP), None, ALU.is_lt).then_inc(chosen_ready, 1)
                for k in range(TOP):
                    last = dve.tensor_scalar(R.pick[:, k, bass.ds(b * TT, TT)], rank[:], float(k), None, ALU.is_equal)
                c.link(last)
            if step == 3:
                wait(dve, places_full, b + 1)
                place = R.place[:, bass.ds(b * TT, TT)]
                c.link(dve.tensor_tensor(place, C.pp[:, 0:TT * E].rearrange("p (t e) -> p t e", e=E),
                                         R.run[:].unsqueeze(1).to_broadcast((P, TT, E)), ALU.add))
                dve.tensor_tensor(R.run[:], R.run[:], C.pp[:, TT * E:(TT + 1) * E], ALU.add).then_inc(places_read, 1)
                c.link(dve.tensor_tensor(at[:], place, R.room[:].unsqueeze(1).to_broadcast((P, TT, E)), ALU.add))
            if step == 4:
                wait(dve, places_read, b + 1)
                for k in range(TOP):
                    last = dve.tensor_tensor(pw[:, k], R.pick[:, k, bass.ds(b * TT, TT)], at[:], ALU.mult)
                c.link(last)
                c.link(dve.tensor_reduce(slot_f[:], pw[:], X, ALU.add))
                wait(dve, scattered, 16 * TOP * TT * b)
                dve.tensor_copy(slot[:], slot_f[:]).then_inc(slot_ready, 1)
                for k in range(TOP):
                    last = dve.tensor_tensor(pw[:, k], R.pick[:, k, bass.ds(b * TT, TT)], g[:], ALU.mult)
                c.link(last)
                c.link(dve.tensor_reduce(R.wk[:, :, bass.ds(b * TT, TT)], pw[:], X, ALU.add))
                c.done()

        def measure(e, m, s):
            n = 2 * e + m
            if s == H:
                wait(dve, stage_in, 16 * (n + 1))
                wait(dve, largest_all_ready, n)
                dve.tensor_reduce(largest[:], stage[:], X, ALU.max, apply_absolute_value=True)\
                   .then_inc(largest_ready, 1)
            if s == H + LAG - 1:
                wait(dve, largest_all_ready, n + 1)
                wait(dve, scaled, n)
                c = Steps(dve, scale_chain, 3, n)
                c.link(dve.tensor_scalar(power[:], largest_all[:], LEAST, None, ALU.max))
                c.link(dve.tensor_scalar(power[:].bitcast(I32), power[:].bitcast(I32), EXPONENT, None,
                                         ALU.bitwise_and))
                c.link(dve.reciprocal(scale[:], power[:]))
                c.done()
                dve.tensor_scalar(R.unscale[:, bass.ds(e, 1), m], power[:], 1.0 / W_SCALE, None, ALU.mult)
                dve.tensor_scalar(scale[:], scale[:], W_SCALE, None, ALU.mult).then_inc(scale_ready, 1)

        def end(T, b, s, readers):
            if s == WEIGHTED[T.cross]:
                normalise(T, b, 0)
            if s == WEIGHTED[T.cross] + 1:
                normalise(T, b, 1)
            if s == OUT[T.cross]:
                residual(T, b)
            if s == NORM[T.cross]:
                layernorm(T, b, readers)

        def iteration(i, odd):
            for s in range(H + LAG):
                if has(i, 0) and s < H:
                    read_max(A, i, s)
                if has(i, 0) and s == H - 1:
                    split_max(A, i)
                if has(i, 0):
                    measure(i, 0, s)
                if has(i, -1):
                    b = i - 1
                    end(A, b, s, ((C.res_copied, i - 1), (C.src_full, i - 1)))
                    if s == C_KEYS - 1:
                        wait(dve, C.keep_in, 16 * (b + 1))
                        wait(dve, C.k_split, b)
                        dve.tensor_scalar(C.keep[:], C.keep_i[:], 0.0, None, ALU.not_equal).then_inc(C.keep_done, 1)
                    if s == C_KEYS_SPLIT:
                        split_k(C, b)
                    if s == C_QUERIES:
                        evac_q(C, b)
                        for step in range(3):
                            split_q(C, b, step)
            for s in range(H + LAG):
                if has(i, -1) and s < H:
                    read_max(C, i - 1, s)
                if has(i, -1) and s == H - 1:
                    split_max(C, i - 1)
                if has(i, -2):
                    b = i - 2
                    end(C, b, s, ((x2_written, 16 * b), (x2T_full, b), (scattered, 16 * TOP * TT * b)))
                    if s == LOGITS + 1:
                        route(b, 0)
                    if s in (RANKS, RANKS + 1):
                        route(b, s - RANKS + 1)
                    if s == H + LAG - 1:
                        route(b, 3)
                        route(b, 4)
                if has(i, -1) and s == VALUES[1]:
                    evac_v(i - 1)
                if has(i, 0):
                    measure(i, 1, s)
                if has(i, 1):
                    if s == A_QUERIES:
                        evac_q(A, i + 1)
                    if s == A_KEYS + 1:
                        split_k(A, i + 1)

        schedule(dve, iteration)
        dve.wait_ge(places_read, B)

        def over(table, shape):
            return table.to_broadcast(shape)

        dve.tensor_tensor(R.rest[:], R.run[:], R.room[:], ALU.add).then_inc(rest_ready, 1)
        setup.link(dve.tensor_tensor(more[:], over(R.run[:].unsqueeze(2), (P, E, B * S // TILE)),
                                 over(R.rows[:].unsqueeze(1), (P, E, B * S // TILE)), ALU.is_gt))
        setup.link(dve.tensor_reduce(R.tiles[:], more[:], X, ALU.add))
        setup.link(dve.tensor_tensor(before[:], over(R.tiles[:].unsqueeze(1), (P, E, E)), R.below[:], ALU.mult))
        setup.link(dve.tensor_reduce(R.first[:], before[:], X, ALU.add))
        setup.link(dve.tensor_tensor(R.behind[:], R.first[:], R.tiles[:], ALU.add))
        setup.link(dve.tensor_tensor(passed[:], over(R.behind[:].unsqueeze(1), (P, NTILE, E)),
                                 over(R.tile_no[:].unsqueeze(2), (P, NTILE, E)), ALU.is_le))
        setup.link(dve.tensor_reduce(owner_f[:], passed[:], X, ALU.add))
        setup.link(dve.tensor_tensor(skipped[:], passed[:], over(R.tiles[:].unsqueeze(1), (P, NTILE, E)), ALU.mult))
        setup.link(dve.tensor_reduce(start[:], skipped[:], X, ALU.add))
        setup.link(dve.tensor_tensor(start[:], R.tile_no[:], start[:], ALU.subtract))
        setup.link(dve.tensor_scalar(some[:], owner_f[:], float(E), float(TILE), ALU.is_lt, ALU.mult))
        setup.link(dve.tensor_tensor(start[:], start[:], some[:], ALU.mult))
        setup.link(dve.scalar_tensor_tensor(source_f[:], owner_f[:], float(ROOM), start[:], ALU.mult, ALU.add))
        setup.link(dve.tensor_copy(R.source[:], source_f[:]))
        dve.tensor_scalar(R.owner[:], owner_f[:], float(E - 1), None, ALU.min)

def experts(nc, ctx, R, out):
    def sb(n, shape, dt):
        return ctx.enter_context(nc.sbuf_tensor(n, shape, dt))

    def sem(n):
        return ctx.enter_context(nc.semaphore(n))

    XT = TILE // P
    GROUP = 4
    identf = sb("ident2", [P, P], F32)
    tile_no, first, behind, owner, source, rest = R.tile_no, R.first, R.behind, R.owner, R.source, R.rest
    gs = sb("gs2", [P, NT], F32)
    pw = sb("pw2", [P, TOP, NT, E], F32)
    wk = R.wk
    used = sb("used", [P, NTILE], F32)
    stores_f = sb("stores_f", [P, 2], F32)
    stores = sb("stores", [P, 2], I32)
    nmr = sb("nmr", [P, NT], F32)
    at = sb("at2", [P, NT, E], F32)
    slot_f = sb("slot_f2", [P, TOP, NT], F32)
    slot = sb("slot2", [P, TOP, NT], I32)
    w1 = sb("w1", [P, 2, 2, KT, F], F16)
    w2 = sb("w2", [P, 2, 2, FT, D], F16)
    unscale = sb("unscale2", [P, E], F32)
    factor = sb("factor", [P, TOP, NT], F32)
    xin = sb("xin", [P, 2, XT, D], F32)
    xT = sb("xTt", [P, 2, 2, KT, TILE], F16)
    hid = sb("hid", [P, 2, 2, FT, TILE], F16)
    yt = sb("yt", [P, 2, XT, D], F32)
    yg = sb("yg", [P, NT, TOP, D], F32)
    y = sb("y", [P, NT, D], F32)
    st = sb("fst", [P, NT, 6], F32)
    mv = sb("fmv", [P, NT, 2], F32)
    ve = sb("fve", [P, NT], F32)
    lnv = sb("flnv", [P, NT], F32)
    y0 = sb("fy0", [P, NT], F32)
    yy = sb("fyy", [P, NT], F32)
    rstd = sb("frstd", [P, NT], F32)
    ph = ctx.enter_context(nc.psum_tensor("ph", [P, 4, 512], F32))
    py = ctx.enter_context(nc.psum_tensor("py", [P, 2, 512], F32))
    pt = ctx.enter_context(nc.psum_tensor("pt", [P, 512], F32))
    ys_d = R.ys_d

    tables = sem("tables")
    tables_ready = sem("tables_ready")
    dve_chain = sem("dve_chain2")
    slot_ready = sem("slot_ready")
    w1_in = [sem("w1_in0"), sem("w1_in1")]
    w2_in = [sem("w2_in0"), sem("w2_in1")]
    x_in = [sem("x_in0"), sem("x_in1")]
    t_done = sem("t_done")
    xT_evac = sem("xT_evac")
    h_full = sem("h_full")
    relu_done = sem("relu_done")
    low_done = sem("low_done")
    x_high = sem("x_high")
    m2_done = sem("m2_done")
    y_evac = sem("y_evac")
    y_stored = [sem("y_stored0"), sem("y_stored1")]
    gathered = [sem(f"gathered{s}") for s in range(NT // GROUP)]
    stats = sem("fstats")
    lns = sem("flns")
    root = sem("froot")
    outs = sem("outs")
    rstd_ready = sem("rstd_ready")
    stored = sem("stored")
    sp_tick, act_tick = R.sp_tick, R.act_tick
    block = ctx.enter_context(nc.Block())

    PEEL = 4

    def schedule(eng, step):
        for j in range(PEEL):
            step(j, j % 2, j // 2)
        with eng.Fori(PEEL // 2, NTILE // 2) as i:
            for u in range(2):
                step(2 * i + u, u, i)
        for j in range(NTILE // 2 * 2, NTILE):
            step(j, j % 2, j // 2)

    def tile_rows(dram, j):
        return dram[bass.ds(j * TILE, TILE)].rearrange("(t p) d -> p t d", p=P)

    @block.sync
    def _(sp):
        def load_w1(j, u, expert):
            if not (isinstance(j, int) and j < 2):
                fence(sp, h_full, 4 * (j - 1), sp_tick)
            sp.dma_start(w1[:, u].rearrange("p s k n -> p (s k n)"),
                         R.parts_d[bass.ds(expert, 1), 0].rearrange("o p s n -> p (o s n)"))\
              .then_inc(w1_in[u], 16)

        def load_w2(j, u, expert):
            if not (isinstance(j, int) and j < 2):
                fence(sp, m2_done, j - 1, sp_tick)
            sp.dma_start(w2[:, u].rearrange("p s k n -> p (s k n)"),
                         R.parts_d[bass.ds(expert, 1), 1].rearrange("o p s n -> p (o s n)"))\
              .then_inc(w2_in[u], 16)

        def load_x(j, u):
            if not (isinstance(j, int) and j < 2):
                fence(sp, t_done, j - 1, sp_tick)
            row = sp.value_load(source[0:1, bass.ds(j, 1)], min_val=0, max_val=E * ROOM)
            sp.dma_start(xin[:, u], R.xs_d[bass.ds(row, TILE)].rearrange("(t p) d -> p t d", p=P))\
              .then_inc(x_in[u], 16)

        def step(j, u, i):
            expert = sp.value_load(owner[0:1, bass.ds(j, 1)], min_val=0, max_val=E - 1)
            if isinstance(j, int) and j == 0:
                load_x(0, 0)
            load_w1(j, u, expert)
            if isinstance(j, int) and j < 2:
                if j == 0:
                    load_x(1, 1)
                load_w2(j, u, expert)
                if j == 1:
                    load_x(2, 0)
            else:
                if not (isinstance(j, int) and j == NTILE - 1):
                    load_x(j + 1, 1 - u)
                load_w2(j, u, expert)

        schedule(sp, step)
        for s in range(NT // GROUP):
            sp.wait_ge(outs, s + 1)
            sp.dma_start(out.rearrange("b (t p) d -> p (b t) d", p=P)[:, s * GROUP:(s + 1) * GROUP],
                         y[:, s * GROUP:(s + 1) * GROUP]).then_inc(stored, 16)
        for u in range(2):
            sp.wait_ge(y_stored[u], 16 * ((NTILE + 1 - u) // 2))
        sp.wait_ge(stored, 16 * NT // GROUP)

    @block.gpsimd
    def _(pool):
        c = Steps(pool, tables, 100, 0)
        c.link(pool.memset(identf[:], 0.0))
        c.link(pool.affine_select(out=identf[:], in_=identf[:], compare_op=ALU.not_equal, fill=1.0, base=0,
                                  pattern=[[-1, P]], channel_multiplier=1))
        pool.drain().then_inc(tables_ready, 1)
        pool.wait_ge(slot_ready, 1)
        for u in range(2):
            count = pool.value_load(stores[0:1, u:u + 1], min_val=16 * (B * S * TOP // TILE // 2),
                                    max_val=16 * ((NTILE + 1) // 2))
            pool.wait_ge(y_stored[u], count)
            pool.sem_inc(R.pool_tick)
        for t in range(NT):
            for k in range(TOP):
                pool.indirect_dma_start(yg[:, t, k], None, ys_d,
                                        bass.IndirectOffsetOnAxis(ap=slot[:, k, t:t + 1], axis=0))\
                    .then_inc(gathered[t // GROUP], 16)

    @block.tensor
    def _(pe):
        pe.wait_ge(tables_ready, 1)
        def transpose(j, u, i):
            pe.wait_ge(x_in[u], 16 * (i + 1))
            wait(pe, xT_evac, j)
            for k in range(KT):
                for t in range(XT):
                    o = (k * XT + t) * P
                    last = pe.transpose(pt[:, o:o + P], xin[:, u, t, k * P:(k + 1) * P], identf[:])
            last.then_inc(t_done, 1)

        def hidden(j, u, i):
            wait(pe, xT_evac, j + 1)
            pe.wait_ge(w1_in[u], 16 * (i + 1))
            for f in range(FT):
                if f % 2 == 0:
                    wait(pe, low_done, 4 * j + f // 2 - 3)
                o = ph[:, f // 2, f % 2 * TILE:(f % 2 + 1) * TILE]
                for n, (a, b) in enumerate(PRODUCTS):
                    for k in range(KT):
                        last = pe.matmul(o, w1[:, u, a, k, f * P:(f + 1) * P], xT[:, u, b, k],
                                         start=(n == k == 0), stop=(n == len(PRODUCTS) - 1 and k == KT - 1))
                if f % 2 == 1:
                    last.then_inc(h_full, 1)

        def output(j, u, i):
            pe.wait_ge(w2_in[u], 16 * (i + 1))
            wait(pe, low_done, 4 * (j + 1))
            wait(pe, y_evac, j - 1)
            for t in range(XT):
                for f in range(FT):
                    for n, (a, b) in enumerate(PRODUCTS):
                        last = pe.matmul(py[:, u, t * D:(t + 1) * D], hid[:, u, a, f, t * P:(t + 1) * P],
                                         w2[:, u, b, f], start=(f == n == 0), stop=(f == FT - 1 and n == len(PRODUCTS) - 1))
            last.then_inc(m2_done, 1)

        transpose(0, 0, 0)

        def step(j, u, i):
            if not (isinstance(j, int) and j == NTILE - 1):
                transpose(j + 1, 1 - u, i + u)
            hidden(j, u, i)
            if not (isinstance(j, int) and j == 0):
                output(j - 1, 1 - u, i - 1 + u)

        schedule(pe, step)
        output(NTILE - 1, (NTILE - 1) % 2, (NTILE - 1) // 2)

    @block.scalar
    def _(act):
        def store(j, u, i):
            fence(act, y_evac, j + 1, act_tick)
            act.dma_start(tile_rows(ys_d, j), yt[:, u]).then_inc(y_stored[u], 16)

        def step(j, u, i):
            for f in range(FT // 2):
                wait(act, h_full, 4 * j + f + 1)
                if f == 0:
                    wait(act, m2_done, j - 1)
                act.activation(hid[:, u, 0, 2 * f:2 * f + 2], ph[:, f].rearrange("p (f t) -> p f t", f=2), ACT.Relu)\
                   .then_inc(relu_done, 1)
            if not (isinstance(j, int) and j < 2):
                store(j - 2, u, i - 1)

        schedule(act, step)
        for j in range(NTILE - 2, NTILE):
            store(j, j % 2, j // 2)
        def normalise(s):
            act.wait_ge(rstd_ready, s + 1)
            for t in range(s * GROUP, (s + 1) * GROUP):
                last = act.activation(y[:, t], y[:, t], ACT.Identity, bias=nmr[:, t:t + 1], scale=rstd[:, t:t + 1])
            last.then_inc(outs, 1)

        for s in range(NT // GROUP):
            sl = slice(s * GROUP, (s + 1) * GROUP)
            act.wait_ge(stats, s + 1)
            act.activation(lnv[:, sl], ve[:, sl], ACT.Ln).then_inc(lns, 1)
            act.wait_ge(lns, s + 1)
            act.activation(y0[:, sl], lnv[:, sl], ACT.Exp, scale=-0.5).then_inc(root, 1)
            if s > 0:
                normalise(s - 1)
        normalise(NT // GROUP - 1)

    @block.vector
    def _(dve):
        c = Steps(dve, dve_chain, 200, 0)
        def over(table, shape):
            return table.to_broadcast(shape)

        dve.wait_ge(tables_ready, 1)
        c.link(dve.scalar_tensor_tensor(at[:], over(first[:].unsqueeze(1), (P, NT, E)), float(TILE), R.place[:],
                                        ALU.mult, ALU.add))
        c.link(dve.tensor_tensor(pw[:], R.pick[:], over(at[:].unsqueeze(1), (P, TOP, NT, E)), ALU.mult))
        c.link(dve.tensor_reduce(slot_f[:], pw[:], X, ALU.add))
        c.link(dve.tensor_tensor(used[:], tile_no[:], over(behind[:, E - 1:E], (P, NTILE)), ALU.is_lt))
        for u in range(2):
            c.link(dve.tensor_reduce(stores_f[:, u:u + 1], used[:, bass.ds(u, (NTILE + 1 - u) // 2, step=2)],
                                     X, ALU.add))
        c.link(dve.tensor_scalar(stores[:], stores_f[:], 16.0, None, ALU.mult))
        dve.tensor_copy(slot[:], slot_f[:]).then_inc(slot_ready, 1)
        c.link(dve.tensor_tensor(gs[:], wk[:, 0], wk[:, 1], ALU.add))
        c.link(dve.reciprocal(gs[:], gs[:]))
        c.link(dve.tensor_tensor(wk[:], wk[:], over(gs[:].unsqueeze(1), (P, TOP, NT)), ALU.mult))
        c.link(dve.scalar_tensor_tensor(unscale[:], R.unscale[:, :, 0], 1.0 / X_SCALE, R.unscale[:, :, 1],
                                        ALU.mult, ALU.mult))
        c.link(dve.tensor_tensor(pw[:], R.pick[:], over(unscale[:].unsqueeze(1).unsqueeze(1), (P, TOP, NT, E)),
                                 ALU.mult))
        c.link(dve.tensor_reduce(factor[:], pw[:], X, ALU.add))
        c.link(dve.tensor_tensor(wk[:], wk[:], factor[:], ALU.mult))

        def evac_x(j, u):
            dve.wait_ge(t_done, j + 1)
            wait(dve, h_full, 4 * (j - 1))
            tile = pt[:].rearrange("p (k t) -> p k t", k=KT)
            dve.tensor_scalar(xT[:, u, 0], tile, X_SCALE, None, ALU.mult).then_inc(x_high, 1)
            dve.wait_ge(x_high, j + 1)
            dve.scalar_tensor_tensor(xT[:, u, 1], tile, X_SCALE, xT[:, u, 0], ALU.mult, ALU.subtract)\
               .then_inc(xT_evac, 1)

        def low_hidden(j, u):
            for f in range(FT // 2):
                dve.wait_ge(relu_done, 4 * j + f + 1)
                dve.scalar_tensor_tensor(hid[:, u, 1, 2 * f:2 * f + 2], ph[:, f].rearrange("p (f t) -> p f t", f=2),
                                         0.0, hid[:, u, 0, 2 * f:2 * f + 2], ALU.max, ALU.subtract)\
                   .then_inc(low_done, 1)

        def evac_y(j, u, i):
            dve.wait_ge(m2_done, j + 1)
            wait(dve, y_stored[u], 16 * i)
            dve.tensor_copy(yt[:, u], py[:, u].rearrange("p (t d) -> p t d", t=XT)).then_inc(y_evac, 1)

        evac_x(0, 0)

        def step(j, u, i):
            if not (isinstance(j, int) and j == NTILE - 1):
                evac_x(j + 1, 1 - u)
            low_hidden(j, u)
            if not (isinstance(j, int) and j == 0):
                evac_y(j - 1, 1 - u, i - 1 + u)

        schedule(dve, step)
        evac_y(NTILE - 1, (NTILE - 1) % 2, (NTILE - 1) // 2)

        def finish(s):
            sl = slice(s * GROUP, (s + 1) * GROUP)
            dve.wait_ge(root, s + 1)
            dve.wait_ge(stats, s + 1)
            c.link(dve.tensor_tensor(yy[:, sl], y0[:, sl], y0[:, sl], ALU.mult))
            c.link(dve.scalar_tensor_tensor(yy[:, sl], yy[:, sl], -0.5, ve[:, sl], ALU.mult, ALU.mult))
            c.link(dve.scalar_tensor_tensor(rstd[:, sl], yy[:, sl], 1.5, y0[:, sl], ALU.add, ALU.mult))
            dve.scalar_tensor_tensor(nmr[:, sl], mv[:, sl, 0], -1.0, rstd[:, sl], ALU.mult, ALU.mult)\
               .then_inc(rstd_ready, 1)

        for s in range(NT // GROUP):
            sl = slice(s * GROUP, (s + 1) * GROUP)
            dve.wait_ge(gathered[s], 16 * TOP * GROUP)
            for k in range(TOP):
                for t in range(s * GROUP, (s + 1) * GROUP):
                    c.n += 1
                    dve.scalar_tensor_tensor(y[:, t], yg[:, t, k], wk[:, k, t:t + 1], (R.x2, y)[k][:, t],
                                             ALU.mult, ALU.add).then_inc(dve_chain, 1)
                dve.wait_ge(dve_chain, c.n)
            for t in range(s * GROUP, (s + 1) * GROUP):
                c.n += 1
                dve.bn_stats(st[:, t], y[:, t]).then_inc(dve_chain, 1)
            dve.wait_ge(dve_chain, c.n)
            for t in range(s * GROUP, (s + 1) * GROUP):
                c.n += 1
                dve.bn_aggr(mv[:, t], st[:, t]).then_inc(dve_chain, 1)
            dve.wait_ge(dve_chain, c.n)
            dve.tensor_scalar(ve[:, sl], mv[:, sl, 1], EPS, None, ALU.add).then_inc(stats, 1)
            if s > 0:
                finish(s - 1)
        finish(NT // GROUP - 1)


def kernel(**inputs):
    import numpy as np
    import concourse.bacc as bacc
    from concourse.bass_utils import run_bass_kernel_spmd

    cycles = np.array([5 + h % 4 for h in range(H)])
    phases = np.arange(S)[None, :] % cycles[:, None]
    raw = np.asarray(inputs["L0_attn_bandha_gate"])
    order = np.arange(D).reshape(H, HD).T.reshape(D)
    gate_rows = np.tile(np.take_along_axis(raw, phases, axis=1), (HD, 1))
    w_qkv = np.asarray(inputs["L0_attn_w_qkv"])
    arrays = {
        "x": inputs["x"], "ctx_in": inputs["ctx_1024"],
        "mask": np.asarray(inputs["mask_Bx1x1xS2_ik0"]).reshape(B, S),
        "w_q1": w_qkv[:, 0:D][:, order], "w_k1": w_qkv[:, D:2 * D][:, order], "w_v1": w_qkv[:, 2 * D:3 * D],
        "w_o1": inputs["L0_attn_w_out"], "gate_raw": gate_rows,
        "wqT": np.asarray(inputs["L0_xattn_Wq"]).T[:, order],
        "bq": np.asarray(inputs["L0_xattn_bq"])[order].reshape(KT, P).T,
        "wkT": np.asarray(inputs["L0_xattn_Wk"]).T[:, order],
        "bk": np.asarray(inputs["L0_xattn_bk"])[order].reshape(KT, P).T,
        "wvT": np.asarray(inputs["L0_xattn_Wv"]).T, "bv": inputs["L0_xattn_bv"],
        "woT": np.asarray(inputs["L0_xattn_Wo"]).T, "bo": inputs["L0_xattn_bo"],
        "w_r": inputs["L0_ffn_Wr"], "w_1": inputs["L0_ffn_W1"], "w_2": inputs["L0_ffn_W2"],
    }
    nc = bacc.Bacc("TRN2", target_bir_lowering=False, num_devices=1)
    arrays = {n: np.ascontiguousarray(a) for n, a in arrays.items()}
    args = [nc.dram_tensor(n, a.shape, mybir.dt.from_np(a.dtype), kind="ExternalInput").ap()
            for n, a in arrays.items()]
    args.append(nc.dram_tensor("out", (B, S, D), F32, kind="ExternalOutput").ap())
    decoder_layer(nc, *args)
    r = run_bass_kernel_spmd(nc, [arrays], core_ids=[0])
    return r.results[0]["out"]
```
